# Optimizing a Trainium2 kernel written in Bass

```python
import numpy as np
import jax
import jax.numpy as jnp

def _softmax(x, axis=-1):
    return jax.nn.softmax(x, axis=axis)

def _gelu(x):
    return jax.nn.gelu(x, approximate=True)

def _silu(x):
    return jax.nn.silu(x)

def _sigmoid(x):
    return jax.nn.sigmoid(x)

def _layernorm(x, axis=-1, eps=1e-05):
    m = jnp.mean(x, axis=axis, keepdims=True)
    v = jnp.var(x, axis=axis, keepdims=True)
    return (x - m) / jnp.sqrt(v + eps)

def _scatter_add(tgt, idx, src, axis=0):
    return tgt.at[idx].add(src)

def _segment_sum(src, seg, n):
    return jax.ops.segment_sum(src, seg, n)
kernel_name = 'mk_recurrent_d2_jaxref_r8_b607f4'

def setup_inputs(seed: int=0):
    np.random.seed(seed)
    _w = jnp.asarray

    def _L0_attn_setup():
        import jax, jax.numpy as jnp
        import numpy as np
        B, N, D, H = (4, 256, 128, 16)
        HD = D // H
        key = jax.random.key(seed)
        k1, k2, k3 = jax.random.split(key, 3)
        scale = 1.0 / np.sqrt(D)
        return {'x': jax.random.normal(k1, (B, N, D), dtype=jnp.float32), 'w_qkv': jax.random.normal(k2, (D, 3 * D), dtype=jnp.float32) * scale, 'b_qkv': jnp.zeros((3 * D,), dtype=jnp.float32), 'w_proj': jax.random.normal(k3, (D, D), dtype=jnp.float32) * scale, 'b_proj': jnp.zeros((D,), dtype=jnp.float32)}
    _L0_attn_in = _L0_attn_setup()

    def _L0_ffn_setup():
        import jax, jax.numpy as jnp
        import numpy as np
        D = 128
        F = 352
        E = 8
        TOP_K = 2
        key = jax.random.key(seed)
        ks = jax.random.split(key, 6)
        std = 0.02
        x = jax.random.normal(ks[0], (2, 256, D), dtype=jnp.float32)
        router_w = jax.random.normal(ks[1], (D, E), dtype=jnp.float32) * std
        w1 = jax.random.normal(ks[2], (E, D, F), dtype=jnp.float32) * std
        v1 = jax.random.normal(ks[3], (E, D, F), dtype=jnp.float32) * std
        w2 = jax.random.normal(ks[4], (E, F, D), dtype=jnp.float32) * std
        bias = jnp.zeros((D,), dtype=jnp.float32)
        return {'x': x, 'router_w': router_w, 'w1': w1, 'v1': v1, 'w2': w2, 'bias': bias}
    _L0_ffn_in = _L0_ffn_setup()

    def _L1_attn_setup():
        import jax, jax.numpy as jnp
        import numpy as np
        B, L, D, H = (2, 256, 128, 16)
        d = D // H
        key = jax.random.key(seed)
        ks = jax.random.split(key, 6)
        X = jax.random.normal(ks[0], (B, L, D), dtype=jnp.float32)
        scale = 0.02
        Wq = scale * jax.random.normal(ks[1], (D, D), dtype=jnp.float32)
        Wk = scale * jax.random.normal(ks[2], (D, D), dtype=jnp.float32)
        Wv = scale * jax.random.normal(ks[3], (D, D), dtype=jnp.float32)
        Wc = scale * jax.random.normal(ks[4], (D, D), dtype=jnp.float32)
        Ltri = scale * jax.random.normal(ks[5], (H, d, d), dtype=jnp.float32)
        return {'X': X, 'Wq': Wq, 'Wk': Wk, 'Wv': Wv, 'Wc': Wc, 'Ltri': Ltri}
    _L1_attn_in = _L1_attn_setup()

    def _L1_ffn_setup():
        import jax, jax.numpy as jnp
        import numpy as np
        E, K = (8, 2)
        B, S, H, F = (2, 256, 128, 512)
        EPS = 1e-12

        def _expert_ffn(xf, Wi_e, bi_e, Wg_e, bg_e, Wo_e, bo_e, g_e, b_e):
            h = jax.nn.gelu(xf @ Wi_e + bi_e, approximate=False) * jax.nn.sigmoid(xf @ Wg_e + bg_e)
            r = xf + (h @ Wo_e + bo_e)
            mu = jnp.mean(r, axis=-1, keepdims=True)
            var = jnp.mean(jnp.square(r - mu), axis=-1, keepdims=True)
            return (r - mu) * jax.lax.rsqrt(var + EPS) * g_e + b_e
        key = jax.random.key(seed)
        ks = jax.random.split(key, 8)
        s = 0.02
        return {'x': jax.random.normal(ks[0], (B, S, H), jnp.float32), 'Wr': jax.random.normal(ks[1], (H, E), jnp.float32) * s, 'br': jnp.zeros((E,), jnp.float32), 'Wi': jax.random.normal(ks[2], (E, H, F), jnp.float32) * s, 'bi': jnp.zeros((E, F), jnp.float32), 'Wg': jax.random.normal(ks[3], (E, H, F), jnp.float32) * s, 'bg': jnp.zeros((E, F), jnp.float32), 'Wo': jax.random.normal(ks[4], (E, F, H), jnp.float32) * s, 'bo': jnp.zeros((E, H), jnp.float32), 'gamma': jnp.ones((E, H), jnp.float32), 'beta': jnp.zeros((E, H), jnp.float32)}
    _L1_ffn_in = _L1_ffn_setup()
    _d = {'L0_attn_x': _L0_attn_in['x'], 'L0_attn_w_qkv': _L0_attn_in['w_qkv'], 'L0_attn_b_qkv': _L0_attn_in['b_qkv'], 'L0_attn_w_proj': _L0_attn_in['w_proj'], 'L0_attn_b_proj': _L0_attn_in['b_proj'], 'L0_ffn_router_w': _L0_ffn_in['router_w'], 'L0_ffn_w1': _L0_ffn_in['w1'], 'L0_ffn_v1': _L0_ffn_in['v1'], 'L0_ffn_w2': _L0_ffn_in['w2'], 'L0_ffn_bias': _L0_ffn_in['bias'], 'L1_attn_Wq': _L1_attn_in['Wq'], 'L1_attn_Wk': _L1_attn_in['Wk'], 'L1_attn_Wv': _L1_attn_in['Wv'], 'L1_attn_Wc': _L1_attn_in['Wc'], 'L1_attn_Ltri': _L1_attn_in['Ltri'], 'L1_ffn_Wr': _L1_ffn_in['Wr'], 'L1_ffn_br': _L1_ffn_in['br'], 'L1_ffn_Wi': _L1_ffn_in['Wi'], 'L1_ffn_bi': _L1_ffn_in['bi'], 'L1_ffn_Wg': _L1_ffn_in['Wg'], 'L1_ffn_bg': _L1_ffn_in['bg'], 'L1_ffn_Wo': _L1_ffn_in['Wo'], 'L1_ffn_bo': _L1_ffn_in['bo'], 'L1_ffn_gamma': _L1_ffn_in['gamma'], 'L1_ffn_beta': _L1_ffn_in['beta']}
    _x0 = _d['L0_attn_x']
    _d['L0_attn_x'] = jax.random.normal(jax.random.fold_in(jax.random.key(seed), 1), (8, 512, 128), dtype=_x0.dtype)
    del _x0
    return _d

def reference(L0_attn_x, L0_attn_w_qkv, L0_attn_b_qkv, L0_attn_w_proj, L0_attn_b_proj, L0_ffn_router_w, L0_ffn_w1, L0_ffn_v1, L0_ffn_w2, L0_ffn_bias, L1_attn_Wq, L1_attn_Wk, L1_attn_Wv, L1_attn_Wc, L1_attn_Ltri, L1_ffn_Wr, L1_ffn_br, L1_ffn_Wi, L1_ffn_bi, L1_ffn_Wg, L1_ffn_bg, L1_ffn_Wo, L1_ffn_bo, L1_ffn_gamma, L1_ffn_beta):

    def _L0_attn_ref(x, w_qkv, b_qkv, w_proj, b_proj):
        import jax, jax.numpy as jnp
        import numpy as np
        B, N, D, H = (4, 256, 128, 16)
        HD = D // H
        b, n, c = x.shape
        h, hd = (H, HD)
        qkv = x @ w_qkv + b_qkv
        qkv = qkv.reshape(b, n, 3, h, hd)
        q = jnp.transpose(qkv[:, :, 0], (0, 2, 1, 3))
        k = jnp.transpose(qkv[:, :, 1], (0, 2, 1, 3))
        v = jnp.transpose(qkv[:, :, 2], (0, 2, 1, 3))
        attn = jnp.einsum('bhqd,bhkd->bhqk', q, k) * hd ** (-0.5)
        attn = jax.nn.softmax(attn, axis=-1)
        out = jnp.einsum('bhqk,bhkd->bhqd', attn, v)
        out = jnp.transpose(out, (0, 2, 1, 3)).reshape(b, n, c)
        return out @ w_proj + b_proj

    def _L0_ffn_ref(x, router_w, w1, v1, w2, bias):
        import jax, jax.numpy as jnp
        import numpy as np
        D = 128
        F = 352
        E = 8
        TOP_K = 2
        B, S, d = x.shape
        xt = x.reshape(B * S, d)
        scores = jax.nn.softmax(xt @ router_w, axis=-1)
        expert_weights, expert_idx = jax.lax.top_k(scores, TOP_K)
        h = jax.nn.gelu(jnp.einsum('td,edf->tef', xt, w1), approximate=False) * jnp.einsum('td,edf->tef', xt, v1)
        y = jnp.einsum('tef,efd->ted', h, w2)
        yk = jnp.take_along_axis(y, expert_idx[:, :, None], axis=1)
        out = jnp.sum(expert_weights[:, :, None] * yk, axis=1) + bias
        return out.reshape(B, S, d)

    def _L1_attn_ref(X, Wq, Wk, Wv, Wc, Ltri):
        import jax, jax.numpy as jnp
        import numpy as np
        B, L, D, H = (2, 256, 128, 16)
        d = D // H
        Bsz, Lq, Dm = X.shape
        Q = (X @ Wq.T).reshape(Bsz, Lq, H, d)
        K = (X @ Wk.T).reshape(Bsz, Lq, H, d)
        V = (X @ Wv.T).reshape(Bsz, Lq, H, d)
        KV = jnp.einsum('blhd,blhe->blhde', K, V)
        KVc = jnp.cumsum(KV, axis=1)
        Y = jnp.einsum('blhd,blhde->blhe', Q, KVc)
        mask = jnp.tril(jnp.ones((1, d, d), dtype=X.dtype))
        Lm = Ltri * mask
        Bm = Lm @ jnp.swapaxes(Lm, -2, -1)
        Y = jnp.einsum('hed,blhd->blhe', Bm, Y)
        Y = Y.reshape(Bsz, Lq, Dm)
        return Y @ Wc.T

    def _L1_ffn_ref(x, Wr, br, Wi, bi, Wg, bg, Wo, bo, gamma, beta):
        import jax, jax.numpy as jnp
        import numpy as np
        E, K = (8, 2)
        B, S, H, F = (2, 256, 128, 512)
        EPS = 1e-12

        def _expert_ffn(xf, Wi_e, bi_e, Wg_e, bg_e, Wo_e, bo_e, g_e, b_e):
            h = jax.nn.gelu(xf @ Wi_e + bi_e, approximate=False) * jax.nn.sigmoid(xf @ Wg_e + bg_e)
            r = xf + (h @ Wo_e + bo_e)
            mu = jnp.mean(r, axis=-1, keepdims=True)
            var = jnp.mean(jnp.square(r - mu), axis=-1, keepdims=True)
            return (r - mu) * jax.lax.rsqrt(var + EPS) * g_e + b_e
        b, s, h = x.shape
        T = b * s
        xf = x.reshape(T, h)
        probs = jax.nn.softmax(xf @ Wr + br, axis=-1)
        topw, topi = jax.lax.top_k(probs, K)
        topw = topw / jnp.sum(topw, axis=-1, keepdims=True)
        c = jnp.zeros((T, E), x.dtype).at[jnp.arange(T)[:, None], topi].set(topw)
        y = jax.vmap(_expert_ffn, in_axes=(None, 0, 0, 0, 0, 0, 0, 0, 0))(xf, Wi, bi, Wg, bg, Wo, bo, gamma, beta)
        out = jnp.einsum('te,eth->th', c, y)
        return out.reshape(b, s, h)
    x = L0_attn_x
    xn = _layernorm(x, axis=-1)
    s = _L0_attn_ref(xn, L0_attn_w_qkv, L0_attn_b_qkv, L0_attn_w_proj, L0_attn_b_proj)
    g = _silu(_L0_ffn_ref(xn, L0_ffn_router_w, L0_ffn_w1, L0_ffn_v1, L0_ffn_w2, L0_ffn_bias))
    x = x + s * g
    xn = _layernorm(x, axis=-1)
    s = _L1_attn_ref(xn, L1_attn_Wq, L1_attn_Wk, L1_attn_Wv, L1_attn_Wc, L1_attn_Ltri)
    g = _silu(_L1_ffn_ref(xn, L1_ffn_Wr, L1_ffn_br, L1_ffn_Wi, L1_ffn_bi, L1_ffn_Wg, L1_ffn_bg, L1_ffn_Wo, L1_ffn_bo, L1_ffn_gamma, L1_ffn_beta))
    x = x + s * g
    return x

_drawn_inputs = setup_inputs


def setup_inputs(seed=0):
    import zlib

    import numpy as np

    out = dict(_drawn_inputs(seed))
    spreads = {'L0_attn_b_qkv': (0.0, 0.8),
     'L0_attn_b_proj': (0.0, 0.8),
     'L0_ffn_bias': (0.0, 0.8),
     'L1_ffn_br': (0.0, 0.8),
     'L1_ffn_bi': (0.0, 0.8),
     'L1_ffn_bg': (0.0, 0.8),
     'L1_ffn_bo': (0.0, 0.8),
     'L1_ffn_gamma': (1.0, 0.6),
     'L1_ffn_beta': (0.0, 0.8)}
    factors = {'L0_attn_w_qkv': 8.0,
     'L0_attn_w_proj': 7.379,
     'L0_ffn_router_w': 8.0,
     'L0_ffn_w1': 8.0,
     'L0_ffn_v1': 8.0,
     'L0_ffn_w2': 8.0,
     'L1_attn_Wq': 8.0,
     'L1_attn_Wk': 8.0,
     'L1_attn_Wv': 8.0,
     'L1_attn_Wc': 8.0,
     'L1_attn_Ltri': 8.0,
     'L1_ffn_Wr': 8.0,
     'L1_ffn_Wi': 8.0,
     'L1_ffn_Wg': 8.0,
     'L1_ffn_Wo': 8.0}
    for name, (base, spread) in spreads.items():
        noise = np.random.default_rng([zlib.crc32(name.encode()), seed]).standard_normal(out[name].shape)
        drawn = base * np.exp(spread * noise) if base else spread * noise
        out[name] = jnp.asarray(drawn.astype(out[name].dtype))
    for name, factor in factors.items():
        out[name] = (out[name] * factor).astype(out[name].dtype)
    return out
```

```python
from contextlib import ExitStack

import concourse.bass as bass
from concourse import mybir

F32 = mybir.dt.float32
F32R = mybir.dt.float32r
BF16 = mybir.dt.bfloat16
I32 = mybir.dt.int32
U32 = mybir.dt.uint32
ALU = mybir.AluOpType
ACT = mybir.ActivationFunctionType
AX = mybir.AxisListType.X

P = 128
EXPERTS = 8
SEQS = 8
SEQ = 512
QT = SEQ // P
TOK_TILES = SEQS * QT
HEADS = 16
HD = 8
GROUPS = 4
TILE = 512
TILES = 24
CHOICES = 2 * TOK_TILES
EPS_LN = 1e-5
EPS_EXPERT = 1e-12


def build(nc, x, w_qkv, b_qkv, w_proj, b_proj, router_w, w1, v1, w2, ffn_bias,
          Wq, Wk, Wv, Wc, Ltri, Wr, br, Wi, bi, Wg, bg, Wo, bo, gamma, beta, out):
    D = x.shape[2]
    F0 = w1.shape[2]
    F1 = Wi.shape[2]
    SCALE = float(HD) ** -0.5
    CH = [[(0, 128), (128, 128), (256, F0 - 256)], [(c * 128, 128) for c in range(F1 // 128)]]
    FMAX = F1
    slots_x = nc.dram_tensor("slots_x", [TILES * TILE, D], F32, kind="Internal").ap()
    slots_y = nc.dram_tensor("slots_y", [TILES * TILE, D], F32, kind="Internal").ap()

    ctx = ExitStack()
    with ctx:
        def sb(name, shape, dt=F32):
            return ctx.enter_context(nc.sbuf_tensor(name, shape, dt))

        def sem(name):
            return ctx.enter_context(nc.semaphore(name))

        ps = ctx.enter_context(nc.psum_tensor("ps", [P, 8, 512], F32))

        xres = sb("xres", [P, TOK_TILES, D])
        xn = sb("xn", [P, TOK_TILES, D])
        attn = sb("attn", [P, TOK_TILES, D])
        xT_hi = sb("xT_hi", [P, SEQS, SEQ], F32R)
        xT_lo = sb("xT_lo", [P, SEQS, SEQ], F32R)

        ident = sb("ident", [P, P])
        before = sb("before", [P, P], BF16)
        ones_b = sb("ones_b", [P, 1], BF16)
        before64 = sb("before64", [CHOICES, CHOICES])
        ones64 = sb("ones64", [CHOICES, P])
        causal = sb("causal", [P, P])
        same_head = sb("same_head", [P, HEADS, HD])
        key8 = sb("key8", [P, EXPERTS])
        thr = sb("thr", [P, EXPERTS])
        before8 = sb("before8", [P, EXPERTS, EXPERTS])
        tile_no = sb("tile_no", [1, TILES])
        half = sb("half", [P, TOK_TILES])
        HMASK, LOQ, LOK, BQ, BK, BV, NROWS = 0, 4, 5, 6, 10, 14, 15
        rows = sb("rows", [1, NROWS, P])
        one_row = sb("one_row", [1, P])
        cols = sb("cols", [P, NROWS])
        sign = sb("sign", [P, 2])
        lobias = sb("lobias", [P, 2, GROUPS])
        head_cols = sb("head_cols", [P, 4, P])
        bproj_bc = sb("bproj_bc", [P, D])
        fbias_bc = sb("fbias_bc", [P, D])
        br_bc = sb("br_bc", [P, EXPERTS])
        bqkv_row = sb("bqkv_row", [1, 3 * D])

        wqkv = sb("wqkv", [P, 3 * D])
        ws_hi = sb("ws_hi", [P, 2, GROUPS, P], F32R)
        ws_lo = sb("ws_lo", [P, 2, GROUPS, P], F32R)
        wv_hi = sb("wv_hi", [P, D], F32R)
        wv_lo = sb("wv_lo", [P, D], F32R)
        wproj = sb("wproj", [P, D])
        wrout = sb("wrout", [P, 2, EXPERTS])
        w4 = sb("w4", [P, 4, D])
        w4T = sb("w4T", [P, 4, D])
        w3_hi = sb("w3_hi", [P, 3, D], F32R)
        w3_lo = sb("w3_lo", [P, 3, D], F32R)
        ltri = sb("ltri", [P, HD])
        ldiag = sb("ldiag", [P, HEADS, HD])
        ldiagT = sb("ldiagT", [P, P])
        bdiag = sb("bdiag", [P, P])
        wcomb = sb("wcomb", [P, D])
        ebias_rows = sb("ebias_rows", [2 * 4 * EXPERTS, P])
        ebias = sb("ebias", [P, EXPERTS, 8])

        stats = sb("stats", [P, TOK_TILES, 6])
        mv = sb("mv", [P, TOK_TILES, 2])
        veps = sb("veps", [P, TOK_TILES])
        rstd = sb("rstd", [P, TOK_TILES])
        logits = sb("logits", [P, TOK_TILES, EXPERTS])
        elog = sb("elog", [P, TOK_TILES, EXPERTS])
        esum = sb("esum", [P, TOK_TILES])
        top = sb("top", [P, TOK_TILES, 2])
        pick = sb("pick", [P, TOK_TILES, EXPERTS])
        kmax = sb("kmax", [P, TOK_TILES])
        lmax = sb("lmax", [P, TOK_TILES])
        hot = sb("hot", [P, TOK_TILES, 2, EXPERTS])
        hot_b = sb("hot_b", [P, TOK_TILES, 2, EXPERTS], BF16)
        wsel = sb("wsel", [P, TOK_TILES, 2])
        tot = sb("tot", [CHOICES, EXPERTS])
        carry = sb("carry", [CHOICES, CHOICES, EXPERTS])
        cmp8 = sb("cmp8", [P, EXPERTS, EXPERTS])
        ntile = sb("ntile", [P, EXPERTS])
        first = sb("first", [P, EXPERTS])
        off = sb("off", [P, EXPERTS])
        posw = sb("posw", [P, CHOICES, EXPERTS])
        posf = sb("posf", [P, CHOICES])
        pos = sb("pos", [P, CHOICES], U32)
        ecmp = sb("ecmp", [1, TILES, EXPERTS - 1])
        eidf = sb("eidf", [1, TILES])
        eid = sb("eid", [1, TILES], I32)

        ARENA, ARENA_R = 11520, 6144
        arena = sb("arena", [P, ARENA])
        arena_r = sb("arena_r", [P, ARENA_R], F32R)

        def carve(store):
            at = [0]

            def take(*shape):
                n = 1
                for k in shape:
                    n *= k
                v = store[:, at[0]:at[0] + n]
                at[0] += n
                assert at[0] <= store.shape[1], at
                if len(shape) == 2:
                    v = v.rearrange("p (a b) -> p a b", a=shape[0])
                if len(shape) == 3:
                    v = v.rearrange("p (a b c) -> p a b c", a=shape[0], b=shape[1])
                return v
            return take

        take = carve(arena)
        zeros = take(4096)
        wstack = take(2, GROUPS * 4, 32)
        take, take_r = carve(arena), carve(arena_r)
        Qs = take_r(GROUPS, SEQ)
        Ks = take_r(GROUPS, SEQ)
        Hi = take_r(2, SEQ)
        Lo = take(2, SEQ)
        probs = take(2, 4, SEQ)
        vaug = take(QT, HEADS, 32)
        vT = take(SEQ)
        o_sb = take(SEQ)
        onorm = take(QT, D)
        onT = take(SEQ)
        rden = sb("rden", [P, QT, 4])
        nmax = sb("nmax", [P, 2, 16])
        m_hi = sb("m_hi", [16, 2, P], F32R)
        m_lo = sb("m_lo", [16, 2, P], F32R)
        take = carve(arena)
        QT1 = take(SEQ)
        KT1 = take(SEQ)
        KTm = take(4, SEQ)
        VT1 = take(SEQ)
        ktok = take(QT, D)
        vtok = take(QT, D)
        vpad = take(QT, 4, D)
        scores = take(2, 4, SEQ)
        yT = VT1
        state = sb("state", [P, QT, D])
        take, take_r = carve(arena), carve(arena_r)
        wu_hi = take_r(2, 2 * F1)
        wu_lo = take_r(2, 2 * F1)
        gT_hi = take_r(2, TILE)
        gT_lo = take_r(2, TILE)
        wraw = take(2, 2 * F1)
        wdn = take(2, 4, D)
        xg = take(2, 4, D)
        gact = take(2, TILE)
        gsig = take(2, TILE)
        hT = take(2, TILE)
        ysb = take(2, 4, D)
        vecs = take(2, 3, D)
        ebcol = sb("ebcol", [P, 2, 8])
        estats = sb("estats", [P, 4, 6])
        eagg = sb("eagg", [P, 5, 4])
        emean = sb("emean", [P, 4])
        everstd = sb("everstd", [P, 2, 4])
        take = carve(arena)
        yg = take(2, QT * 2, D)
        zg = take(2, QT, D)
        sg = take(2, QT, D)

        ld_x = sem("ld_x")
        ld_a = sem("ld_a")
        ld_b = sem("ld_b")
        zero_set = sem("zero_set")
        slots_zero = sem("slots_zero")
        pool_mem = sem("pool_mem")
        pool_con = sem("pool_con")
        rows_set = sem("rows_set")
        dve_chain = sem("dve_chain")
        pe_setup = sem("pe_setup")
        setup_ev = sem("setup_ev")
        setup_done = sem("setup_done")
        two = lambda name: [sem(f"{name}{L}") for L in range(2)]
        veps_set, rstd_set, xn_set = two("veps_set"), two("rstd_set"), two("xn_set")
        tp_done, xhi_set, xlo_set = two("tp_done"), two("xhi_set"), two("xlo_set")
        logit_mm, z_set, e_set = two("logit_mm"), two("z_set"), two("e_set")
        hot_set, tot_mm, carry_set = two("hot_set"), two("tot_mm"), two("carry_set")
        pos_mm, pos_set, scattered = two("pos_mm"), two("pos_set"), two("scattered")
        up_in = [[sem(f"up_in{L}{r}") for r in range(2)] for L in range(2)]
        xg_in = [[sem(f"xg_in{L}{r}") for r in range(2)] for L in range(2)]
        dn_in = [[sem(f"dn_in{L}{r}") for r in range(2)] for L in range(2)]
        w_hi_set, w_lo_set = two("w_hi_set"), two("w_lo_set")
        gT_mm, ghi_set, glo_set = two("gT_mm"), two("ghi_set"), two("glo_set")
        gate_mm, up_mm, act_set = two("gate_mm"), two("up_mm"), two("act_set")
        h_set, down_mm, y_read = two("h_set"), two("down_mm"), two("y_read")
        xb_set, y_set = sem("xb_set"), two("y_set")
        est_chain, evar_set, erstd_set, xhat_set, gam_set = (
            sem("est_chain"), sem("evar_set"), sem("erstd_set"), sem("xhat_set"), sem("gam_set"))
        y_stored = [[sem(f"y_stored{L}{r}") for r in range(2)] for L in range(2)]
        gelu_set, w_stack_set = sem("gelu_set"), sem("w_stack_set")
        gathered = [[sem(f"gathered{L}{r}") for r in range(2)] for L in range(2)]
        z_ready, silu_set, x_set = two("z_ready"), two("silu_set"), two("x_set")
        stored = sem("stored")
        proj_mm, hi_set, lo_set, stack_set = (
            sem("proj_mm"), sem("hi_set"), sem("lo_set"), sem("stack_set"))
        s_mm, max_set, nmT_mm, mhi_set, mlo_set, m_in = (
            sem("s_mm"), sem("max_set"), sem("nmT_mm"), sem("mhi_set"), sem("mlo_set"), sem("m_in"))
        st_mm, exp_set, pv_mm, o_read, oT_mm, onorm_set = (
            sem("st_mm"), sem("exp_set"), sem("pv_mm"), sem("o_read"), sem("oT_mm"), sem("onorm_set"))
        rden_set = sem("rden_set")
        vT_mm, vT_set, vtp_mm, vaug_set = sem("vT_mm"), sem("vT_set"), sem("vtp_mm"), sem("vaug_set")
        vaug_const = sem("vaug_const")
        onT_mm, onT_set, out_mm, attn_set = sem("onT_mm"), sem("onT_set"), sem("out_mm"), sem("attn_set")
        qkv_mm, qkv_set, kvt_mm, ktok_set, vtok_set, vpad_set = (
            sem("qkv_mm"), sem("qkv_set"), sem("kvt_mm"), sem("ktok_set"), sem("vtok_set"), sem("vpad_set"))
        kv_mm, state_set, sc_mm, sc_set, y1_mm, yT_set, out1_mm, attn1_set = (
            sem("kv_mm"), sem("state_set"), sem("sc_mm"), sem("sc_set"), sem("y1_mm"),
            sem("yT_set"), sem("out1_mm"), sem("attn1_set"))

        def spread(ap, axis, shape):
            return ap.unsqueeze(axis).to_broadcast(shape)

        def seq_of(tile, b):
            return tile[:, b, :] if isinstance(b, int) else tile[:, bass.ds(b, 1), :].rearrange("p a n -> p (a n)")

        def rows_of(tile, b):
            return tile[:, b * QT:(b + 1) * QT, :] if isinstance(b, int) else tile[:, bass.ds(b * QT, QT), :]

        def split3(pe, out_ap, w_hi_ap, w_lo_ap, x_hi_ap, x_lo_ap, start=True, stop=True):
            pe.matmul(out_ap, w_hi_ap, x_hi_ap, start=start, stop=False)
            pe.matmul(out_ap, w_hi_ap, x_lo_ap, start=False, stop=False)
            return pe.matmul(out_ap, w_lo_ap, x_hi_ap, start=False, stop=stop)

        def steps(eng, step):
            class Now:
                def __init__(self, u):
                    self.main, self.tail = 0 <= u < 32, 1 <= u <= 32
                    self.max, self.proj, self.low = 0 <= u + 2 < 32, 0 <= u + 3 < 32, 0 <= u + 1 < 32
                    self.first = u < 1
            for u in range(-3, 1):
                step(u, u % GROUPS, u // GROUPS, Now(u))
            with eng.Fori(0, SEQS - 1) as b:
                for s in range(1, 5):
                    step(b * 4 + s, s % GROUPS, b + s // GROUPS, Now(s + 4))
            for u in range(29, 33):
                step(u, u % GROUPS, u // GROUPS, Now(u))

        N_A, N_B = 8, 7
        NDN = [2, 5]
        block = ctx.enter_context(nc.Block())

        @block.sync
        def _(sp):
            sp.dma_start(xres[:, :, :], x.rearrange("s (t p) d -> p (s t) d", p=P)).then_inc(ld_x, 16)
            sp.dma_start(wqkv[:, :], w_qkv).then_inc(ld_a, 16)
            sp.dma_start(bqkv_row[:, :], b_qkv.rearrange("(a n) -> a n", a=1)).then_inc(ld_a, 16)
            sp.dma_start(wproj[:, :], w_proj).then_inc(ld_a, 16)
            sp.dma_start(wrout[:, 0, :], router_w).then_inc(ld_a, 16)
            sp.dma_start(wrout[:, 1, :], Wr).then_inc(ld_a, 16)
            sp.dma_start(bproj_bc[:, :], b_proj.partition_broadcast(P)).then_inc(ld_a, 16)
            sp.dma_start(fbias_bc[:, :], ffn_bias.partition_broadcast(P)).then_inc(ld_a, 16)
            sp.dma_start(br_bc[:, :], br.partition_broadcast(P)).then_inc(ld_a, 16)
            for n, w in enumerate((Wq, Wk, Wv, Wc)):
                sp.dma_start(w4[:, n, :], w).then_inc(ld_b, 16)
            sp.dma_start(ltri[:, :], Ltri.rearrange("h e f -> (h e) f")).then_inc(ld_b, 16)
            nb = 4 * EXPERTS
            sp.dma_start(ebias_rows[0:nb, :], bi.rearrange("e (c p) -> (e c) p", p=P)).then_inc(ld_b, 16)
            sp.dma_start(ebias_rows[nb:2 * nb, :], bg.rearrange("e (c p) -> (e c) p", p=P)).then_inc(ld_b, 16)
            sp.wait_ge(zero_set, 1)
            fill = slots_x.rearrange("(p a) d -> p (a d)", p=P)
            for n in range(3):
                sp.dma_start(fill[:, n * 4096:(n + 1) * 4096], zeros).then_inc(slots_zero, 16)

            def max_rows(u, r, g):
                sp.wait_ge(mhi_set, u + 1)
                sp.wait_ge(mlo_set, u + 1)
                for row, src in ((24, m_hi), (25, m_lo)):
                    dst = Qs[row:P:32, g, :].bitcast(F32)
                    sp.dma_start(dst, src[:, r, :].bitcast(F32)).then_inc(m_in, 16)

            for u in range(2):
                max_rows(u, u % 2, u)
            with sp.Fori(0, SEQS - 1) as b:
                for s in range(4):
                    max_rows(b * 4 + s + 2, s % 2, (s + 2) % 4)
            for u in range(30, 32):
                max_rows(u, u % 2, u % 4)

            def expert_loads(L):
                nch = len(CH[L])
                F = (F0, F1)[L]
                gate, up, down = ((w1, v1, w2), (Wi, Wg, Wo))[L]

                def expert_of(i):
                    return sp.value_load(eid[0:1, bass.ds(i, 1)], min_val=0, max_val=EXPERTS - 1)

                def load_up(i, r):
                    e = expert_of(i)
                    for n, w in enumerate((gate, up)):
                        sp.dma_start(wraw[:, r, n * F:(n + 1) * F],
                                     w[bass.ds(e, 1), :, :].rearrange("a p n -> (a p) n")).then_inc(up_in[L][r], 16)

                def load_x(i, r):
                    sp.dma_start(xg[:, r, :, :].rearrange("p k d -> p (k d)"),
                                 slots_x[bass.ds(i * TILE, TILE), :].rearrange("(p k) d -> p (k d)", p=P)
                                 ).then_inc(xg_in[L][r], 16)

                def load_down(i, r):
                    e = expert_of(i)
                    wd = down[bass.ds(e, 1), :, :].rearrange("a f n -> (a f) n")
                    if L == 0:
                        sp.dma_start(wdn[:, r, 0:2, :],
                                     wd[0:2 * P, :].rearrange("(c p) n -> p c n", p=P)).then_inc(dn_in[L][r], 16)
                        sp.dma_start(wdn[0:F - 2 * P, r, 2, :], wd[2 * P:F, :]).then_inc(dn_in[L][r], 16)
                    else:
                        sp.dma_start(wdn[:, r, :, :],
                                     wd.rearrange("(c p) n -> p c n", p=P)).then_inc(dn_in[L][r], 16)
                        sp.dma_start(ebcol[:, r, :],
                                     ebias[:, bass.ds(e, 1), :].rearrange("p a n -> p (a n)")).then_inc(dn_in[L][r], 16)
                        for n, w in enumerate((bo, gamma, beta)):
                            sp.dma_start(vecs[:, r, n, :],
                                         w[bass.ds(e, 1), :].to_broadcast([P, D])).then_inc(dn_in[L][r], 16)

                sp.wait_ge(pos_set[L], 2)
                sp.wait_ge(scattered[L], 16 * CHOICES)
                sp.wait_ge((attn_set, attn1_set)[L], SEQS + 1)
                for i in range(2):
                    load_up(i, i)
                    load_x(i, i)
                    load_down(i, i)
                sp.wait_ge(w_lo_set[L], 1)
                load_up(2, 0)

                def refill(i, r, down=True, up=True):
                    if down:
                        sp.wait_ge(down_mm[L], i * nch)
                        if L == 1:
                            sp.wait_ge(y_set[1], i)
                        load_down(i + 1, 1 - r)
                    if up:
                        sp.wait_ge(w_lo_set[L], i + 2)
                        load_up(i + 3, 1 - r)
                    sp.wait_ge(gT_mm[L], i + 1)
                    if L == 1:
                        sp.wait_ge(xb_set, i + 1)
                    load_x(i + 2, r)

                refill(0, 0, down=False)
                with sp.Fori(0, (TILES - 4) // 2) as k:
                    refill(k * 2 + 1, 1)
                    refill(k * 2 + 2, 0)
                refill(TILES - 3, 1, up=False)
                sp.wait_ge(down_mm[L], (TILES - 2) * nch)
                if L == 1:
                    sp.wait_ge(y_set[1], TILES - 2)
                load_down(TILES - 1, 1)

            expert_loads(0)
            expert_loads(1)
            for b in range(SEQS):
                sp.wait_ge(x_set[1], b + 1)
                sp.dma_start(out[b, :, :].rearrange("(t p) d -> p t d", p=P),
                             xres[:, QT * b:QT * (b + 1), :]).then_inc(stored, 16)
            sp.wait_ge(stored, 16 * SEQS)

        @block.gpsimd
        def _(pool):
            def fill(ap, value):
                pool.memset(ap, value).then_inc(pool_mem, 1)

            fill(ident[:, :], 0.0)
            fill(before[:, :], 1.0)
            fill(ones_b[:, :], 1.0)
            fill(before64[:, :], 1.0)
            fill(ones64[:, :], 1.0)
            fill(causal[:, :], 1.0)
            fill(same_head[:, :, :], 1.0)
            fill(before8[:, :, :], 1.0)
            fill(half[:, :], -0.5)
            fill(one_row[:, :], 1.0)
            pool.wait_ge(pool_mem, 10)

            def keep(ap, pattern, base, mult, op=ALU.is_ge, fill_with=0.0):
                pool.affine_select(out=ap, in_=ap, compare_op=op, fill=fill_with, base=base,
                                   pattern=pattern, channel_multiplier=mult).then_inc(pool_con, 1)

            keep(ident[:, :], [[-1, P]], 0, 1, ALU.not_equal, 1.0)
            keep(before[:, :], [[1, P]], -1, -1)
            keep(before64[:, :], [[1, CHOICES]], -1, -1)
            keep(causal[:, :], [[1, P]], 0, -1)
            keep(before8[:, :, :], [[1, EXPERTS], [-1, EXPERTS]], -1, 0)
            keep(same_head[:, :, :], [[-HD, HEADS], [0, HD]], 0, 1)
            pool.iota(key8[:, :], [[-1, EXPERTS]], base=EXPERTS, channel_multiplier=0,
                      allow_small_or_imprecise_dtypes=True).then_inc(pool_con, 1)
            pool.iota(thr[:, :], [[TILE, EXPERTS]], base=0, channel_multiplier=0,
                      allow_small_or_imprecise_dtypes=True).then_inc(pool_con, 1)
            pool.iota(tile_no[:, :], [[1, TILES]], base=0, channel_multiplier=0,
                      allow_small_or_imprecise_dtypes=True).then_inc(pool_con, 1)
            pool.wait_ge(pool_con, 9)
            keep(same_head[:, :, :], [[HD, HEADS], [0, HD]], HD - 1, -1)
            pool.wait_ge(ld_b, 16 * N_B)
            pool.tensor_copy(ldiag[:, :, :], spread(ltri[:, :], 1, [P, HEADS, HD])).then_inc(pool_con, 1)
            pool.wait_ge(pool_con, 11)
            keep(ldiag[:, :, :], [[-HD, HEADS], [-1, HD]], 0, 1)
            pool.wait_ge(pool_con, 12)
            keep(ldiag[:, :, :], [[HD, HEADS], [0, HD]], HD - 1, -1)

            def norm_and_scatter(L):
                pool.wait_ge(veps_set[L], 1)
                pool.tensor_tensor(rstd[:, :], veps[:, :], half[:, :], ALU.pow).then_inc(rstd_set[L], 1)
                pool.wait_ge(pos_set[L], 1)
                if L == 0:
                    pool.wait_ge(slots_zero, 48)
                for c in range(CHOICES):
                    pool.indirect_dma_start(
                        out=slots_x, out_offset=bass.IndirectOffsetOnAxis(ap=pos[:, c:c + 1], axis=0),
                        in_=xn[:, c // 2, :], in_offset=None).then_inc(scattered[L], 16)

            def experts(L):
                NW = 2 * (F0, F1)[L]
                nch = len(CH[L])

                def low_weights(i, r):
                    pool.wait_ge(w_hi_set[L], i + 1)
                    pool.tensor_tensor(wu_lo[:, r, 0:NW], wraw[:, r, 0:NW],
                                       wu_hi[:, r, 0:NW].bitcast(F32), ALU.subtract).then_inc(w_lo_set[L], 1)

                def add_bias(i, r, k):
                    pool.wait_ge(dn_in[L][r], (k + 1) * 16 * NDN[L])
                    pool.wait_ge(xg_in[L][r], (k + 1) * 16)
                    pool.wait_ge(y_stored[L][r], (k + 1) * 16)
                    pool.tensor_tensor(ysb[:, r, :, :], xg[:, r, :, :],
                                       spread(vecs[:, r, 0, :], 1, [P, 4, D]), ALU.add).then_inc(xb_set, 1)

                def finish(i, r):
                    pool.wait_ge(evar_set, i + 1)
                    pool.tensor_tensor(everstd[:, r, :], everstd[:, r, :], half[:, 0:4], ALU.pow
                                       ).then_inc(erstd_set, 1)
                    pool.wait_ge(xhat_set, i + 1)
                    pool.tensor_tensor(ysb[:, r, :, :], ysb[:, r, :, :],
                                       spread(vecs[:, r, 1, :], 1, [P, 4, D]), ALU.mult).then_inc(gam_set, 1)
                    pool.wait_ge(gam_set, i + 1)
                    pool.tensor_tensor(ysb[:, r, :, :], ysb[:, r, :, :],
                                       spread(vecs[:, r, 2, :], 1, [P, 4, D]), ALU.add).then_inc(y_set[L], 1)

                low_weights(0, 0)
                low_weights(1, 1)
                if L == 0:
                    with pool.Fori(1, TILES // 2) as k:
                        for r in range(2):
                            low_weights(k * 2 + r, r)
                    return
                add_bias(0, 0, 0)
                finish(0, 0)
                low_weights(2, 0)
                add_bias(1, 1, 0)
                with pool.Fori(1, TILES // 2 - 1) as k:
                    finish(k * 2 - 1, 1)
                    low_weights(k * 2 + 1, 1)
                    add_bias(k * 2, 0, k)
                    finish(k * 2, 0)
                    low_weights(k * 2 + 2, 0)
                    add_bias(k * 2 + 1, 1, k)
                finish(TILES - 3, 1)
                low_weights(TILES - 1, 1)
                add_bias(TILES - 2, 0, TILES // 2 - 1)
                finish(TILES - 2, 0)
                add_bias(TILES - 1, 1, TILES // 2 - 1)
                finish(TILES - 1, 1)

            def gather(L):
                for r in range(2):
                    pool.wait_ge(y_stored[L][r], 16 * (TILES // 2 + 1))
                pool.wait_ge(down_mm[L], TILES * len(CH[L]))
                for b in range(SEQS):
                    r = b % 2
                    if b >= 2:
                        pool.wait_ge(z_ready[L], b - 1)
                    for n in range(2 * QT):
                        c = 2 * QT * b + n
                        pool.indirect_dma_start(
                            out=yg[:, r, n, :], out_offset=None, in_=slots_y,
                            in_offset=bass.IndirectOffsetOnAxis(ap=pos[:, c:c + 1], axis=0)
                        ).then_inc(gathered[L][r], 16)

            norm_and_scatter(0)
            experts(0)
            gather(0)
            norm_and_scatter(1)
            experts(1)
            gather(1)

        @block.tensor
        def _(pe):
            pe.wait_ge(pool_mem, 10)
            pe.wait_ge(rows_set, 1)
            for n in range(NROWS):
                pe.matmul(ps[:, 7, n:n + 1], rows[0:1, n, :], one_row[0:1, 0:1], start=True, stop=True)
            pe.matmul(ps[:, 6, :], one_row[0:1, :], rows[0:1, 0:4, :], start=True, stop=True).then_inc(pe_setup, 1)
            pe.wait_ge(pool_con, 13)
            pe.wait_ge(ld_b, 16 * N_B)
            for n in range(4):
                pe.transpose(ps[:, 5, n * P:(n + 1) * P], w4[:, n, :], ident[:, :])
            nb = 8 * EXPERTS
            pe.transpose(ps[:, 3, 0:nb], ebias_rows[:, :], ident[0:nb, 0:nb])
            pe.transpose(ps[:, 4, 0:P], ldiag[:, :, :].rearrange("p h d -> p (h d)"), ident[:, :]).then_inc(pe_setup, 1)
            pe.wait_ge(setup_ev, 1)
            pe.matmul(ps[:, 4, P:2 * P], ldiagT[:, :], ldiagT[:, :], start=True, stop=True).then_inc(pe_setup, 1)
            pe.wait_ge(setup_ev, 2)
            pe.matmul(ps[:, 4, 2 * P:3 * P], bdiag[:, :], w4T[:, 3, :], start=True, stop=True).then_inc(pe_setup, 1)

            def norm(L):
                def router(b):
                    pe.wait_ge(xhi_set[L], b + 1)
                    pe.wait_ge(xlo_set[L], b + 1)
                    for t in range(QT):
                        at = (b * QT + t) * EXPERTS
                        for n, half_x in enumerate((xT_hi, xT_lo)):
                            mm = pe.matmul(ps[:, 2, at:at + EXPERTS],
                                           half_x[:, b, t * P:(t + 1) * P].bitcast(F32), wrout[:, L, :],
                                           start=(n == 0), stop=(n == 1))
                    mm.then_inc(logit_mm[L], 1)

                if L == 0:
                    pe.wait_ge(ld_a, 16 * N_A)
                for b in range(SEQS):
                    pe.wait_ge(xn_set[L], b + 1)
                    if b >= 2:
                        pe.wait_ge(xhi_set[L], b - 1)
                        pe.wait_ge(xlo_set[L], b - 1)
                    for t in range(QT):
                        mm = pe.transpose(ps[:, b % 2, t * P:(t + 1) * P], xn[:, b * QT + t, :], ident[:, :])
                    mm.then_inc(tp_done[L], 1)
                    if b >= 1:
                        router(b - 1)
                router(SEQS - 1)

            def routing(L):
                pe.wait_ge(hot_set[L], 1)
                for e in range(EXPERTS):
                    mm = pe.matmul(ps[0:CHOICES, 3, e:e + 1],
                                   hot_b[:, :, :, e].rearrange("p t k -> p (t k)"), ones_b[:, :],
                                   start=True, stop=True)
                mm.then_inc(tot_mm[L], 1)
                pe.wait_ge(carry_set[L], 1)
                pe.matmul(ps[:, 4, 0:EXPERTS], ones64[:, :], tot[:, :], start=True, stop=True)
                pe.matmul(ps[:, 5, :], before[:, :], hot_b[:, :, :, :].rearrange("p t k e -> p (t k e)"),
                          start=True, stop=False)
                pe.matmul(ps[:, 5, :], ones64[:, :], carry[:, :, :].rearrange("p c e -> p (c e)"),
                          start=False, stop=True).then_inc(pos_mm[L], 1)

            def attend(u, g, b, now):
                v, w = u + 2, u + 3
                bw = b if g == 0 else b + 1
                for t in range(4):
                    if t == 0 and now.main:
                        pe.wait_ge(m_in, (u + 1) * 32)
                    if t == 0 and now.max:
                        pe.wait_ge(stack_set, (v + 1) * 2)
                    for j in range(4):
                        i = t * 4 + j
                        if now.main:
                            free = {0: 0, 1: 3, 2: 3}.get(i, 2)
                            if not (now.first and i < 3):
                                pe.wait_ge(exp_set, u * 16 + (i - free))
                            h = slice(32 * j, 32 * j + 26)
                            pe.matmul(ps[:, 2 + i % 3, :], Ks[h, g, t * P:(t + 1) * P], Qs[h, g, :],
                                      start=True, stop=True).then_inc(st_mm, 1)
                        if now.max:
                            if not (isinstance(v, int) and v * 16 + i < 2):
                                pe.wait_ge(max_set, v * 16 + (i - 1))
                            h = slice(32 * j, 32 * j + 24)
                            g2 = (g + 2) % GROUPS
                            pe.matmul(ps[:, i % 2, :], Qs[h, g2, t * P:(t + 1) * P], Ks[h, g2, :],
                                      start=True, stop=True).then_inc(s_mm, 1)
                    if t == 0 and now.tail:
                        output(u - 1, (g + 3) % GROUPS, 3)
                    if t >= 1 and now.main:
                        if t == 1:
                            if not now.first:
                                pe.wait_ge(o_read, u)
                            pe.wait_ge(vaug_set, b + 1)
                        output(u, g, t - 1)
                    if t == 0:
                        if now.proj:
                            if not (isinstance(w, int) and w < 1):
                                pe.wait_ge(lo_set, w * 2)
                            if g == 1 and now.main:
                                pe.wait_ge(attn_set, b + 1)
                            project(0, (g + 3) % GROUPS, bw)
                        if g == 0 and now.main:
                            pe.wait_ge(mhi_set, u + 2)
                            pe.wait_ge(mlo_set, u + 2)
                            pe.wait_ge(vT_set, b + 1)
                            for q in range(QT):
                                mm = pe.transpose(ps[:, 6, q * P:(q + 1) * P], vT[:, q * P:(q + 1) * P], ident[:, :])
                            mm.then_inc(vtp_mm, 1)
                    if t == 1 and now.tail:
                        if g == 0 and now.main:
                            pe.wait_ge(vaug_set, b + 1)
                        elif now.low:
                            pe.wait_ge(mhi_set, u + 2)
                            pe.wait_ge(mlo_set, u + 2)
                        pe.wait_ge(o_read, u)
                        for q in range(QT):
                            mm = pe.transpose(ps[:, 6, q * P:(q + 1) * P], o_sb[:, q * P:(q + 1) * P], ident[:, :])
                        mm.then_inc(oT_mm, 1)
                    if t == 2:
                        if now.proj:
                            pe.wait_ge(lo_set, w * 2 + 1)
                            project(1, (g + 3) % GROUPS, bw)
                        if g == 0 and now.tail:
                            pe.wait_ge(onorm_set, u)
                            for q in range(QT):
                                mm = pe.transpose(ps[:, 6, q * P:(q + 1) * P], onorm[:, q, :], ident[:, :])
                            mm.then_inc(onT_mm, 1)
                        if g == 3 and now.proj:
                            if now.tail:
                                pe.wait_ge(onorm_set, u)
                            elif now.low:
                                pe.wait_ge(mhi_set, u + 2)
                                pe.wait_ge(mlo_set, u + 2)
                            split3(pe, ps[:, 6, :], wv_hi[:, :], wv_lo[:, :], seq_of(xT_hi, b + 1),
                                   seq_of(xT_lo, b + 1)).then_inc(vT_mm, 1)
                    if t == 3:
                        if g == 0 and now.tail:
                            if now.proj:
                                pe.wait_ge(lo_set, (w + 1) * 2)
                            pe.wait_ge(onT_set, b)
                            for q in range(QT):
                                mm = pe.matmul(ps[:, 7, q * P:(q + 1) * P], onT[:, q * P:(q + 1) * P], wproj[:, :],
                                               start=True, stop=True)
                            mm.then_inc(out_mm, 1)
                        if now.max:
                            pe.wait_ge(max_set, (v + 1) * 16)
                            if g == 3 and now.proj:
                                pe.wait_ge(vT_set, b + 2)
                            elif now.tail:
                                pe.wait_ge(onorm_set, u)
                            elif now.low and now.first and isinstance(u, int) and u > -2:
                                pe.wait_ge(mhi_set, u + 2)
                                pe.wait_ge(mlo_set, u + 2)
                            if g == 0 and now.main:
                                pe.wait_ge(vaug_set, b + 1)
                            pe.transpose(ps[0:16, 6, 0:P], nmax[:, g % 2, :], ident[:, :]).then_inc(nmT_mm, 1)

            def project(which, g, bw):
                split3(pe, ps[:, 7, :], ws_hi[:, which, g, :], ws_lo[:, which, g, :],
                       seq_of(xT_hi, bw), seq_of(xT_lo, bw)).then_inc(proj_mm, 1)

            def output(u, g, t):
                pe.wait_ge(exp_set, u * 16 + (4 * t + 4))
                for j in range(4):
                    mm = pe.matmul(ps[32 * j:32 * j + 32, 5, :], vaug[:, t, 4 * g + j, :],
                                   probs[:, t % 2, j, :], start=(t == 0), stop=(t == 3))
                mm.then_inc(pv_mm, 1)

            def experts(L):
                F = (F0, F1)[L]
                nch = len(CH[L])
                last = nch - 1

                def turn(i, r, k):
                    pe.wait_ge(xg_in[L][r], (k + 1) * 16)
                    if not (isinstance(i, int) and i == 0):
                        pe.wait_ge(ghi_set[L], i)
                        pe.wait_ge(glo_set[L], i)
                    for q in range(4):
                        mm = pe.transpose(ps[:, 0, q * P:(q + 1) * P], xg[:, r, q, :], ident[:, :])
                    mm.then_inc(gT_mm[L], 1)

                def up(i, r, f, fresh=False):
                    n, par = i * nch + f, (r * nch + f) % 2
                    at, M = CH[L][f]
                    if f == 0:
                        pe.wait_ge(ghi_set[L], i + 1)
                        pe.wait_ge(glo_set[L], i + 1)
                        pe.wait_ge(w_lo_set[L], i + 1)
                    for bank, col, done, free in ((1, 0, gate_mm, act_set), (2, F, up_mm, (h_set, act_set)[L])):
                        if not fresh:
                            pe.wait_ge(free[L], n - 1)
                        c = slice(col + at, col + at + M)
                        split3(pe, ps[0:M, bank + 2 * par, :], wu_hi[:, r, c], wu_lo[:, r, c],
                               gT_hi[:, r, :], gT_lo[:, r, :]).then_inc(done[L], 1)

                def down(i, r, f, k, fresh=False):
                    n, par = i * nch + f, (r * nch + f) % 2
                    M = CH[L][f][1]
                    pe.wait_ge(h_set[L], n + 1)
                    if f == 0:
                        pe.wait_ge(dn_in[L][r], (k + 1) * 16 * NDN[L])
                        if not fresh:
                            pe.wait_ge(y_read[L], i - 1)
                    for q in range(4):
                        mm = pe.matmul(ps[:, 5 + r, q * P:(q + 1) * P], hT[0:M, par, q * P:(q + 1) * P],
                                       wdn[0:M, r, f, :], start=(f == 0 and q == 0), stop=(f == last and q == 3),
                                       skip_group_check=True)
                    mm.then_inc(down_mm[L], 1)

                def tile(i, r, k, fresh=False, more=True):
                    for f in range(nch):
                        if f < last:
                            up(i, r, f + 1, fresh=fresh and r == 0 and f + 1 < 2)
                        elif more:
                            up(i + 1, 1 - r, 0)
                        if f == 0 and more:
                            turn(i + 1, 1 - r, k + r)
                        down(i, r, f, k, fresh=fresh)

                turn(0, 0, 0)
                up(0, 0, 0, fresh=True)
                tile(0, 0, 0, fresh=True)
                tile(1, 1, 0, fresh=True)
                with pe.Fori(1, TILES // 2 - 1) as k:
                    for r in range(2):
                        tile(k * 2 + r, r, k)
                k = TILES // 2 - 1
                tile(k * 2, 0, k)
                tile(k * 2 + 1, 1, k, more=False)

            def linear(b, fresh):
                for n in range(3):
                    if not fresh:
                        pe.wait_ge((attn1_set, vpad_set, state_set)[n], (b + 1, b * QT, b * 3)[n])
                        if n == 1:
                            pe.wait_ge(vtok_set, b)
                    split3(pe, ps[:, 5 + n, :], w3_hi[:, n, :], w3_lo[:, n, :],
                           seq_of(xT_hi, b), seq_of(xT_lo, b)).then_inc(qkv_mm, 1)
                pe.wait_ge(qkv_set, (b + 1) * 7)
                for n, src in enumerate((KT1, VT1)):
                    for q in range(QT):
                        mm = pe.transpose(ps[:, 5 + n, q * P:(q + 1) * P], src[:, q * P:(q + 1) * P], ident[:, :])
                    mm.then_inc(kvt_mm, 1)
                for c in range(QT):
                    for s in range(4):
                        if not (fresh and c == 0):
                            pe.wait_ge(sc_set, b * 16 + (c * 4 + s - 3))
                        h, tok = slice(32 * s, 32 * s + 32), slice(c * P, (c + 1) * P)
                        for v in range(4):
                            mm = pe.matmul(ps[:, s, v * P:(v + 1) * P], KTm[h, v, tok], QT1[h, tok],
                                           start=True, stop=True)
                        mm.then_inc(sc_mm, 1)
                    if c < QT - 1:
                        if c == 0:
                            pe.wait_ge(ktok_set, b + 1)
                            pe.wait_ge(vtok_set, b + 1)
                        else:
                            pe.wait_ge(state_set, b * 3 + c)
                        pe.matmul(ps[:, 7, 0:P], ktok[:, c, :], vtok[:, c, :], start=(c == 0), stop=(c == QT - 2),
                                  skip_group_check=True).then_inc(kv_mm, 1)
                    if c >= 1:
                        weigh(b, c - 1, fresh)
                weigh(b, QT - 1, fresh)
                pe.wait_ge(yT_set, b + 1)
                for q in range(QT):
                    mm = pe.matmul(ps[:, 5, q * P:(q + 1) * P], yT[:, q * P:(q + 1) * P], wcomb[:, :],
                                   start=True, stop=True)
                mm.then_inc(out1_mm, 1)

            def weigh(b, c, fresh):
                tok = slice(c * P, (c + 1) * P)
                if c == 0 and not fresh:
                    pe.wait_ge(yT_set, b)
                if c > 0:
                    pe.wait_ge(state_set, b * 3 + c)
                    pe.matmul(ps[:, 4, tok], state[:, c, :], QT1[:, tok], start=False, stop=False,
                              skip_group_check=True)
                pe.wait_ge(vpad_set, b * QT + (c + 1))
                pe.wait_ge(sc_set, b * 16 + (c * 4 + 4))
                for v in range(4):
                    for s in range(4):
                        mm = pe.matmul(ps[32 * s:32 * s + 32, 4, tok], vpad[:, c, v, 32 * s:32 * s + 32],
                                       scores[:, c % 2, s, v * P:(v + 1) * P], start=(c == 0 and v == 0),
                                       stop=(c == QT - 1 and v == 3), skip_group_check=True)
                mm.then_inc(y1_mm, 1)

            norm(0)
            routing(0)
            pe.wait_ge(setup_done, 1)
            pe.wait_ge(pos_set[0], 2)
            pe.wait_ge(w_stack_set, 1)
            steps(pe, attend)
            pe.wait_ge(attn_set, SEQS + 1)
            experts(0)
            pe.wait_ge(y_read[0], TILES)
            norm(1)
            routing(1)
            pe.wait_ge(pos_set[1], 2)
            linear(0, True)
            with pe.Fori(1, SEQS) as b:
                linear(b, False)
            pe.wait_ge(attn1_set, SEQS + 1)
            experts(1)

        @block.scalar
        def _(act):
            ident_f, copy_f = ACT.Identity, ACT.Copy

            def norm(L):
                for b in range(SEQS):
                    act.wait_ge(tp_done[L], b + 1)
                    act.activation(xT_hi[:, b, :], ps[:, b % 2, :], copy_f).then_inc(xhi_set[L], 1)
                act.wait_ge(z_set[L], 1)
                act.activation(elog[:, :, :], logits[:, :, :], ACT.Exp).then_inc(e_set[L], 1)

            def attend(u, g, b, now):
                g3 = (g + 3) % GROUPS
                w = u + 3
                for t in range(4):
                    for j in range(4):
                        i = t * 4 + j
                        if now.main:
                            if j == 0 and not (now.first and t < 2):
                                act.wait_ge(pv_mm, u * 4 + (t - 1))
                            act.wait_ge(st_mm, u * 16 + (i + 1))
                            act.activation(probs[:, t % 2, j, :], ps[:, 2 + i % 3, :], ACT.Exp,
                                           scale=SCALE).then_inc(exp_set, 1)
                    if t == 0 and now.low:
                        act.wait_ge(nmT_mm, u + 2)
                        if not (isinstance(u, int) and u + 1 < 2):
                            act.wait_ge(m_in, u * 32)
                        act.activation(m_hi[:, (g + 1) % 2, :], ps[0:16, 6, 0:P], copy_f).then_inc(mhi_set, 1)
                    if t in (0, 2) and now.proj:
                        which = t // 2
                        act.wait_ge(proj_mm, w * 2 + (which + 1))
                        if not (isinstance(w, int) and w < 1):
                            act.wait_ge(stack_set, w * 2 + (which - 1))
                        act.activation(Hi[:, which, :], ps[:, 7, :], ident_f,
                                       bias=cols[:, (BQ, BK)[which] + g3:(BQ, BK)[which] + g3 + 1]).then_inc(hi_set, 1)
                        act.activation(Lo[:, which, :], ps[:, 7, :], ident_f,
                                       bias=lobias[:, which, g3:g3 + 1],
                                       scale=cols[:, LOQ + which:LOQ + which + 1]).then_inc(lo_set, 1)
                    if t == 2 and g == 3 and now.proj:
                        act.wait_ge(vT_mm, b + 2)
                        act.activation(vT, ps[:, 6, :], ident_f, bias=cols[:, BV:BV + 1]).then_inc(vT_set, 1)
                    if t == 2 and g == 0 and now.tail:
                        act.wait_ge(onT_mm, b)
                        act.activation(onT, ps[:, 6, :], copy_f).then_inc(onT_set, 1)

            def experts(L):
                nch = len(CH[L])

                def high_rows(i, r):
                    act.wait_ge(gT_mm[L], i + 1)
                    act.activation(gT_hi[:, r, :], ps[:, 0, :], copy_f).then_inc(ghi_set[L], 1)

                def write_y(i, r, k):
                    act.wait_ge(down_mm[L], (i + 1) * nch)
                    act.wait_ge(y_stored[L][r], (k + 1) * 16)
                    act.activation(ysb[:, r, :, :].rearrange("p q d -> p (q d)"), ps[:, 5 + r, :], copy_f
                                   ).then_inc(y_read[L], 1)

                def store(i, r):
                    if L == 0:
                        act.wait_ge(y_read[L], i + 1)
                    else:
                        act.wait_ge(y_set[L], i + 1)
                    act.dma_start(slots_y[bass.ds(i * TILE, TILE), :].rearrange("(p k) d -> p (k d)", p=P),
                                  ysb[:, r, :, :].rearrange("p q d -> p (q d)")).then_inc(y_stored[L][r], 16)

                def tile(i, r, k, first=False, last=False):
                    for f in range(nch):
                        n, par, M = i * nch + f, (r * nch + f) % 2, CH[L][f][1]
                        if L == 1 and f == 0:
                            act.wait_ge(dn_in[L][r], (k + 1) * 16 * NDN[L])
                        if not (first and r == 0 and f < 2):
                            act.wait_ge(h_set[L], n - 1)
                        act.wait_ge(gate_mm[L], n + 1)
                        if L == 0:
                            act.activation(gact[0:M, par, :], ps[0:M, 1 + 2 * par, :], ACT.Gelu).then_inc(act_set[L], 1)
                        else:
                            act.activation(gact[:, par, :], ps[:, 1 + 2 * par, :], ACT.Gelu,
                                           bias=ebcol[:, r, f:f + 1]).then_inc(gelu_set, 1)
                            act.wait_ge(up_mm[L], n + 1)
                            act.activation(gsig[:, par, :], ps[:, 2 + 2 * par, :], ACT.Tanh, scale=0.5,
                                           bias=ebcol[:, r, 4 + f:5 + f]).then_inc(act_set[L], 1)
                        if L == 0 and f == 0 and not (first and r == 0):
                            write_y(i - 1, 1 - r, k - 1 + r)
                        if f == 1 and not last:
                            high_rows(i + 1, 1 - r)
                        if f == nch - 1 and not (first and r == 0):
                            store(i - 1, 1 - r)

                for r in range(2):
                    act.sem_inc(y_stored[L][r], 16)
                high_rows(0, 0)
                tile(0, 0, 0, first=True)
                tile(1, 1, 0, first=True)
                with act.Fori(1, TILES // 2 - 1) as k:
                    tile(k * 2, 0, k)
                    tile(k * 2 + 1, 1, k)
                k = TILES // 2 - 1
                tile(k * 2, 0, k)
                tile(k * 2 + 1, 1, k, last=True)
                if L == 0:
                    write_y(TILES - 1, 1, k)
                store(TILES - 1, 1)

            def linear(b, fresh):
                act.wait_ge(qkv_mm, b * 3 + 1)
                if not fresh:
                    act.wait_ge(y1_mm, b * 4)
                    act.wait_ge(out1_mm, b)
                act.activation(QT1, ps[:, 5, :], copy_f).then_inc(qkv_set, 1)
                act.wait_ge(qkv_mm, b * 3 + 2)
                for v in range(4):
                    act.activation(KTm[:, v, :], ps[:, 6, :], ident_f,
                                   scale=cols[:, HMASK + v:HMASK + v + 1]).then_inc(qkv_set, 1)
                act.activation(KT1, ps[:, 6, :], copy_f).then_inc(qkv_set, 1)
                act.wait_ge(qkv_mm, b * 3 + 3)
                act.activation(VT1, ps[:, 7, :], copy_f).then_inc(qkv_set, 1)
                act.wait_ge(kvt_mm, b * 2 + 1)
                act.activation(ktok.rearrange("p a b -> p (a b)"), ps[:, 5, :], copy_f).then_inc(ktok_set, 1)
                act.wait_ge(kvt_mm, b * 2 + 2)
                act.wait_ge(vpad_set, b * QT + QT)
                act.activation(vtok.rearrange("p a b -> p (a b)"), ps[:, 6, :], copy_f).then_inc(vtok_set, 1)
                act.wait_ge(y1_mm, b * 4 + 4)
                act.activation(yT, ps[:, 4, :], copy_f).then_inc(yT_set, 1)

            def gate(L):
                for b in range(SEQS):
                    r = b % 2
                    act.wait_ge(z_ready[L], b + 1)
                    if b >= 2:
                        act.wait_ge(x_set[L], b - 1)
                    act.activation(sg[:, r, :, :], zg[:, r, :, :], ACT.Silu).then_inc(silu_set[L], 1)

            act.wait_ge(setup_done, 1)
            norm(0)
            act.wait_ge(slots_zero, 48)
            act.wait_ge(w_stack_set, 1)
            steps(act, attend)
            experts(0)
            gate(0)
            norm(1)
            linear(0, True)
            with act.Fori(1, SEQS) as b:
                linear(b, False)
            experts(1)
            gate(1)

        @block.vector
        def _(dve):
            links = [0]

            def link(ins):
                ins.then_inc(dve_chain, 1)
                links[0] += 1
                dve.wait_ge(dve_chain, links[0])

            def split(hi, lo, src):
                link(dve.tensor_copy(hi, src))
                link(dve.tensor_tensor(lo, src, hi.bitcast(F32), ALU.subtract))

            def setup():
                dve.memset(zeros, 0.0).then_inc(zero_set, 1)
                link(dve.memset(rows[:, :, :], 0.0))
                link(dve.memset(wstack, 0.0))
                dve.wait_ge(ld_a, 16 * N_A)
                hrow = rows[0:1, 0:4, :].rearrange("a v (s q r) -> a v s q r", s=4, q=4)
                for v in range(4):
                    link(dve.memset(hrow[:, v, :, v, :], 1.0))
                jrow = rows[0:1, :, :].rearrange("a n (j r) -> a n j r", j=4)
                link(dve.memset(jrow[:, LOQ, :, 16:24], 1.0))
                link(dve.memset(jrow[:, LOK, :, 8:16], 1.0))
                for which, at in enumerate((BQ, BK)):
                    src = bqkv_row[0:1, which * D:(which + 1) * D].rearrange("a (g j r) -> a g j r", g=4, j=4)
                    wsrc = wqkv[:, which * D:(which + 1) * D].rearrange("p (h r) -> p h r", r=HD)
                    for n in range(3):
                        link(dve.tensor_copy(jrow[:, at:at + 4, :, 8 * n:8 * n + 8], src))
                        link(dve.tensor_copy(wstack[:, which, :, 8 * n:8 * n + 8], wsrc))
                link(dve.memset(jrow[:, BK:BK + 4, :, 24:26], 1.0))
                dve.tensor_copy(rows[0:1, BV, :], bqkv_row[0:1, 2 * D:3 * D]).then_inc(rows_set, 1)
                split(ws_hi[:, :, :, :].rearrange("p w g m -> p (w g m)"),
                      ws_lo[:, :, :, :].rearrange("p w g m -> p (w g m)"),
                      wstack.rearrange("p w h r -> p (w h r)"))
                split(wv_hi[:, :], wv_lo[:, :], wqkv[:, 2 * D:3 * D])
                dve.wait_ge(pe_setup, 1)
                link(dve.tensor_copy(cols[:, :], ps[:, 7, 0:NROWS]))
                link(dve.tensor_copy(head_cols[:, :, :].rearrange("p v m -> p (v m)"), ps[:, 6, :]))
                for which in range(2):
                    lo_col = cols[:, LOQ + which:LOQ + which + 1]
                    at = (BQ, BK)[which]
                    link(dve.tensor_scalar(sign[:, which:which + 1], lo_col, -2.0, 1.0, ALU.mult, ALU.add))
                    link(dve.tensor_scalar(lobias[:, which, :], cols[:, at:at + 4], lo_col, None, ALU.mult))
                dve.wait_ge(pe_setup, 2)
                link(dve.tensor_copy(w4T[:, :, :].rearrange("p n m -> p (n m)"), ps[:, 5, :]))
                dve.tensor_copy(ldiagT[:, :], ps[:, 4, 0:P]).then_inc(setup_ev, 1)
                split(w3_hi[:, :, :], w3_lo[:, :, :], w4T[:, 0:3, :])
                nb = 4 * EXPERTS
                link(dve.tensor_copy(ebias[:, :, 0:4], ps[:, 3, 0:nb].rearrange("p (e c) -> p e c", e=EXPERTS)))
                link(dve.tensor_scalar(ebias[:, :, 4:8], ps[:, 3, nb:2 * nb].rearrange("p (e c) -> p e c", e=EXPERTS),
                                       0.5, None, ALU.mult))
                dve.wait_ge(pe_setup, 3)
                dve.tensor_copy(bdiag[:, :], ps[:, 4, P:2 * P]).then_inc(setup_ev, 1)
                dve.wait_ge(pe_setup, 4)
                dve.tensor_copy(wcomb[:, :], ps[:, 4, 2 * P:3 * P]).then_inc(setup_done, 1)

            def statistics(t):
                link(dve.bn_stats(stats[:, t, :], xres[:, t, :]))
                return dve.bn_aggr(mv[:, t, :], stats[:, t, :])

            def norm(L):
                if L == 0:
                    dve.wait_ge(ld_x, 16)
                    for t in range(TOK_TILES):
                        link(statistics(t))
                dve.tensor_scalar(veps[:, :], mv[:, :, 1], EPS_LN, None, ALU.add).then_inc(veps_set[L], 1)
                dve.wait_ge(rstd_set[L], 1)
                if L == 1:
                    dve.wait_ge(scattered[0], 16 * CHOICES)

                def low(b):
                    dve.wait_ge(xhi_set[L], b + 1)
                    dve.wait_ge(tp_done[L], b + 1)
                    dve.tensor_tensor(xT_lo[:, b, :], ps[:, b % 2, :], xT_hi[:, b, :].bitcast(F32),
                                      ALU.subtract).then_inc(xlo_set[L], 1)

                for b in range(SEQS):
                    for t in range(b * QT, (b + 1) * QT):
                        ins = dve.tensor_scalar(xn[:, t, :], xres[:, t, :], mv[:, t, 0:1], rstd[:, t:t + 1],
                                                ALU.subtract, ALU.mult)
                    ins.then_inc(xn_set[L], 1)
                    if b >= 1:
                        low(b - 1)
                low(SEQS - 1)

            def routing(L):
                S3 = [P, TOK_TILES, EXPERTS]
                dve.wait_ge(logit_mm[L], SEQS)
                dve.wait_ge(pool_con, 13)
                raw = ps[:, 2, 0:TOK_TILES * EXPERTS].rearrange("p (t e) -> p t e", e=EXPERTS)
                if L == 0:
                    link(dve.tensor_copy(logits[:, :, :], raw))
                else:
                    link(dve.tensor_tensor(logits[:, :, :], raw, spread(br_bc[:, :], 1, S3), ALU.add))
                link(dve.tensor_reduce(lmax[:, :], logits[:, :, :], AX, ALU.max))
                dve.tensor_tensor(logits[:, :, :], logits[:, :, :], spread(lmax[:, :], 2, S3),
                                  ALU.subtract).then_inc(z_set[L], 1)
                dve.wait_ge(e_set[L], 1)
                link(dve.tensor_reduce(esum[:, :], elog[:, :, :], AX, ALU.add))
                for k in range(2):
                    link(dve.tensor_reduce(top[:, :, k], elog[:, :, :], AX, ALU.max))
                    link(dve.tensor_tensor(pick[:, :, :], elog[:, :, :], spread(top[:, :, k], 2, S3), ALU.is_ge))
                    link(dve.tensor_tensor(pick[:, :, :], pick[:, :, :], spread(key8[:, :], 1, S3), ALU.mult))
                    link(dve.tensor_reduce(kmax[:, :], pick[:, :, :], AX, ALU.max))
                    link(dve.tensor_tensor(hot[:, :, k, :], pick[:, :, :], spread(kmax[:, :], 2, S3), ALU.is_equal))
                    if k == 0:
                        link(dve.scalar_tensor_tensor(elog[:, :, :], hot[:, :, 0, :], -2.0, elog[:, :, :],
                                                      ALU.mult, ALU.add))
                dve.tensor_copy(hot_b[:, :, :, :], hot[:, :, :, :]).then_inc(hot_set[L], 1)
                if L == 1:
                    link(dve.tensor_tensor(esum[:, :], top[:, :, 0], top[:, :, 1], ALU.add))
                link(dve.reciprocal(esum[:, :], esum[:, :]))
                link(dve.tensor_tensor(wsel[:, :, :], top[:, :, :], spread(esum[:, :], 2, [P, TOK_TILES, 2]), ALU.mult))
                dve.wait_ge(tot_mm[L], 1)
                link(dve.tensor_copy(tot[:, :], ps[0:CHOICES, 3, 0:EXPERTS]))
                C3 = [CHOICES, CHOICES, EXPERTS]
                dve.tensor_tensor(carry[:, :, :], spread(before64[:, :], 2, C3), spread(tot[:, :], 1, C3),
                                  ALU.mult).then_inc(carry_set[L], 1)
                dve.wait_ge(pos_mm[L], 1)
                E3 = [P, EXPERTS, EXPERTS]
                link(dve.tensor_copy(off[:, :], ps[:, 4, 0:EXPERTS]))
                link(dve.tensor_tensor(cmp8[:, :, :], spread(off[:, :], 2, E3), spread(thr[:, :], 1, E3), ALU.is_gt))
                link(dve.tensor_reduce(ntile[:, :], cmp8[:, :, :], AX, ALU.add))
                link(dve.tensor_tensor(cmp8[:, :, :], before8[:, :, :], spread(ntile[:, :], 1, E3), ALU.mult))
                link(dve.tensor_reduce(first[:, :], cmp8[:, :, :], AX, ALU.add))
                link(dve.tensor_scalar(off[:, :], first[:, :], float(TILE), None, ALU.mult))
                W3 = [P, CHOICES, EXPERTS]
                link(dve.tensor_tensor(posw[:, :, :], ps[:, 5, :].rearrange("p (c e) -> p c e", e=EXPERTS),
                                       spread(off[:, :], 1, W3), ALU.add))
                link(dve.tensor_tensor(posw[:, :, :], posw[:, :, :],
                                       hot[:, :, :, :].rearrange("p t k e -> p (t k) e"), ALU.mult))
                link(dve.tensor_reduce(posf[:, :], posw[:, :, :], AX, ALU.add))
                if L == 1:
                    dve.wait_ge(z_ready[0], SEQS)
                dve.tensor_copy(pos[:, :], posf[:, :]).then_inc(pos_set[L], 1)
                N3 = [1, TILES, EXPERTS - 1]
                link(dve.tensor_tensor(ecmp[:, :, :], spread(first[0:1, 1:EXPERTS], 1, N3),
                                       spread(tile_no[:, :], 2, N3), ALU.is_le))
                link(dve.tensor_reduce(eidf[:, :], ecmp[:, :, :], AX, ALU.add))
                dve.tensor_copy(eid[:, :], eidf[:, :]).then_inc(pos_set[L], 1)

            def attend(u, g, b, now):
                g3, g2, gt = (g + 3) % GROUPS, (g + 2) % GROUPS, (g + 3) % GROUPS
                v, w = u + 2, u + 3
                for t in range(4):
                    for j in range(4):
                        i = t * 4 + j
                        if now.max:
                            dve.wait_ge(s_mm, v * 16 + (i + 1))
                            at = j * 4 + t
                            dve.tensor_reduce(nmax[:, g % 2, at:at + 1], ps[:, i % 2, :], AX, ALU.max,
                                              negate=True).then_inc(max_set, 1)
                    if t == 0 and now.low:
                        dve.wait_ge(mhi_set, u + 2)
                        dve.wait_ge(nmT_mm, u + 2)
                        if not (isinstance(u, int) and u + 1 < 2):
                            dve.wait_ge(m_in, u * 32)
                        r = (g + 1) % 2
                        dve.tensor_tensor(m_lo[:, r, :], ps[0:16, 6, 0:P], m_hi[:, r, :].bitcast(F32),
                                          ALU.subtract).then_inc(mlo_set, 1)
                    if t == 0 and now.tail:
                        dve.wait_ge(pv_mm, u * 4)
                        dve.tensor_copy(o_sb, ps[:, 5, :]).then_inc(o_read, 1)
                    if t == 0 and g == 0 and now.main:
                        dve.wait_ge(vtp_mm, b + 1)
                        dve.tensor_copy(vaug[:, :, :, 0:HD],
                                        ps[:, 6, :].rearrange("p (t h r) -> p t h r", t=QT, r=HD)).then_inc(vaug_set, 1)
                    if t in (1, 3) and now.proj:
                        which = t // 2
                        dst = (Qs, Ks)[which]
                        dve.wait_ge(hi_set, w * 2 + (which + 1))
                        dve.wait_ge(lo_set, w * 2 + (which + 1))
                        if not (isinstance(u, int) and u < 1):
                            dve.wait_ge(st_mm, u * 16)
                        dve.scalar_tensor_tensor(dst[:, g3, :], Hi[:, which, :].bitcast(F32), sign[:, which:which + 1],
                                                 Lo[:, which, :], ALU.mult, ALU.add).then_inc(stack_set, 1)
                    if t == 2 and now.tail:
                        dve.wait_ge(oT_mm, u)
                        turned = ps[:, 6, :].rearrange("p (q j r) -> p q j r", q=QT, j=4)
                        dve.reciprocal(rden[:, :, :], turned[:, :, :, HD]).then_inc(rden_set, 1)
                        dve.wait_ge(rden_set, u)
                        dve.tensor_tensor(onorm[:, :, 32 * gt:32 * gt + 32].rearrange("p q (j r) -> p q j r", j=4),
                                          turned[:, :, :, 0:HD], spread(rden[:, :, :], 3, [P, QT, 4, HD]),
                                          ALU.mult).then_inc(onorm_set, 1)
                    if t == 3 and g == 0 and now.tail:
                        dve.wait_ge(out_mm, b)
                        dve.tensor_tensor(rows_of(attn, b - 1), ps[:, 7, :].rearrange("p (q d) -> p q d", q=QT),
                                          spread(bproj_bc[:, :], 1, [P, QT, D]), ALU.add).then_inc(attn_set, 1)

            def experts(L):
                NW = 2 * (F0, F1)[L]
                nch = len(CH[L])

                def high_weights(i, r, k):
                    dve.wait_ge(up_in[L][r], (k + 1) * 32)
                    dve.tensor_copy(wu_hi[:, r, 0:NW], wraw[:, r, 0:NW]).then_inc(w_hi_set[L], 1)

                def low_rows(i, r):
                    dve.wait_ge(gT_mm[L], i + 1)
                    dve.wait_ge(ghi_set[L], i + 1)
                    dve.tensor_tensor(gT_lo[:, r, :], ps[:, 0, :], gT_hi[:, r, :].bitcast(F32),
                                      ALU.subtract).then_inc(glo_set[L], 1)

                def finish(i, r):
                    dve.wait_ge(down_mm[L], (i + 1) * nch)
                    dve.wait_ge(xb_set, i + 1)
                    y = ysb[:, r, :, :]
                    dve.scalar_tensor_tensor(y.rearrange("p q d -> p (q d)"), ps[:, 5 + r, :], 0.5,
                                             y.rearrange("p q d -> p (q d)"), ALU.mult, ALU.add
                                             ).then_inc(y_read[L], 1)
                    dve.wait_ge(y_read[L], i + 1)
                    for q in range(4):
                        dve.bn_stats(estats[:, q, :], ysb[:, r, q, :]).then_inc(est_chain, 1)
                    even, odd = estats[:, :, 0:3], estats[:, :, 3:6]
                    dve.wait_ge(est_chain, i * 10 + 4)
                    dve.tensor_tensor(eagg[:, 0, :], even[:, :, 1], odd[:, :, 1], ALU.add).then_inc(est_chain, 1)
                    dve.tensor_tensor(eagg[:, 1, :], even[:, :, 1], odd[:, :, 1], ALU.subtract).then_inc(est_chain, 1)
                    dve.tensor_tensor(eagg[:, 2, :], even[:, :, 2], odd[:, :, 2], ALU.add).then_inc(est_chain, 1)
                    dve.wait_ge(est_chain, i * 10 + 7)
                    dve.tensor_scalar(emean[:, :], eagg[:, 0, :], 0.5, None, ALU.mult).then_inc(est_chain, 1)
                    dve.tensor_tensor(eagg[:, 3, :], eagg[:, 1, :], eagg[:, 1, :], ALU.mult).then_inc(est_chain, 1)
                    dve.tensor_scalar(eagg[:, 4, :], eagg[:, 2, :], 1.0 / D, EPS_EXPERT, ALU.mult, ALU.add
                                      ).then_inc(est_chain, 1)
                    dve.wait_ge(est_chain, i * 10 + 10)
                    dve.scalar_tensor_tensor(everstd[:, r, :], eagg[:, 3, :], 0.25, eagg[:, 4, :],
                                             ALU.mult, ALU.add).then_inc(evar_set, 1)

                def normalize(i, r):
                    dve.wait_ge(erstd_set, i + 1)
                    for q in range(4):
                        ins = dve.tensor_scalar(ysb[:, r, q, :], ysb[:, r, q, :], emean[:, q:q + 1],
                                                everstd[:, r, q:q + 1], ALU.subtract, ALU.mult)
                    ins.then_inc(xhat_set, 1)

                def tile(i, r, k, first=False, last=False):
                    for f in range(nch):
                        n, par, M = i * nch + f, (r * nch + f) % 2, CH[L][f][1]
                        dve.wait_ge(act_set[L], n + 1)
                        if not (first and r == 0 and f < 2):
                            dve.wait_ge(down_mm[L], n - 1)
                        if L == 0:
                            dve.wait_ge(up_mm[L], n + 1)
                            dve.tensor_tensor(hT[0:M, par, :], ps[0:M, 2 + 2 * par, :], gact[0:M, par, :],
                                              ALU.mult).then_inc(h_set[L], 1)
                        else:
                            dve.scalar_tensor_tensor(hT[:, par, :], gsig[:, par, :], 1.0, gact[:, par, :],
                                                     ALU.add, ALU.mult).then_inc(h_set[L], 1)
                        if f == 0 and not last:
                            high_weights(i + 1, 1 - r, k + r)
                        if f == 1 and not last:
                            low_rows(i + 1, 1 - r)
                        if L == 1 and f == 1 and not (first and r == 0):
                            finish(i - 1, 1 - r)
                        if L == 1 and f == 2 and not (first and r == 0):
                            normalize(i - 1, 1 - r)

                high_weights(0, 0, 0)
                low_rows(0, 0)
                tile(0, 0, 0, first=True)
                tile(1, 1, 0, first=True)
                with dve.Fori(1, TILES // 2 - 1) as k:
                    tile(k * 2, 0, k)
                    tile(k * 2 + 1, 1, k)
                k = TILES // 2 - 1
                tile(k * 2, 0, k)
                tile(k * 2 + 1, 1, k, last=True)
                if L == 1:
                    finish(TILES - 1, 1)
                    normalize(TILES - 1, 1)

            def linear(b, fresh):
                if not fresh:
                    dve.wait_ge(y1_mm, b * 4)
                dve.wait_ge(kvt_mm, b * 2 + 2)
                for c in range(QT):
                    dve.tensor_tensor(vpad[:, c, :, :], spread(ps[:, 6, c * P:(c + 1) * P], 1, [P, 4, P]),
                                      head_cols[:, :, :], ALU.mult).then_inc(vpad_set, 1)
                for c in range(QT):
                    for s in range(4):
                        dve.wait_ge(sc_mm, b * 16 + (c * 4 + s + 1))
                        if s == 0 and not (fresh and c < 2):
                            dve.wait_ge(y1_mm, b * 4 + (c - 1))
                        dve.tensor_tensor(scores[:, c % 2, s, :].rearrange("p (v q) -> p v q", v=4),
                                          ps[:, s, :].rearrange("p (v q) -> p v q", v=4),
                                          spread(causal[:, :], 1, [P, 4, P]), ALU.mult).then_inc(sc_set, 1)
                    if c < QT - 1:
                        dve.wait_ge(kv_mm, b * 3 + (c + 1))
                        dve.tensor_tensor(state[:, c + 1, :], ps[:, 7, 0:P],
                                          same_head[:, :, :].rearrange("p h r -> p (h r)"), ALU.mult).then_inc(state_set, 1)
                dve.wait_ge(out1_mm, b + 1)
                dve.tensor_copy(rows_of(attn, b), ps[:, 5, :].rearrange("p (q d) -> p q d", q=QT)).then_inc(attn1_set, 1)

            def combine(L):
                def weigh(b):
                    r = b % 2
                    dve.wait_ge(gathered[L][r], 16 * 2 * QT * (b // 2 + 1))
                    if b >= 2:
                        dve.wait_ge(silu_set[L], b - 1)
                    for q in range(QT):
                        ins = dve.tensor_scalar(zg[:, r, q, :], yg[:, r, 2 * q, :],
                                                wsel[:, b * QT + q, 0:1], None, ALU.mult)
                    link(ins)
                    for q in range(QT):
                        ins = dve.scalar_tensor_tensor(zg[:, r, q, :], yg[:, r, 2 * q + 1, :],
                                                       wsel[:, b * QT + q, 1:2], zg[:, r, q, :], ALU.mult, ALU.add)
                    if L == 0:
                        link(ins)
                        ins = dve.tensor_tensor(zg[:, r, :, :], zg[:, r, :, :],
                                                spread(fbias_bc[:, :], 1, [P, QT, D]), ALU.add)
                    ins.then_inc(z_ready[L], 1)

                def add(b):
                    r = b % 2
                    dve.wait_ge(silu_set[L], b + 1)
                    link(dve.tensor_tensor(sg[:, r, :, :], sg[:, r, :, :], rows_of(attn, b), ALU.mult))
                    ins = dve.tensor_tensor(rows_of(xres, b), rows_of(xres, b), sg[:, r, :, :], ALU.add)
                    ins.then_inc(x_set[L], 1)
                    dve.wait_ge(x_set[L], b + 1)
                    if L == 0:
                        for t in range(b * QT, (b + 1) * QT):
                            link(statistics(t))

                for b in range(SEQS):
                    weigh(b)
                    if b >= 1:
                        add(b - 1)
                add(SEQS - 1)

            setup()
            norm(0)
            routing(0)
            dve.wait_ge(slots_zero, 48)
            link(dve.memset(vaug, 0.0))
            link(dve.memset(vaug[:, :, :, HD:HD + 1], 1.0))
            dve.sem_inc(attn_set, 1)
            dve.sem_inc(w_stack_set, 1)
            steps(dve, attend)
            experts(0)
            combine(0)
            norm(1)
            routing(1)
            dve.sem_inc(attn1_set, 1)
            linear(0, True)
            with dve.Fori(1, SEQS) as b:
                linear(b, False)
            experts(1)
            combine(1)


_INS = ['L0_attn_x', 'L0_attn_w_qkv', 'L0_attn_b_qkv', 'L0_attn_w_proj', 'L0_attn_b_proj', 'L0_ffn_router_w',
        'L0_ffn_w1', 'L0_ffn_v1', 'L0_ffn_w2', 'L0_ffn_bias', 'L1_attn_Wq', 'L1_attn_Wk', 'L1_attn_Wv',
        'L1_attn_Wc', 'L1_attn_Ltri', 'L1_ffn_Wr', 'L1_ffn_br', 'L1_ffn_Wi', 'L1_ffn_bi', 'L1_ffn_Wg',
        'L1_ffn_bg', 'L1_ffn_Wo', 'L1_ffn_bo', 'L1_ffn_gamma', 'L1_ffn_beta']


def kernel(**inputs):
    import numpy as np
    import concourse.bacc as bacc
    from concourse.bass_utils import run_bass_kernel_spmd

    nc = bacc.Bacc("TRN2", target_bir_lowering=False, num_devices=1)
    arrays, args = {}, []
    for name in _INS:
        a = np.ascontiguousarray(inputs[name])
        arrays[f"in_{name}"] = a
        args.append(nc.dram_tensor(f"in_{name}", a.shape, mybir.dt.from_np(a.dtype), kind="ExternalInput").ap())
    shape = inputs['L0_attn_x'].shape
    args.append(nc.dram_tensor("out_x", shape, F32, kind="ExternalOutput").ap())
    build(nc, *args)
    r = run_bass_kernel_spmd(nc, [arrays], core_ids=[0])
    return r.results[0]["out_x"]
```

```python
from contextlib import ExitStack

import concourse.bass as bass
from concourse import mybir

F32 = mybir.dt.float32
F32R = mybir.dt.float32r
BF16 = mybir.dt.bfloat16
I32 = mybir.dt.int32
U32 = mybir.dt.uint32
ALU = mybir.AluOpType
ACT = mybir.ActivationFunctionType
AX = mybir.AxisListType.X

P = 128
EXPERTS = 8
SEQS = 8
SEQ = 512
QT = SEQ // P
TOK_TILES = SEQS * QT
HEADS = 16
HD = 8
GROUPS = 4
TILE = 512
TILES = 24
CHOICES = 2 * TOK_TILES
EPS_LN = 1e-5
EPS_EXPERT = 1e-12


def build(nc, x, w_qkv, b_qkv, w_proj, b_proj, router_w, w1, v1, w2, ffn_bias,
          Wq, Wk, Wv, Wc, Ltri, Wr, br, Wi, bi, Wg, bg, Wo, bo, gamma, beta, out):
    D = x.shape[2]
    F0 = w1.shape[2]
    F1 = Wi.shape[2]
    SCALE = float(HD) ** -0.5
    CH = [[(0, 128), (128, 128), (256, F0 - 256)], [(c * 128, 128) for c in range(F1 // 128)]]
    FMAX = F1
    slots_x = nc.dram_tensor("slots_x", [TILES * TILE, D], F32, kind="Internal").ap()
    slots_y = nc.dram_tensor("slots_y", [TILES * TILE, D], F32, kind="Internal").ap()

    ctx = ExitStack()
    with ctx:
        def sb(name, shape, dt=F32):
            return ctx.enter_context(nc.sbuf_tensor(name, shape, dt))

        def sem(name):
            return ctx.enter_context(nc.semaphore(name))

        ps = ctx.enter_context(nc.psum_tensor("ps", [P, 8, 512], F32))

        with nc.sbuf_tensor("Km01", [P, 2, 4, SEQ], F32R) as Km01:
            pass
        xres = sb("xres", [P, TOK_TILES, D])
        xn = sb("xn", [P, TOK_TILES, D])
        attn = sb("attn", [P, TOK_TILES, D])
        xT_hi = sb("xT_hi", [P, SEQS, SEQ], F32R)
        xT_lo = sb("xT_lo", [P, SEQS, SEQ], F32R)

        ident = sb("ident", [P, P])
        before = sb("before", [P, P], BF16)
        ones_b = sb("ones_b", [P, 1], BF16)
        before64 = sb("before64", [CHOICES, CHOICES])
        ones64 = sb("ones64", [CHOICES, P])
        causal = sb("causal", [P, P])
        tri = sb("tri", [P, P], F32R)
        cotri = sb("cotri", [P, P], F32R)
        key8 = sb("key8", [P, EXPERTS])
        thr = sb("thr", [P, EXPERTS])
        before8 = sb("before8", [P, EXPERTS, EXPERTS])
        tile_no = sb("tile_no", [1, TILES])
        half = sb("half", [P, TOK_TILES])
        LOQ, LOK, BQ, BK, BV, NROWS = 0, 1, 2, 6, 10, 11
        rows = sb("rows", [1, NROWS, P])
        one_row = sb("one_row", [1, P])
        cols = sb("cols", [P, NROWS])
        sign = sb("sign", [P, 2])
        lobias = sb("lobias", [P, 2, GROUPS])
        bproj_bc = sb("bproj_bc", [P, D])
        fbias_bc = sb("fbias_bc", [P, D])
        br_bc = sb("br_bc", [P, EXPERTS])
        bqkv_row = sb("bqkv_row", [1, 3 * D])

        wqkv = sb("wqkv", [P, 3 * D])
        ws_hi = sb("ws_hi", [P, 2, GROUPS, P], F32R)
        ws_lo = sb("ws_lo", [P, 2, GROUPS, P], F32R)
        wv_hi = sb("wv_hi", [P, D], F32R)
        wv_lo = sb("wv_lo", [P, D], F32R)
        wproj = sb("wproj", [P, D])
        wrout = sb("wrout", [P, 2, EXPERTS])
        w4 = sb("w4", [P, 4, D])
        w4T = sb("w4T", [P, 4, D])
        w3_hi = sb("w3_hi", [P, 3, D], F32R)
        w3_lo = sb("w3_lo", [P, 3, D], F32R)
        ltri = sb("ltri", [P, HD])
        ldiag = sb("ldiag", [P, HEADS, HD])
        ldiagT = sb("ldiagT", [P, P])
        bdiag = sb("bdiag", [P, P])
        wcomb = sb("wcomb", [P, D])
        ebias_rows = sb("ebias_rows", [2 * 4 * EXPERTS, P])
        ebias = sb("ebias", [P, EXPERTS, 8])

        stats = sb("stats", [P, TOK_TILES, 6])
        mv = sb("mv", [P, TOK_TILES, 2])
        veps = sb("veps", [P, TOK_TILES])
        rstd = sb("rstd", [P, TOK_TILES])
        logits = sb("logits", [P, TOK_TILES, EXPERTS])
        elog = sb("elog", [P, TOK_TILES, EXPERTS])
        esum = sb("esum", [P, TOK_TILES])
        top = sb("top", [P, TOK_TILES, 2])
        pick = sb("pick", [P, TOK_TILES, EXPERTS])
        kmax = sb("kmax", [P, TOK_TILES])
        lmax = sb("lmax", [P, TOK_TILES])
        hot = sb("hot", [P, TOK_TILES, 2, EXPERTS])
        hot_b = sb("hot_b", [P, TOK_TILES, 2, EXPERTS], BF16)
        wsel = sb("wsel", [P, TOK_TILES, 2])
        tot = sb("tot", [CHOICES, EXPERTS])
        carry = sb("carry", [CHOICES, CHOICES, EXPERTS])
        cmp8 = sb("cmp8", [P, EXPERTS, EXPERTS])
        ntile = sb("ntile", [P, EXPERTS])
        first = sb("first", [P, EXPERTS])
        off = sb("off", [P, EXPERTS])
        posw = sb("posw", [P, CHOICES, EXPERTS])
        posf = sb("posf", [P, CHOICES])
        pos = sb("pos", [P, CHOICES], U32)
        ecmp = sb("ecmp", [1, TILES, EXPERTS - 1])
        eidf = sb("eidf", [1, TILES])
        eid = sb("eid", [1, TILES], I32)

        zero_col = sb("zero_col", [P, 1])
        rden = sb("rden", [P, QT, 4])
        nmax = sb("nmax", [P, 2, 16])
        m_hi = sb("m_hi", [16, 2, P], F32R)
        m_lo = sb("m_lo", [16, 2, P], F32R)
        ebcol = sb("ebcol", [P, 2, 8])
        estats = sb("estats", [P, 4, 6])
        eagg = sb("eagg", [P, 5, 4])
        emean = sb("emean", [P, 4])
        everstd = sb("everstd", [P, 2, 4])

        def stage():
            space = ExitStack()
            count = [0]

            def take(*shape, dt=F32):
                count[0] += 1
                return space.enter_context(nc.sbuf_tensor(f"stage{len(stages)}_{count[0]}", [P, *shape], dt)
                                           )[tuple([slice(None)] * (1 + len(shape)))]
            stages.append(space)
            return take, lambda *shape: take(*shape, dt=F32R)

        stages = []
        take, take_r = stage()
        zeros = take(4096)
        wstack = take(2, GROUPS * 4, 32)
        stages[-1].close()
        take, take_r = stage()
        Qs = take_r(GROUPS, SEQ)
        Ks = take_r(2, SEQ)
        Km23 = take_r(2, 4, SEQ)
        Km = [Km01[:, 0, :, :], Km01[:, 1, :, :], Km23[:, 0, :, :], Km23[:, 1, :, :]]
        Hi = take_r(2, SEQ)
        Lo = take(2, SEQ)
        probs = take(2, 4, SEQ)
        vaug = take(QT, HEADS, 32)
        vT = take(SEQ)
        o_sb = take(SEQ)
        onorm = take(QT, D)
        onT = take(SEQ)
        stages[-1].close()
        take, take_r = stage()
        xs = take_r(4, 2, P)
        qkv = take(4, 3, D)
        kv = take(2, HEADS, HD, HD)
        kv_hi = take_r(4, HEADS * HD * HD)
        kv_lo = take_r(4, HEADS * HD * HD)
        qkv_sum = take(HEADS, HD, HD)
        y1 = take(2, D)
        y1T = take(2, P)
        stages[-1].close()
        take, take_r = stage()
        wu_hi = take_r(2, 2 * F1)
        wu_lo = take_r(2, 2 * F1)
        gT_hi = take_r(2, TILE)
        gT_lo = take_r(2, TILE)
        wraw = take(2, 2 * F1)
        wdn = take(2, 4, D)
        xg = take(2, 4, D)
        gact = take(2, TILE)
        gsig = take(2, TILE)
        hT = take(2, TILE)
        ysb = take(2, 4, D)
        vecs = take(2, 3, D)
        stages[-1].close()
        take, take_r = stage()
        yg = take(2, QT * 2, D)
        zg = take(2, QT, D)
        sg = take(2, QT, D)
        stages[-1].close()

        ld_x = sem("ld_x")
        ld_x_again = sem("ld_x_again")
        ld_a = sem("ld_a")
        ld_b = sem("ld_b")
        zero_set = sem("zero_set")
        slots_zero = sem("slots_zero")
        pool_mem = sem("pool_mem")
        pool_con = sem("pool_con")
        rows_set = sem("rows_set")
        dve_chain = sem("dve_chain")
        pe_setup = sem("pe_setup")
        setup_ev = sem("setup_ev")
        setup_done = sem("setup_done")
        two = lambda name: [sem(f"{name}{L}") for L in range(2)]
        veps_set, rstd_set, xn_set = two("veps_set"), two("rstd_set"), two("xn_set")
        tp_done, xhi_set, xlo_set = two("tp_done"), two("xhi_set"), two("xlo_set")
        logit_mm, z_set, e_set = two("logit_mm"), two("z_set"), two("e_set")
        hot_set, tot_mm, carry_set = two("hot_set"), two("tot_mm"), two("carry_set")
        pos_mm, pos_set, scattered = two("pos_mm"), two("pos_set"), two("scattered")
        up_in = [[sem(f"up_in{L}{r}") for r in range(2)] for L in range(2)]
        xg_in = [[sem(f"xg_in{L}{r}") for r in range(2)] for L in range(2)]
        dn_in = [[sem(f"dn_in{L}{r}") for r in range(2)] for L in range(2)]
        vec_in = [sem(f"vec_in{r}") for r in range(2)]
        w_hi_set, w_lo_set = two("w_hi_set"), two("w_lo_set")
        gT_mm, ghi_set, glo_set = two("gT_mm"), two("ghi_set"), two("glo_set")
        gate_mm, up_mm, act_set = two("gate_mm"), two("up_mm"), two("act_set")
        h_set, down_mm, y_read = two("h_set"), two("down_mm"), two("y_read")
        xb_set, y_set = sem("xb_set"), two("y_set")
        est_chain, evar_set, erstd_set, xhat_set, gam_set = (
            sem("est_chain"), sem("evar_set"), sem("erstd_set"), sem("xhat_set"), sem("gam_set"))
        y_stored = [[sem(f"y_stored{L}{r}") for r in range(2)] for L in range(2)]
        gelu_set, w_stack_set = sem("gelu_set"), sem("w_stack_set")
        gathered = [[sem(f"gathered{L}{r}") for r in range(2)] for L in range(2)]
        z_ready, silu_set, x_set = two("z_ready"), two("silu_set"), two("x_set")
        stored = sem("stored")
        proj_mm, hi_set, lo_set, stack_set = (
            sem("proj_mm"), sem("hi_set"), sem("lo_set"), sem("stack_set"))
        s_mm, max_set, nmT_mm, mhi_set, mlo_set, m_in = (
            sem("s_mm"), sem("max_set"), sem("nmT_mm"), sem("mhi_set"), sem("mlo_set"), sem("m_in"))
        k_in, km_zero = sem("k_in"), sem("km_zero")
        st_mm, exp_set, pv_mm, o_read, oT_mm, onorm_set = (
            sem("st_mm"), sem("exp_set"), sem("pv_mm"), sem("o_read"), sem("oT_mm"), sem("onorm_set"))
        rden_set = sem("rden_set")
        vT_mm, vT_set, vtp_mm, vaug_set = sem("vT_mm"), sem("vT_set"), sem("vtp_mm"), sem("vaug_set")
        vaug_const = sem("vaug_const")
        onT_mm, onT_set, out_mm, attn_set = sem("onT_mm"), sem("onT_set"), sem("out_mm"), sem("attn_set")
        xs_in = [sem(f"xs_in{n}") for n in range(4)]
        qkv_mm, qkv_set, kv_set, kv_hi_set, kv_lo_set = (
            sem("qkv_mm"), sem("qkv_set"), sem("kv_set"), sem("kv_hi_set"), sem("kv_lo_set"))
        sum_mm, weigh_set, y1_set, y1T_mm, y1T_set, out1_mm, attn1_set = (
            sem("sum_mm"), sem("weigh_set"), sem("y1_set"), sem("y1T_mm"), sem("y1T_set"),
            sem("out1_mm"), sem("attn1_set"))

        def spread(ap, axis, shape):
            return ap.unsqueeze(axis).to_broadcast(shape)

        def seq_of(tile, b):
            return tile[:, b, :] if isinstance(b, int) else tile[:, bass.ds(b, 1), :].rearrange("p a n -> p (a n)")

        def rows_of(tile, b):
            return tile[:, b * QT:(b + 1) * QT, :] if isinstance(b, int) else tile[:, bass.ds(b * QT, QT), :]

        def split3(pe, out_ap, w_hi_ap, w_lo_ap, x_hi_ap, x_lo_ap, start=True, stop=True):
            pe.matmul(out_ap, w_hi_ap, x_hi_ap, start=start, stop=False)
            pe.matmul(out_ap, w_hi_ap, x_lo_ap, start=False, stop=False)
            return pe.matmul(out_ap, w_lo_ap, x_hi_ap, start=False, stop=stop)

        def steps(eng, step):
            class Now:
                def __init__(self, u):
                    self.main, self.tail = 0 <= u < 32, 1 <= u <= 32
                    self.max, self.proj, self.low = 0 <= u + 2 < 32, 0 <= u + 3 < 32, 0 <= u + 1 < 32
                    self.first = u < 1
            for u in range(-3, 1):
                step(u, u % GROUPS, u // GROUPS, Now(u))
            with eng.Fori(0, SEQS - 1) as b:
                for s in range(1, 5):
                    step(b * 4 + s, s % GROUPS, b + s // GROUPS, Now(s + 4))
            for u in range(29, 33):
                step(u, u % GROUPS, u // GROUPS, Now(u))

        def chunk_steps(eng, step):
            for m in range(-4, 2):
                step(m, m, 0, lambda n, m=m: 0 <= m + n < TOK_TILES)
            with eng.Fori(0, TOK_TILES // 8 - 1) as k:
                for s in range(2, 10):
                    step(k * 8 + s, s, k, lambda n: True)
            for m in range(26, TOK_TILES + 2):
                step(m, m, 0, lambda n, m=m: 0 <= m + n < TOK_TILES)

        def chunk_of(s, k):
            return k * 2 + (s // 8 * 2 + s % 2), s % 8 // 2

        N_A, N_B = 8, 7
        NDN = [2, 2]
        block = ctx.enter_context(nc.Block())

        @block.sync
        def _(sp):
            sp.dma_start(xres[:, :, :], x.rearrange("s (t p) d -> p (s t) d", p=P)).then_inc(ld_x, 16)
            sp.dma_start(wqkv[:, :], w_qkv).then_inc(ld_a, 16)
            sp.dma_start(bqkv_row[:, :], b_qkv.rearrange("(a n) -> a n", a=1)).then_inc(ld_a, 16)
            sp.dma_start(wproj[:, :], w_proj).then_inc(ld_a, 16)
            sp.dma_start(wrout[:, 0, :], router_w).then_inc(ld_a, 16)
            sp.dma_start(wrout[:, 1, :], Wr).then_inc(ld_a, 16)
            sp.dma_start(bproj_bc[:, :], b_proj.partition_broadcast(P)).then_inc(ld_a, 16)
            sp.dma_start(fbias_bc[:, :], ffn_bias.partition_broadcast(P)).then_inc(ld_a, 16)
            sp.dma_start(br_bc[:, :], br.partition_broadcast(P)).then_inc(ld_a, 16)
            for n, w in enumerate((Wq, Wk, Wv, Wc)):
                sp.dma_start(w4[:, n, :], w).then_inc(ld_b, 16)
            sp.dma_start(ltri[:, :], Ltri.rearrange("h e f -> (h e) f")).then_inc(ld_b, 16)
            nb = 4 * EXPERTS
            sp.dma_start(ebias_rows[0:nb, :], bi.rearrange("e (c p) -> (e c) p", p=P)).then_inc(ld_b, 16)
            sp.dma_start(ebias_rows[nb:2 * nb, :], bg.rearrange("e (c p) -> (e c) p", p=P)).then_inc(ld_b, 16)
            sp.wait_ge(zero_set, 1)
            fill = slots_x.rearrange("(p a) d -> p (a d)", p=P)
            for n in range(3):
                sp.dma_start(fill[:, n * 4096:(n + 1) * 4096], zeros).then_inc(slots_zero, 16)

            def max_rows(u, r, g):
                sp.wait_ge(mhi_set, u + 1)
                sp.wait_ge(mlo_set, u + 1)
                for row, src in ((24, m_hi), (25, m_lo)):
                    dst = Qs[row:P:32, g, :].bitcast(F32)
                    sp.dma_start(dst, src[:, r, :].bitcast(F32)).then_inc(m_in, 16)

            def mask_keys(w, g):
                sp.wait_ge(stack_set, w * 2 + 1)
                for j in range(4):
                    h = slice(32 * j, 32 * j + 32)
                    sp.dma_start(Km[g][h, j, :].bitcast(F32), Ks[h, g % 2, :].bitcast(F32)).then_inc(k_in, 16)

            def attend(u, g, b, now):
                if now.low:
                    max_rows(u + 1, (g + 1) % 2, (g + 1) % GROUPS)
                if now.proj:
                    mask_keys(u + 3, (g + 3) % GROUPS)

            sp.wait_ge(km_zero, 1)
            steps(sp, attend)

            def expert_loads(L):
                nch = len(CH[L])
                F = (F0, F1)[L]
                gate, up, down = ((w1, v1, w2), (Wi, Wg, Wo))[L]

                def expert_of(i):
                    return sp.value_load(eid[0:1, bass.ds(i, 1)], min_val=0, max_val=EXPERTS - 1)

                def load_up(i, r, e=None):
                    e = expert_of(i) if e is None else e
                    for n, w in enumerate((gate, up)):
                        sp.dma_start(wraw[:, r, n * F:(n + 1) * F],
                                     w[bass.ds(e, 1), :, :].rearrange("a p n -> (a p) n")).then_inc(up_in[L][r], 16)

                def load_x(i, r):
                    sp.dma_start(xg[:, r, :, :].rearrange("p k d -> p (k d)"),
                                 slots_x[bass.ds(i * TILE, TILE), :].rearrange("(p k) d -> p (k d)", p=P)
                                 ).then_inc(xg_in[L][r], 16)

                def load_down(i, r, e=None):
                    e = expert_of(i) if e is None else e
                    wd = down[bass.ds(e, 1), :, :].rearrange("a f n -> (a f) n")
                    if L == 0:
                        sp.dma_start(wdn[:, r, 0:2, :],
                                     wd[0:2 * P, :].rearrange("(c p) n -> p c n", p=P)).then_inc(dn_in[L][r], 16)
                        sp.dma_start(wdn[0:F - 2 * P, r, 2, :], wd[2 * P:F, :]).then_inc(dn_in[L][r], 16)
                    else:
                        sp.dma_start(wdn[:, r, :, :],
                                     wd.rearrange("(c p) n -> p c n", p=P)).then_inc(dn_in[L][r], 16)
                        sp.dma_start(ebcol[:, r, :],
                                     ebias[:, bass.ds(e, 1), :].rearrange("p a n -> p (a n)")).then_inc(dn_in[L][r], 16)

                def load_vecs(i, r, e=None):
                    e = expert_of(i) if e is None else e
                    for n, w in enumerate((bo, gamma, beta)):
                        sp.dma_start(vecs[:, r, n, :],
                                     w[bass.ds(e, 1), :].to_broadcast([P, D])).then_inc(vec_in[r], 16)

                sp.wait_ge(pos_set[L], 2)
                sp.wait_ge(scattered[L], 16 * CHOICES)
                sp.wait_ge((attn_set, attn1_set)[L], (SEQS + 1, TOK_TILES)[L])
                for i in range(2):
                    load_up(i, i)
                    load_x(i, i)
                    load_down(i, i)
                    if L == 1:
                        load_vecs(i, i)
                sp.wait_ge(w_lo_set[L], 1)
                load_up(2, 0)

                def refill(i, r, down=True, up=True):
                    e1 = expert_of(i + 1) if down else None
                    e3 = expert_of(i + 3) if up else None
                    if down:
                        sp.wait_ge(down_mm[L], i * nch)
                        load_down(i + 1, 1 - r, e1)
                    if up:
                        sp.wait_ge(w_lo_set[L], i + 2)
                        load_up(i + 3, 1 - r, e3)
                    sp.wait_ge(gT_mm[L], i + 1)
                    if L == 1:
                        sp.wait_ge(xb_set, i + 1)
                    load_x(i + 2, r)
                    if L == 1 and down:
                        sp.wait_ge(y_set[1], i)
                        load_vecs(i + 1, 1 - r, e1)

                refill(0, 0, down=False)
                with sp.Fori(0, (TILES - 4) // 2) as k:
                    refill(k * 2 + 1, 1)
                    refill(k * 2 + 2, 0)
                refill(TILES - 3, 1, up=False)
                sp.wait_ge(down_mm[L], (TILES - 2) * nch)
                load_down(TILES - 1, 1)
                if L == 1:
                    sp.wait_ge(y_set[1], TILES - 2)
                    load_vecs(TILES - 1, 1)

            sp.wait_ge(attn_set, SEQS + 1)
            sp.dma_start(xres[:, :, :], x.rearrange("s (t p) d -> p (s t) d", p=P)).then_inc(ld_x_again, 16)
            expert_loads(0)

            def load_chunk(m, s, k, now):
                if now(4):
                    if now(0):
                        sp.wait_ge(qkv_mm, m + 1)
                    b, c = chunk_of(s + 4, k)
                    for n, src in enumerate((xT_hi, xT_lo)):
                        sp.dma_start(xs[:, s % 4, n, :].bitcast(F32),
                                     seq_of(src, b)[:, c * P:(c + 1) * P].bitcast(F32)).then_inc(xs_in[s % 4], 16)

            sp.wait_ge(pos_set[1], 2)
            sp.wait_ge(xlo_set[1], SEQS)
            chunk_steps(sp, load_chunk)
            expert_loads(1)
            for b in range(SEQS):
                sp.wait_ge(x_set[1], b + 1)
                sp.dma_start(out[b, :, :].rearrange("(t p) d -> p t d", p=P),
                             xres[:, QT * b:QT * (b + 1), :]).then_inc(stored, 16)
            sp.wait_ge(stored, 16 * SEQS)

        @block.gpsimd
        def _(pool):
            def fill(ap, value):
                pool.memset(ap, value).then_inc(pool_mem, 1)

            fill(ident[:, :], 0.0)
            fill(before[:, :], 1.0)
            fill(ones_b[:, :], 1.0)
            fill(before64[:, :], 1.0)
            fill(ones64[:, :], 1.0)
            fill(causal[:, :], 1.0)
            fill(before8[:, :, :], 1.0)
            fill(half[:, :], -0.5)
            fill(one_row[:, :], 1.0)
            pool.wait_ge(pool_mem, 9)

            def keep(ap, pattern, base, mult, op=ALU.is_ge, fill_with=0.0):
                pool.affine_select(out=ap, in_=ap, compare_op=op, fill=fill_with, base=base,
                                   pattern=pattern, channel_multiplier=mult).then_inc(pool_con, 1)

            keep(ident[:, :], [[-1, P]], 0, 1, ALU.not_equal, 1.0)
            keep(before[:, :], [[1, P]], -1, -1)
            keep(before64[:, :], [[1, CHOICES]], -1, -1)
            keep(causal[:, :], [[1, P]], 0, -1)
            keep(before8[:, :, :], [[1, EXPERTS], [-1, EXPERTS]], -1, 0)
            pool.iota(key8[:, :], [[-1, EXPERTS]], base=EXPERTS, channel_multiplier=0,
                      allow_small_or_imprecise_dtypes=True).then_inc(pool_con, 1)
            pool.iota(thr[:, :], [[TILE, EXPERTS]], base=0, channel_multiplier=0,
                      allow_small_or_imprecise_dtypes=True).then_inc(pool_con, 1)
            pool.iota(tile_no[:, :], [[1, TILES]], base=0, channel_multiplier=0,
                      allow_small_or_imprecise_dtypes=True).then_inc(pool_con, 1)
            pool.wait_ge(ld_b, 16 * N_B)
            pool.tensor_copy(ldiag[:, :, :], spread(ltri[:, :], 1, [P, HEADS, HD])).then_inc(pool_con, 1)
            pool.wait_ge(pool_con, 9)
            keep(ldiag[:, :, :], [[-HD, HEADS], [-1, HD]], 0, 1)
            pool.wait_ge(pool_con, 10)
            keep(ldiag[:, :, :], [[HD, HEADS], [0, HD]], HD - 1, -1)

            def outer(m):
                pool.wait_ge(qkv_set, m + 1)
                if m >= 2:
                    pool.wait_ge(kv_lo_set, m - 1)
                four = [P, HEADS, HD, HD]
                by_head = qkv[:, m % 4, :, :].rearrange("p n (h r) -> p n h r", r=HD)
                pool.tensor_tensor(kv[:, m % 2, :, :, :], spread(by_head[:, 1, :, :], 2, four),
                                   spread(by_head[:, 2, :, :], 3, four), ALU.mult).then_inc(kv_set, 1)

            def norm_and_scatter(L):
                pool.wait_ge(veps_set[L], 1)
                pool.tensor_tensor(rstd[:, :], veps[:, :], half[:, :], ALU.pow).then_inc(rstd_set[L], 1)
                pool.wait_ge(pos_set[L], 1)
                if L == 0:
                    pool.wait_ge(slots_zero, 48)
                if L == 1:
                    for m in (0, 1):
                        outer(m)
                for c in range(CHOICES):
                    if L == 1 and c % 2 == 0 and c // 2 + 2 < TOK_TILES:
                        outer(c // 2 + 2)
                    pool.indirect_dma_start(
                        out=slots_x, out_offset=bass.IndirectOffsetOnAxis(ap=pos[:, c:c + 1], axis=0),
                        in_=xn[:, c // 2, :], in_offset=None).then_inc(scattered[L], 16)

            def experts(L):
                NW = 2 * (F0, F1)[L]
                nch = len(CH[L])

                def low_weights(i, r):
                    pool.wait_ge(w_hi_set[L], i + 1)
                    pool.tensor_tensor(wu_lo[:, r, 0:NW], wraw[:, r, 0:NW],
                                       wu_hi[:, r, 0:NW].bitcast(F32), ALU.subtract).then_inc(w_lo_set[L], 1)

                def add_bias(i, r, k):
                    pool.wait_ge(vec_in[r], (k + 1) * 48)
                    pool.wait_ge(xg_in[L][r], (k + 1) * 16)
                    pool.wait_ge(y_stored[L][r], (k + 1) * 16)
                    pool.tensor_tensor(ysb[:, r, :, :], xg[:, r, :, :],
                                       spread(vecs[:, r, 0, :], 1, [P, 4, D]), ALU.add).then_inc(xb_set, 1)

                def finish(i, r):
                    pool.wait_ge(evar_set, i + 1)
                    pool.tensor_tensor(everstd[:, r, :], everstd[:, r, :], half[:, 0:4], ALU.pow
                                       ).then_inc(erstd_set, 1)
                    pool.wait_ge(xhat_set, i + 1)
                    pool.tensor_tensor(ysb[:, r, :, :], ysb[:, r, :, :],
                                       spread(vecs[:, r, 1, :], 1, [P, 4, D]), ALU.mult).then_inc(gam_set, 1)
                    pool.wait_ge(gam_set, i + 1)
                    pool.tensor_tensor(ysb[:, r, :, :], ysb[:, r, :, :],
                                       spread(vecs[:, r, 2, :], 1, [P, 4, D]), ALU.add).then_inc(y_set[L], 1)

                low_weights(0, 0)
                low_weights(1, 1)
                if L == 0:
                    with pool.Fori(1, TILES // 2) as k:
                        for r in range(2):
                            low_weights(k * 2 + r, r)
                    return
                add_bias(0, 0, 0)
                low_weights(2, 0)
                add_bias(1, 1, 0)
                finish(0, 0)
                with pool.Fori(1, TILES // 2 - 1) as k:
                    low_weights(k * 2 + 1, 1)
                    add_bias(k * 2, 0, k)
                    finish(k * 2 - 1, 1)
                    low_weights(k * 2 + 2, 0)
                    add_bias(k * 2 + 1, 1, k)
                    finish(k * 2, 0)
                low_weights(TILES - 1, 1)
                add_bias(TILES - 2, 0, TILES // 2 - 1)
                finish(TILES - 3, 1)
                add_bias(TILES - 1, 1, TILES // 2 - 1)
                finish(TILES - 2, 0)
                finish(TILES - 1, 1)

            def gather(L):
                for r in range(2):
                    pool.wait_ge(y_stored[L][r], 16 * (TILES // 2 + 1))
                pool.wait_ge(down_mm[L], TILES * len(CH[L]))
                for b in range(SEQS):
                    r = b % 2
                    if b >= 2:
                        pool.wait_ge(z_ready[L], b - 1)
                    for n in range(2 * QT):
                        c = 2 * QT * b + n
                        pool.indirect_dma_start(
                            out=yg[:, r, n, :], out_offset=None, in_=slots_y,
                            in_offset=bass.IndirectOffsetOnAxis(ap=pos[:, c:c + 1], axis=0)
                        ).then_inc(gathered[L][r], 16)

            norm_and_scatter(0)
            experts(0)
            gather(0)
            norm_and_scatter(1)
            experts(1)
            gather(1)

        @block.tensor
        def _(pe):
            pe.wait_ge(pool_mem, 9)
            pe.wait_ge(rows_set, 1)
            for n in range(NROWS):
                mm = pe.matmul(ps[:, 7, n:n + 1], rows[0:1, n, :], one_row[0:1, 0:1], start=True, stop=True)
            mm.then_inc(pe_setup, 1)
            pe.wait_ge(pool_con, 11)
            pe.wait_ge(ld_b, 16 * N_B)
            for n in range(4):
                pe.transpose(ps[:, 5, n * P:(n + 1) * P], w4[:, n, :], ident[:, :])
            nb = 8 * EXPERTS
            pe.transpose(ps[:, 3, 0:nb], ebias_rows[:, :], ident[0:nb, 0:nb])
            pe.transpose(ps[:, 4, 0:P], ldiag[:, :, :].rearrange("p h d -> p (h d)"), ident[:, :]).then_inc(pe_setup, 1)
            pe.wait_ge(setup_ev, 1)
            pe.matmul(ps[:, 4, P:2 * P], ldiagT[:, :], ldiagT[:, :], start=True, stop=True).then_inc(pe_setup, 1)
            pe.wait_ge(setup_ev, 2)
            pe.matmul(ps[:, 4, 2 * P:3 * P], bdiag[:, :], w4T[:, 3, :], start=True, stop=True).then_inc(pe_setup, 1)

            def norm(L):
                def router(b):
                    pe.wait_ge(xhi_set[L], b + 1)
                    pe.wait_ge(xlo_set[L], b + 1)
                    for t in range(QT):
                        at = (b * QT + t) * EXPERTS
                        for n, half_x in enumerate((xT_hi, xT_lo)):
                            mm = pe.matmul(ps[:, 2, at:at + EXPERTS],
                                           half_x[:, b, t * P:(t + 1) * P].bitcast(F32), wrout[:, L, :],
                                           start=(n == 0), stop=(n == 1))
                    mm.then_inc(logit_mm[L], 1)

                if L == 0:
                    pe.wait_ge(ld_a, 16 * N_A)
                for b in range(SEQS):
                    pe.wait_ge(xn_set[L], b + 1)
                    if b >= 2:
                        pe.wait_ge(xhi_set[L], b - 1)
                        pe.wait_ge(xlo_set[L], b - 1)
                    for t in range(QT):
                        mm = pe.transpose(ps[:, b % 2, t * P:(t + 1) * P], xn[:, b * QT + t, :], ident[:, :])
                    mm.then_inc(tp_done[L], 1)
                    if b >= 1:
                        router(b - 1)
                router(SEQS - 1)

            def routing(L):
                pe.wait_ge(hot_set[L], 1)
                for e in range(EXPERTS):
                    mm = pe.matmul(ps[0:CHOICES, 3, e:e + 1],
                                   hot_b[:, :, :, e].rearrange("p t k -> p (t k)"), ones_b[:, :],
                                   start=True, stop=True)
                mm.then_inc(tot_mm[L], 1)
                pe.wait_ge(carry_set[L], 1)
                pe.matmul(ps[:, 4, 0:EXPERTS], ones64[:, :], tot[:, :], start=True, stop=True)
                pe.matmul(ps[:, 5, :], before[:, :], hot_b[:, :, :, :].rearrange("p t k e -> p (t k e)"),
                          start=True, stop=False)
                pe.matmul(ps[:, 5, :], ones64[:, :], carry[:, :, :].rearrange("p c e -> p (c e)"),
                          start=False, stop=True).then_inc(pos_mm[L], 1)

            def attend(u, g, b, now):
                v, w = u + 2, u + 3
                bw = b if g == 0 else b + 1
                for t in range(4):
                    if t == 0 and now.main:
                        pe.wait_ge(m_in, (u + 1) * 32)
                    if t == 0 and now.max:
                        pe.wait_ge(stack_set, (v + 1) * 2)
                        pe.wait_ge(k_in, (v + 1) * 64)
                    for j in range(4):
                        i = t * 4 + j
                        if now.main:
                            free = {0: 0, 1: 3, 2: 3}.get(i, 2)
                            if not (now.first and i < 3):
                                pe.wait_ge(exp_set, u * 16 + (i - free))
                            pe.matmul(ps[:, 2 + i % 3, :], Km[g][:, j, t * P:(t + 1) * P], Qs[:, g, :],
                                      start=True, stop=True).then_inc(st_mm, 1)
                        if now.max:
                            if not (isinstance(v, int) and v * 16 + i < 2):
                                pe.wait_ge(max_set, v * 16 + (i - 1))
                            g2 = (g + 2) % GROUPS
                            pe.matmul(ps[:, i % 2, :], Qs[:, g2, t * P:(t + 1) * P], Km[g2][:, j, :],
                                      start=True, stop=True).then_inc(s_mm, 1)
                        if j == 1 and t == 0 and now.tail:
                            output(u - 1, (g + 3) % GROUPS, 3)
                        if j == 1 and t == 0 and now.low:
                            pe.wait_ge(max_set, (u + 2) * 16)
                            if isinstance(u, int) and u == 0:
                                pe.wait_ge(vT_set, 1)
                            if isinstance(u, int) and u >= 2:
                                pe.wait_ge(onorm_set, u - 1)
                            pe.transpose(ps[0:16, 6, 0:P], nmax[:, (g + 1) % 2, :], ident[:, :]).then_inc(nmT_mm, 1)
                        if j == 1 and t >= 1 and now.main:
                            if t == 1:
                                if not now.first:
                                    pe.wait_ge(o_read, u)
                                pe.wait_ge(vaug_set, b + 1)
                            output(u, g, t - 1)
                    if t == 0:
                        if now.proj:
                            if not (isinstance(w, int) and w < 1):
                                pe.wait_ge(lo_set, w * 2)
                            if g == 1 and now.main:
                                pe.wait_ge(attn_set, b + 1)
                            project(1, (g + 3) % GROUPS, bw)
                        if g == 0 and now.main:
                            pe.wait_ge(mhi_set, u + 2)
                            pe.wait_ge(mlo_set, u + 2)
                            pe.wait_ge(vT_set, b + 1)
                            for q in range(QT):
                                mm = pe.transpose(ps[:, 6, q * P:(q + 1) * P], vT[:, q * P:(q + 1) * P], ident[:, :])
                            mm.then_inc(vtp_mm, 1)
                    if t == 1 and now.proj:
                        pe.wait_ge(lo_set, w * 2 + 1)
                        project(0, (g + 3) % GROUPS, bw)
                    if t == 1 and now.tail:
                        if g == 0 and now.main:
                            pe.wait_ge(vaug_set, b + 1)
                        elif now.low:
                            pe.wait_ge(mhi_set, u + 2)
                            pe.wait_ge(mlo_set, u + 2)
                        pe.wait_ge(o_read, u)
                        for q in range(QT):
                            mm = pe.transpose(ps[:, 6, q * P:(q + 1) * P], o_sb[:, q * P:(q + 1) * P], ident[:, :])
                        mm.then_inc(oT_mm, 1)
                    if t == 2:
                        if g == 0 and now.tail:
                            pe.wait_ge(onorm_set, u)
                            for q in range(QT):
                                mm = pe.transpose(ps[:, 6, q * P:(q + 1) * P], onorm[:, q, :], ident[:, :])
                            mm.then_inc(onT_mm, 1)
                        if g == 3 and now.proj:
                            if now.tail:
                                pe.wait_ge(onorm_set, u)
                            elif now.low:
                                pe.wait_ge(mhi_set, u + 2)
                                pe.wait_ge(mlo_set, u + 2)
                            split3(pe, ps[:, 6, :], wv_hi[:, :], wv_lo[:, :], seq_of(xT_hi, b + 1),
                                   seq_of(xT_lo, b + 1)).then_inc(vT_mm, 1)
                    if t == 3:
                        if g == 0 and now.tail:
                            if now.proj:
                                pe.wait_ge(lo_set, (w + 1) * 2)
                            pe.wait_ge(onT_set, b)
                            for q in range(QT):
                                mm = pe.matmul(ps[:, 7, q * P:(q + 1) * P], onT[:, q * P:(q + 1) * P], wproj[:, :],
                                               start=True, stop=True)
                            mm.then_inc(out_mm, 1)

            def project(which, g, bw):
                split3(pe, ps[:, 7, :], ws_hi[:, which, g, :], ws_lo[:, which, g, :],
                       seq_of(xT_hi, bw), seq_of(xT_lo, bw)).then_inc(proj_mm, 1)

            def output(u, g, t):
                pe.wait_ge(exp_set, u * 16 + (4 * t + 4))
                for j in range(4):
                    mm = pe.matmul(ps[32 * j:32 * j + 32, 5, :], vaug[:, t, 4 * g + j, :],
                                   probs[:, t % 2, j, :], start=(t == 0), stop=(t == 3))
                mm.then_inc(pv_mm, 1)

            def experts(L):
                F = (F0, F1)[L]
                nch = len(CH[L])
                last = nch - 1

                def turn(i, r, k):
                    pe.wait_ge(xg_in[L][r], (k + 1) * 16)
                    if not (isinstance(i, int) and i == 0):
                        pe.wait_ge(ghi_set[L], i)
                        pe.wait_ge(glo_set[L], i)
                    for q in range(4):
                        mm = pe.transpose(ps[:, 0, q * P:(q + 1) * P], xg[:, r, q, :], ident[:, :])
                    mm.then_inc(gT_mm[L], 1)

                def up(i, r, f, fresh=False):
                    n, par = i * nch + f, (r * nch + f) % 2
                    at, M = CH[L][f]
                    if f == 0:
                        pe.wait_ge(ghi_set[L], i + 1)
                        pe.wait_ge(glo_set[L], i + 1)
                        pe.wait_ge(w_lo_set[L], i + 1)
                    for bank, col, done, free in ((1, 0, gate_mm, act_set), (2, F, up_mm, (h_set, act_set)[L])):
                        if not fresh:
                            pe.wait_ge(free[L], n - 1)
                        c = slice(col + at, col + at + M)
                        split3(pe, ps[0:M, bank + 2 * par, :], wu_hi[:, r, c], wu_lo[:, r, c],
                               gT_hi[:, r, :], gT_lo[:, r, :]).then_inc(done[L], 1)

                def down(i, r, f, k, fresh=False):
                    n, par = i * nch + f, (r * nch + f) % 2
                    M = CH[L][f][1]
                    pe.wait_ge(h_set[L], n + 1)
                    if f == 0:
                        pe.wait_ge(dn_in[L][r], (k + 1) * 16 * NDN[L])
                        if not fresh:
                            pe.wait_ge(y_read[L], i - 1)
                    for q in range(4):
                        mm = pe.matmul(ps[:, 5 + r, q * P:(q + 1) * P], hT[0:M, par, q * P:(q + 1) * P],
                                       wdn[0:M, r, f, :], start=(f == 0 and q == 0), stop=(f == last and q == 3),
                                       skip_group_check=True)
                    mm.then_inc(down_mm[L], 1)

                def tile(i, r, k, fresh=False, more=True):
                    for f in range(nch):
                        if f < last:
                            up(i, r, f + 1, fresh=fresh and r == 0 and f + 1 < 2)
                        elif more:
                            up(i + 1, 1 - r, 0)
                        if f == 0 and more:
                            turn(i + 1, 1 - r, k + r)
                        down(i, r, f, k, fresh=fresh)

                turn(0, 0, 0)
                up(0, 0, 0, fresh=True)
                tile(0, 0, 0, fresh=True)
                tile(1, 1, 0, fresh=True)
                with pe.Fori(1, TILES // 2 - 1) as k:
                    for r in range(2):
                        tile(k * 2 + r, r, k)
                k = TILES // 2 - 1
                tile(k * 2, 0, k)
                tile(k * 2 + 1, 1, k, more=False)

            def chunk(m, s, k, now):
                if now(-2):
                    pe.wait_ge(y1T_set, m - 1)
                    pe.matmul(ps[:, 7, 0:P], y1T[:, s % 2, :], wcomb[:, :], start=True, stop=True
                              ).then_inc(out1_mm, 1)
                if now(3):
                    r = (s + 3) % 4
                    pe.wait_ge(xs_in[r], (k * 2 + ((s + 3) // 4 + 1)) * 32)
                    if now(1):
                        pe.wait_ge(qkv_set, m + 2)
                    w = [v[:, :, :].rearrange("p n d -> p (n d)") for v in (w3_hi, w3_lo)]
                    bank = ps[:, 4 + (s + 3) % 2, 0:3 * D]
                    pe.matmul(bank, xs[:, r, 0, :], w[0], start=True, stop=False)
                    pe.matmul(bank, xs[:, r, 0, :], w[1], start=False, stop=False)
                    pe.matmul(bank, xs[:, r, 1, :], w[0], start=False, stop=True).then_inc(qkv_mm, 1)

                def sums(at, mask, start, stop):
                    for n in range(2):
                        for half_kv in (kv_hi, kv_lo):
                            mm = pe.matmul(ps[:, 2 * (at % 2) + n, :], mask[:, :],
                                           half_kv[:, at % 4, n * 512:(n + 1) * 512],
                                           start=start and half_kv is kv_hi, stop=stop and half_kv is kv_lo,
                                           skip_group_check=True)
                    return mm

                if now(0):
                    pe.wait_ge(kv_lo_set, m + 1)
                    if now(-2):
                        pe.wait_ge(weigh_set, m - 1)
                    sums(s, tri, s % 8 < 2, s % 8 >= 6).then_inc(sum_mm, 1)
                if now(-1):
                    pe.wait_ge(weigh_set, m)
                    if (s - 1) % 8 < 6:
                        sums(s - 1, cotri, False, False)
                    pe.wait_ge(y1_set, m)
                    if now(-2):
                        pe.wait_ge(y1T_set, m - 1)
                    pe.transpose(ps[:, 6, 0:P], y1[:, (s - 1) % 2, :], ident[:, :]).then_inc(y1T_mm, 1)

            norm(0)
            routing(0)
            pe.wait_ge(setup_done, 1)
            pe.wait_ge(pos_set[0], 2)
            pe.wait_ge(w_stack_set, 1)
            steps(pe, attend)
            pe.wait_ge(attn_set, SEQS + 1)
            experts(0)
            pe.wait_ge(y_read[0], TILES)
            norm(1)
            routing(1)
            pe.wait_ge(pos_set[1], 2)
            chunk_steps(pe, chunk)
            pe.wait_ge(attn1_set, TOK_TILES)
            experts(1)

        @block.scalar
        def _(act):
            ident_f, copy_f = ACT.Identity, ACT.Copy

            def norm(L):
                for b in range(SEQS):
                    act.wait_ge(tp_done[L], b + 1)
                    act.activation(xT_hi[:, b, :], ps[:, b % 2, :], copy_f).then_inc(xhi_set[L], 1)
                act.wait_ge(z_set[L], 1)
                act.activation(elog[:, :, :], logits[:, :, :], ACT.Exp).then_inc(e_set[L], 1)

            def attend(u, g, b, now):
                g3 = (g + 3) % GROUPS
                w = u + 3
                for t in range(4):
                    for j in range(4):
                        i = t * 4 + j
                        if now.main:
                            if j == 0 and not (now.first and t < 2):
                                act.wait_ge(pv_mm, u * 4 + (t - 1))
                            act.wait_ge(st_mm, u * 16 + (i + 1))
                            act.activation(probs[:, t % 2, j, :], ps[:, 2 + i % 3, :], ACT.Exp,
                                           scale=SCALE).then_inc(exp_set, 1)
                        if (t, j) == (0, 2) and now.low:
                            act.wait_ge(nmT_mm, u + 2)
                            if not (isinstance(u, int) and u + 1 < 2):
                                act.wait_ge(m_in, u * 32)
                            act.activation(m_hi[:, (g + 1) % 2, :], ps[0:16, 6, 0:P], copy_f).then_inc(mhi_set, 1)
                        if (t, j) in ((1, 0), (2, 0)) and now.proj:
                            which = 2 - t
                            act.wait_ge(proj_mm, w * 2 + t)
                            if not (isinstance(w, int) and w < 1):
                                act.wait_ge(stack_set, w * 2 + (t - 2))
                            bias = (BQ, BK)[which] + g3
                            act.activation(Hi[:, which, :], ps[:, 7, :], ident_f,
                                           bias=cols[:, bias:bias + 1]).then_inc(hi_set, 1)
                            act.activation(Lo[:, which, :], ps[:, 7, :], ident_f,
                                           bias=lobias[:, which, g3:g3 + 1],
                                           scale=cols[:, LOQ + which:LOQ + which + 1]).then_inc(lo_set, 1)
                        if (t, j) == (3, 0) and g == 3 and now.proj:
                            act.wait_ge(vT_mm, b + 2)
                            act.activation(vT, ps[:, 6, :], ident_f, bias=cols[:, BV:BV + 1]).then_inc(vT_set, 1)
                        if (t, j) == (3, 0) and g == 0 and now.tail:
                            act.wait_ge(onT_mm, b)
                            act.activation(onT, ps[:, 6, :], copy_f).then_inc(onT_set, 1)

            def experts(L):
                nch = len(CH[L])

                def high_rows(i, r):
                    act.wait_ge(gT_mm[L], i + 1)
                    act.activation(gT_hi[:, r, :], ps[:, 0, :], copy_f).then_inc(ghi_set[L], 1)

                def write_y(i, r, k):
                    act.wait_ge(down_mm[L], (i + 1) * nch)
                    act.wait_ge(y_stored[L][r], (k + 1) * 16)
                    act.activation(ysb[:, r, :, :].rearrange("p q d -> p (q d)"), ps[:, 5 + r, :], copy_f
                                   ).then_inc(y_read[L], 1)

                def store(i, r):
                    if L == 0:
                        act.wait_ge(y_read[L], i + 1)
                    else:
                        act.wait_ge(y_set[L], i + 1)
                    act.dma_start(slots_y[bass.ds(i * TILE, TILE), :].rearrange("(p k) d -> p (k d)", p=P),
                                  ysb[:, r, :, :].rearrange("p q d -> p (q d)")).then_inc(y_stored[L][r], 16)

                def tile(i, r, k, first=False, last=False):
                    for f in range(nch):
                        n, par, M = i * nch + f, (r * nch + f) % 2, CH[L][f][1]
                        if L == 1 and f == 0:
                            act.wait_ge(dn_in[L][r], (k + 1) * 16 * NDN[L])
                        if not (first and r == 0 and f < 2):
                            act.wait_ge(h_set[L], n - 1)
                        act.wait_ge(gate_mm[L], n + 1)
                        if L == 0:
                            act.activation(gact[0:M, par, :], ps[0:M, 1 + 2 * par, :], ACT.Gelu).then_inc(act_set[L], 1)
                        else:
                            act.activation(gact[:, par, :], ps[:, 1 + 2 * par, :], ACT.Gelu,
                                           bias=ebcol[:, r, f:f + 1]).then_inc(gelu_set, 1)
                            act.wait_ge(up_mm[L], n + 1)
                            act.activation(gsig[:, par, :], ps[:, 2 + 2 * par, :], ACT.Tanh, scale=0.5,
                                           bias=ebcol[:, r, 4 + f:5 + f]).then_inc(act_set[L], 1)
                        if L == 0 and f == 0 and not (first and r == 0):
                            write_y(i - 1, 1 - r, k - 1 + r)
                        if f == 1 and not last:
                            high_rows(i + 1, 1 - r)
                        if f == nch - 1 and not (first and r == 0):
                            store(i - 1, 1 - r)

                for r in range(2):
                    act.sem_inc(y_stored[L][r], 16)
                high_rows(0, 0)
                tile(0, 0, 0, first=True)
                tile(1, 1, 0, first=True)
                with act.Fori(1, TILES // 2 - 1) as k:
                    tile(k * 2, 0, k)
                    tile(k * 2 + 1, 1, k)
                k = TILES // 2 - 1
                tile(k * 2, 0, k)
                tile(k * 2 + 1, 1, k, last=True)
                if L == 0:
                    write_y(TILES - 1, 1, k)
                store(TILES - 1, 1)

            def chunk(m, s, k, now):
                if now(1):
                    act.wait_ge(kv_set, m + 2)
                    act.activation(kv_hi[:, (s + 1) % 4, :], kv[:, (s + 1) % 2, :, :, :].rearrange("p h e d -> p (h e d)"),
                                   copy_f).then_inc(kv_hi_set, 1)
                if now(3):
                    act.wait_ge(qkv_mm, m + 4)
                    if now(-1):
                        act.wait_ge(weigh_set, m)
                    act.activation(qkv[:, (s + 3) % 4, :, :].rearrange("p n d -> p (n d)"),
                                   ps[:, 4 + (s + 3) % 2, 0:3 * D], copy_f).then_inc(qkv_set, 1)
                if now(-2):
                    b, c = chunk_of(s - 2, k)
                    t = b * QT + c
                    act.wait_ge(out1_mm, m - 1)
                    act.activation(attn[:, t, :] if isinstance(t, int) else
                                   attn[:, bass.ds(t, 1), :].rearrange("p a d -> p (a d)"),
                                   ps[:, 7, 0:P], copy_f).then_inc(attn1_set, 1)
                if now(-1):
                    act.wait_ge(y1T_mm, m)
                    act.activation(y1T[:, (s - 1) % 2, :], ps[:, 6, 0:P], copy_f).then_inc(y1T_set, 1)

            def gate(L):
                for b in range(SEQS):
                    r = b % 2
                    act.wait_ge(z_ready[L], b + 1)
                    if b >= 2:
                        act.wait_ge(x_set[L], b - 1)
                    act.activation(sg[:, r, :, :], zg[:, r, :, :], ACT.Silu).then_inc(silu_set[L], 1)

            act.wait_ge(setup_done, 1)
            norm(0)
            act.wait_ge(slots_zero, 48)
            act.wait_ge(w_stack_set, 1)
            steps(act, attend)
            experts(0)
            gate(0)
            norm(1)
            chunk_steps(act, chunk)
            experts(1)
            gate(1)

        @block.vector
        def _(dve):
            links = [0]

            def link(ins):
                ins.then_inc(dve_chain, 1)
                links[0] += 1
                dve.wait_ge(dve_chain, links[0])

            def split(hi, lo, src):
                link(dve.tensor_copy(hi, src))
                link(dve.tensor_tensor(lo, src, hi.bitcast(F32), ALU.subtract))

            def setup():
                dve.memset(zeros, 0.0).then_inc(zero_set, 1)
                link(dve.memset(rows[:, :, :], 0.0))
                link(dve.memset(wstack, 0.0))
                dve.wait_ge(ld_a, 16 * N_A)
                jrow = rows[0:1, :, :].rearrange("a n (j r) -> a n j r", j=4)
                link(dve.memset(jrow[:, LOQ, :, 16:24], 1.0))
                link(dve.memset(jrow[:, LOK, :, 8:16], 1.0))
                for which, at in enumerate((BQ, BK)):
                    src = bqkv_row[0:1, which * D:(which + 1) * D].rearrange("a (g j r) -> a g j r", g=4, j=4)
                    wsrc = wqkv[:, which * D:(which + 1) * D].rearrange("p (h r) -> p h r", r=HD)
                    for n in range(3):
                        link(dve.tensor_copy(jrow[:, at:at + 4, :, 8 * n:8 * n + 8], src))
                        link(dve.tensor_copy(wstack[:, which, :, 8 * n:8 * n + 8], wsrc))
                link(dve.memset(jrow[:, BK:BK + 4, :, 24:26], 1.0))
                dve.tensor_copy(rows[0:1, BV, :], bqkv_row[0:1, 2 * D:3 * D]).then_inc(rows_set, 1)
                split(ws_hi[:, :, :, :].rearrange("p w g m -> p (w g m)"),
                      ws_lo[:, :, :, :].rearrange("p w g m -> p (w g m)"),
                      wstack.rearrange("p w h r -> p (w h r)"))
                split(wv_hi[:, :], wv_lo[:, :], wqkv[:, 2 * D:3 * D])
                dve.wait_ge(pe_setup, 1)
                link(dve.tensor_copy(cols[:, :], ps[:, 7, 0:NROWS]))
                for which in range(2):
                    lo_col = cols[:, LOQ + which:LOQ + which + 1]
                    at = (BQ, BK)[which]
                    link(dve.tensor_scalar(sign[:, which:which + 1], lo_col, -2.0, 1.0, ALU.mult, ALU.add))
                    link(dve.tensor_scalar(lobias[:, which, :], cols[:, at:at + 4], lo_col, None, ALU.mult))
                dve.wait_ge(pe_setup, 2)
                link(dve.tensor_copy(w4T[:, :, :].rearrange("p n m -> p (n m)"), ps[:, 5, :]))
                dve.tensor_copy(ldiagT[:, :], ps[:, 4, 0:P]).then_inc(setup_ev, 1)
                dve.wait_ge(pool_con, 11)
                link(dve.tensor_copy(tri[:, :], causal[:, :]))
                link(dve.tensor_scalar(cotri[:, :], causal[:, :], -1.0, 1.0, ALU.mult, ALU.add))
                split(w3_hi[:, :, :], w3_lo[:, :, :], w4T[:, 0:3, :])
                nb = 4 * EXPERTS
                link(dve.tensor_copy(ebias[:, :, 0:4], ps[:, 3, 0:nb].rearrange("p (e c) -> p e c", e=EXPERTS)))
                link(dve.tensor_scalar(ebias[:, :, 4:8], ps[:, 3, nb:2 * nb].rearrange("p (e c) -> p e c", e=EXPERTS),
                                       0.5, None, ALU.mult))
                dve.wait_ge(pe_setup, 3)
                dve.tensor_copy(bdiag[:, :], ps[:, 4, P:2 * P]).then_inc(setup_ev, 1)
                dve.wait_ge(pe_setup, 4)
                dve.tensor_copy(wcomb[:, :], ps[:, 4, 2 * P:3 * P]).then_inc(setup_done, 1)

            def statistics(t):
                link(dve.bn_stats(stats[:, t, :], xres[:, t, :]))
                return dve.bn_aggr(mv[:, t, :], stats[:, t, :])

            def norm(L):
                if L == 0:
                    dve.wait_ge(ld_x, 16)
                    for t in range(TOK_TILES):
                        link(statistics(t))
                dve.tensor_scalar(veps[:, :], mv[:, :, 1], EPS_LN, None, ALU.add).then_inc(veps_set[L], 1)
                dve.wait_ge(rstd_set[L], 1)
                if L == 1:
                    dve.wait_ge(scattered[0], 16 * CHOICES)

                def low(b):
                    dve.wait_ge(xhi_set[L], b + 1)
                    dve.wait_ge(tp_done[L], b + 1)
                    dve.tensor_tensor(xT_lo[:, b, :], ps[:, b % 2, :], xT_hi[:, b, :].bitcast(F32),
                                      ALU.subtract).then_inc(xlo_set[L], 1)

                for b in range(SEQS):
                    for t in range(b * QT, (b + 1) * QT):
                        ins = dve.tensor_scalar(xn[:, t, :], xres[:, t, :], mv[:, t, 0:1], rstd[:, t:t + 1],
                                                ALU.subtract, ALU.mult)
                    ins.then_inc(xn_set[L], 1)
                    if b >= 1:
                        low(b - 1)
                low(SEQS - 1)

            def routing(L):
                S3 = [P, TOK_TILES, EXPERTS]
                dve.wait_ge(logit_mm[L], SEQS)
                dve.wait_ge(pool_con, 11)
                raw = ps[:, 2, 0:TOK_TILES * EXPERTS].rearrange("p (t e) -> p t e", e=EXPERTS)
                if L == 0:
                    link(dve.tensor_copy(logits[:, :, :], raw))
                else:
                    link(dve.tensor_tensor(logits[:, :, :], raw, spread(br_bc[:, :], 1, S3), ALU.add))
                link(dve.tensor_reduce(lmax[:, :], logits[:, :, :], AX, ALU.max))
                dve.tensor_tensor(logits[:, :, :], logits[:, :, :], spread(lmax[:, :], 2, S3),
                                  ALU.subtract).then_inc(z_set[L], 1)
                dve.wait_ge(e_set[L], 1)
                link(dve.tensor_reduce(esum[:, :], elog[:, :, :], AX, ALU.add))
                for k in range(2):
                    link(dve.tensor_reduce(top[:, :, k], elog[:, :, :], AX, ALU.max))
                    link(dve.tensor_tensor(pick[:, :, :], elog[:, :, :], spread(top[:, :, k], 2, S3), ALU.is_ge))
                    link(dve.tensor_tensor(pick[:, :, :], pick[:, :, :], spread(key8[:, :], 1, S3), ALU.mult))
                    link(dve.tensor_reduce(kmax[:, :], pick[:, :, :], AX, ALU.max))
                    link(dve.tensor_tensor(hot[:, :, k, :], pick[:, :, :], spread(kmax[:, :], 2, S3), ALU.is_equal))
                    if k == 0:
                        link(dve.scalar_tensor_tensor(elog[:, :, :], hot[:, :, 0, :], -2.0, elog[:, :, :],
                                                      ALU.mult, ALU.add))
                dve.tensor_copy(hot_b[:, :, :, :], hot[:, :, :, :]).then_inc(hot_set[L], 1)
                if L == 1:
                    link(dve.tensor_tensor(esum[:, :], top[:, :, 0], top[:, :, 1], ALU.add))
                link(dve.reciprocal(esum[:, :], esum[:, :]))
                link(dve.tensor_tensor(wsel[:, :, :], top[:, :, :], spread(esum[:, :], 2, [P, TOK_TILES, 2]), ALU.mult))
                dve.wait_ge(tot_mm[L], 1)
                link(dve.tensor_copy(tot[:, :], ps[0:CHOICES, 3, 0:EXPERTS]))
                C3 = [CHOICES, CHOICES, EXPERTS]
                dve.tensor_tensor(carry[:, :, :], spread(before64[:, :], 2, C3), spread(tot[:, :], 1, C3),
                                  ALU.mult).then_inc(carry_set[L], 1)
                dve.wait_ge(pos_mm[L], 1)
                E3 = [P, EXPERTS, EXPERTS]
                link(dve.tensor_copy(off[:, :], ps[:, 4, 0:EXPERTS]))
                link(dve.tensor_tensor(cmp8[:, :, :], spread(off[:, :], 2, E3), spread(thr[:, :], 1, E3), ALU.is_gt))
                link(dve.tensor_reduce(ntile[:, :], cmp8[:, :, :], AX, ALU.add))
                link(dve.tensor_tensor(cmp8[:, :, :], before8[:, :, :], spread(ntile[:, :], 1, E3), ALU.mult))
                link(dve.tensor_reduce(first[:, :], cmp8[:, :, :], AX, ALU.add))
                link(dve.tensor_scalar(off[:, :], first[:, :], float(TILE), None, ALU.mult))
                W3 = [P, CHOICES, EXPERTS]
                link(dve.tensor_tensor(posw[:, :, :], ps[:, 5, :].rearrange("p (c e) -> p c e", e=EXPERTS),
                                       spread(off[:, :], 1, W3), ALU.add))
                link(dve.tensor_tensor(posw[:, :, :], posw[:, :, :],
                                       hot[:, :, :, :].rearrange("p t k e -> p (t k) e"), ALU.mult))
                link(dve.tensor_reduce(posf[:, :], posw[:, :, :], AX, ALU.add))
                if L == 1:
                    dve.wait_ge(z_ready[0], SEQS)
                dve.tensor_copy(pos[:, :], posf[:, :]).then_inc(pos_set[L], 1)
                N3 = [1, TILES, EXPERTS - 1]
                link(dve.tensor_tensor(ecmp[:, :, :], spread(first[0:1, 1:EXPERTS], 1, N3),
                                       spread(tile_no[:, :], 2, N3), ALU.is_le))
                link(dve.tensor_reduce(eidf[:, :], ecmp[:, :, :], AX, ALU.add))
                dve.tensor_copy(eid[:, :], eidf[:, :]).then_inc(pos_set[L], 1)

            def attend(u, g, b, now):
                g3, g2, gt = (g + 3) % GROUPS, (g + 2) % GROUPS, (g + 3) % GROUPS
                v, w = u + 2, u + 3
                for t in range(4):
                    for j in range(4):
                        i = t * 4 + j
                        if now.max:
                            dve.wait_ge(s_mm, v * 16 + (i + 1))
                            at = j * 4 + t
                            dve.tensor_reduce(nmax[:, g % 2, at:at + 1], ps[:, i % 2, :], AX, ALU.max,
                                              negate=True).then_inc(max_set, 1)
                        if (t, j) == (0, 3) and now.low:
                            dve.wait_ge(mhi_set, u + 2)
                            dve.wait_ge(nmT_mm, u + 2)
                            if not (isinstance(u, int) and u + 1 < 2):
                                dve.wait_ge(m_in, u * 32)
                            r = (g + 1) % 2
                            dve.tensor_tensor(m_lo[:, r, :], ps[0:16, 6, 0:P], m_hi[:, r, :].bitcast(F32),
                                              ALU.subtract).then_inc(mlo_set, 1)
                        if (t, j) == (0, 2) and now.tail:
                            dve.wait_ge(pv_mm, u * 4)
                            dve.tensor_copy(o_sb, ps[:, 5, :]).then_inc(o_read, 1)
                        if (t, j) == (1, 0) and g == 0 and now.main:
                            dve.wait_ge(vtp_mm, b + 1)
                            dve.tensor_copy(vaug[:, :, :, 0:HD],
                                            ps[:, 6, :].rearrange("p (t h r) -> p t h r", t=QT, r=HD)).then_inc(vaug_set, 1)
                        if (t, j) in ((1, 3), (2, 3)) and now.proj:
                            which = 2 - t
                            dst = (Qs[:, g3, :], Ks[:, g3 % 2, :])[which]
                            dve.wait_ge(hi_set, w * 2 + t)
                            dve.wait_ge(lo_set, w * 2 + t)
                            if not (isinstance(u, int) and u < 1):
                                dve.wait_ge(st_mm, u * 16)
                            if which == 1 and not (isinstance(w, int) and w < 2):
                                dve.wait_ge(k_in, w * 64)
                            dve.scalar_tensor_tensor(dst, Hi[:, which, :].bitcast(F32), sign[:, which:which + 1],
                                                     Lo[:, which, :], ALU.mult, ALU.add).then_inc(stack_set, 1)
                        if (t, j) == (2, 1) and now.tail:
                            dve.wait_ge(oT_mm, u)
                            turned = ps[:, 6, :].rearrange("p (q j r) -> p q j r", q=QT, j=4)
                            dve.reciprocal(rden[:, :, :], turned[:, :, :, HD]).then_inc(rden_set, 1)
                            dve.wait_ge(rden_set, u)
                            dve.tensor_tensor(onorm[:, :, 32 * gt:32 * gt + 32].rearrange("p q (j r) -> p q j r", j=4),
                                              turned[:, :, :, 0:HD], spread(rden[:, :, :], 3, [P, QT, 4, HD]),
                                              ALU.mult).then_inc(onorm_set, 1)
                        if (t, j) == (3, 3) and g == 0 and now.tail:
                            dve.wait_ge(out_mm, b)
                            dve.tensor_tensor(rows_of(attn, b - 1), ps[:, 7, :].rearrange("p (q d) -> p q d", q=QT),
                                              spread(bproj_bc[:, :], 1, [P, QT, D]), ALU.add).then_inc(attn_set, 1)

            def experts(L):
                NW = 2 * (F0, F1)[L]
                nch = len(CH[L])

                def high_weights(i, r, k):
                    dve.wait_ge(up_in[L][r], (k + 1) * 32)
                    dve.tensor_copy(wu_hi[:, r, 0:NW], wraw[:, r, 0:NW]).then_inc(w_hi_set[L], 1)

                def low_rows(i, r):
                    dve.wait_ge(gT_mm[L], i + 1)
                    dve.wait_ge(ghi_set[L], i + 1)
                    dve.tensor_tensor(gT_lo[:, r, :], ps[:, 0, :], gT_hi[:, r, :].bitcast(F32),
                                      ALU.subtract).then_inc(glo_set[L], 1)

                def finish(i, r):
                    dve.wait_ge(down_mm[L], (i + 1) * nch)
                    dve.wait_ge(xb_set, i + 1)
                    y = ysb[:, r, :, :]
                    dve.scalar_tensor_tensor(y.rearrange("p q d -> p (q d)"), ps[:, 5 + r, :], 0.5,
                                             y.rearrange("p q d -> p (q d)"), ALU.mult, ALU.add
                                             ).then_inc(y_read[L], 1)
                    dve.wait_ge(y_read[L], i + 1)
                    for q in range(4):
                        dve.bn_stats(estats[:, q, :], ysb[:, r, q, :]).then_inc(est_chain, 1)
                    even, odd = estats[:, :, 0:3], estats[:, :, 3:6]
                    dve.wait_ge(est_chain, i * 10 + 4)
                    dve.tensor_tensor(eagg[:, 0, :], even[:, :, 1], odd[:, :, 1], ALU.add).then_inc(est_chain, 1)
                    dve.tensor_tensor(eagg[:, 1, :], even[:, :, 1], odd[:, :, 1], ALU.subtract).then_inc(est_chain, 1)
                    dve.tensor_tensor(eagg[:, 2, :], even[:, :, 2], odd[:, :, 2], ALU.add).then_inc(est_chain, 1)
                    dve.wait_ge(est_chain, i * 10 + 7)
                    dve.tensor_scalar(emean[:, :], eagg[:, 0, :], 0.5, None, ALU.mult).then_inc(est_chain, 1)
                    dve.tensor_tensor(eagg[:, 3, :], eagg[:, 1, :], eagg[:, 1, :], ALU.mult).then_inc(est_chain, 1)
                    dve.tensor_scalar(eagg[:, 4, :], eagg[:, 2, :], 1.0 / D, EPS_EXPERT, ALU.mult, ALU.add
                                      ).then_inc(est_chain, 1)
                    dve.wait_ge(est_chain, i * 10 + 10)
                    dve.scalar_tensor_tensor(everstd[:, r, :], eagg[:, 3, :], 0.25, eagg[:, 4, :],
                                             ALU.mult, ALU.add).then_inc(evar_set, 1)

                def normalize(i, r):
                    dve.wait_ge(erstd_set, i + 1)
                    for q in range(4):
                        ins = dve.tensor_scalar(ysb[:, r, q, :], ysb[:, r, q, :], emean[:, q:q + 1],
                                                everstd[:, r, q:q + 1], ALU.subtract, ALU.mult)
                    ins.then_inc(xhat_set, 1)

                def tile(i, r, k, first=False, last=False):
                    for f in range(nch):
                        n, par, M = i * nch + f, (r * nch + f) % 2, CH[L][f][1]
                        dve.wait_ge(act_set[L], n + 1)
                        if not (first and r == 0 and f < 2):
                            dve.wait_ge(down_mm[L], n - 1)
                        if L == 0:
                            dve.wait_ge(up_mm[L], n + 1)
                            dve.tensor_tensor(hT[0:M, par, :], ps[0:M, 2 + 2 * par, :], gact[0:M, par, :],
                                              ALU.mult).then_inc(h_set[L], 1)
                        else:
                            dve.scalar_tensor_tensor(hT[:, par, :], gsig[:, par, :], 1.0, gact[:, par, :],
                                                     ALU.add, ALU.mult).then_inc(h_set[L], 1)
                        if f == 0 and not last:
                            high_weights(i + 1, 1 - r, k + r)
                        if f == 1 and not last:
                            low_rows(i + 1, 1 - r)
                        if L == 1 and f == 1 and not (first and r == 0):
                            finish(i - 1, 1 - r)
                        if L == 1 and f == 2 and not (first and r == 0):
                            normalize(i - 1, 1 - r)

                high_weights(0, 0, 0)
                low_rows(0, 0)
                tile(0, 0, 0, first=True)
                tile(1, 1, 0, first=True)
                with dve.Fori(1, TILES // 2 - 1) as k:
                    tile(k * 2, 0, k)
                    tile(k * 2 + 1, 1, k)
                k = TILES // 2 - 1
                tile(k * 2, 0, k)
                tile(k * 2 + 1, 1, k, last=True)
                if L == 1:
                    finish(TILES - 1, 1)
                    normalize(TILES - 1, 1)

            def chunk(m, s, k, now):
                if now(1):
                    r = (s + 1) % 4
                    dve.wait_ge(kv_hi_set, m + 2)
                    dve.tensor_tensor(kv_lo[:, r, :], kv[:, r % 2, :, :, :].rearrange("p h e d -> p (h e d)"),
                                      kv_hi[:, r, :].bitcast(F32), ALU.subtract).then_inc(kv_lo_set, 1)
                if now(0):
                    dve.wait_ge(sum_mm, m + 1)
                    if now(-1):
                        dve.wait_ge(y1_set, m)
                    bank = 2 * (s % 2)
                    sums = ps[:, bank:bank + 2, :].rearrange("p n (h e d) -> p (n h) e d", e=HD, d=HD)
                    q = qkv[:, s % 4, 0, :].rearrange("p (h d) -> p h d", d=HD)
                    dve.tensor_tensor(qkv_sum, sums, spread(q, 2, [P, HEADS, HD, HD]), ALU.mult
                                      ).then_inc(weigh_set, 1)
                    dve.wait_ge(weigh_set, m + 1)
                    if now(-2):
                        dve.wait_ge(y1T_mm, m - 1)
                    dve.tensor_reduce(y1[:, s % 2, :].rearrange("p (h e) -> p h e", e=HD), qkv_sum, AX, ALU.add
                                      ).then_inc(y1_set, 1)

            def combine(L):
                if L == 0:
                    dve.wait_ge(ld_x_again, 16)
                def weigh(b):
                    r = b % 2
                    dve.wait_ge(gathered[L][r], 16 * 2 * QT * (b // 2 + 1))
                    if b >= 2:
                        dve.wait_ge(silu_set[L], b - 1)
                    for q in range(QT):
                        ins = dve.tensor_scalar(zg[:, r, q, :], yg[:, r, 2 * q, :],
                                                wsel[:, b * QT + q, 0:1], None, ALU.mult)
                    link(ins)
                    for q in range(QT):
                        ins = dve.scalar_tensor_tensor(zg[:, r, q, :], yg[:, r, 2 * q + 1, :],
                                                       wsel[:, b * QT + q, 1:2], zg[:, r, q, :], ALU.mult, ALU.add)
                    if L == 0:
                        link(ins)
                        ins = dve.tensor_tensor(zg[:, r, :, :], zg[:, r, :, :],
                                                spread(fbias_bc[:, :], 1, [P, QT, D]), ALU.add)
                    ins.then_inc(z_ready[L], 1)

                def add(b):
                    r = b % 2
                    dve.wait_ge(silu_set[L], b + 1)
                    link(dve.tensor_tensor(sg[:, r, :, :], sg[:, r, :, :], rows_of(attn, b), ALU.mult))
                    ins = dve.tensor_tensor(rows_of(xres, b), rows_of(xres, b), sg[:, r, :, :], ALU.add)
                    ins.then_inc(x_set[L], 1)
                    dve.wait_ge(x_set[L], b + 1)
                    if L == 0:
                        for t in range(b * QT, (b + 1) * QT):
                            link(statistics(t))

                for b in range(SEQS):
                    weigh(b)
                    if b >= 1:
                        add(b - 1)
                add(SEQS - 1)

            setup()
            norm(0)
            routing(0)
            dve.wait_ge(slots_zero, 48)
            link(dve.memset(vaug, 0.0))
            link(dve.memset(zero_col[:, :], 0.0))
            for g in range(GROUPS):
                ins = dve.tensor_copy(Km[g], spread(zero_col[:, :], 2, [P, 4, SEQ]))
            ins.then_inc(km_zero, 1)
            link(dve.memset(vaug[:, :, :, HD:HD + 1], 1.0))
            dve.sem_inc(attn_set, 1)
            dve.sem_inc(w_stack_set, 1)
            steps(dve, attend)
            experts(0)
            combine(0)
            norm(1)
            routing(1)
            chunk_steps(dve, chunk)
            experts(1)
            combine(1)


_INS = ['L0_attn_x', 'L0_attn_w_qkv', 'L0_attn_b_qkv', 'L0_attn_w_proj', 'L0_attn_b_proj', 'L0_ffn_router_w',
        'L0_ffn_w1', 'L0_ffn_v1', 'L0_ffn_w2', 'L0_ffn_bias', 'L1_attn_Wq', 'L1_attn_Wk', 'L1_attn_Wv',
        'L1_attn_Wc', 'L1_attn_Ltri', 'L1_ffn_Wr', 'L1_ffn_br', 'L1_ffn_Wi', 'L1_ffn_bi', 'L1_ffn_Wg',
        'L1_ffn_bg', 'L1_ffn_Wo', 'L1_ffn_bo', 'L1_ffn_gamma', 'L1_ffn_beta']


def kernel(**inputs):
    import numpy as np
    import concourse.bacc as bacc
    from concourse.bass_utils import run_bass_kernel_spmd

    nc = bacc.Bacc("TRN2", target_bir_lowering=False, num_devices=1)
    arrays, args = {}, []
    for name in _INS:
        a = np.ascontiguousarray(inputs[name])
        arrays[f"in_{name}"] = a
        args.append(nc.dram_tensor(f"in_{name}", a.shape, mybir.dt.from_np(a.dtype), kind="ExternalInput").ap())
    shape = inputs['L0_attn_x'].shape
    args.append(nc.dram_tensor("out_x", shape, F32, kind="ExternalOutput").ap())
    build(nc, *args)
    r = run_bass_kernel_spmd(nc, [arrays], core_ids=[0])
    return r.results[0]["out_x"]
```

```python
from contextlib import ExitStack

import concourse.bass as bass
from concourse import mybir

F32 = mybir.dt.float32
F32R = mybir.dt.float32r
BF16 = mybir.dt.bfloat16
I32 = mybir.dt.int32
U32 = mybir.dt.uint32
ALU = mybir.AluOpType
ACT = mybir.ActivationFunctionType
AX = mybir.AxisListType.X

P = 128
EXPERTS = 8
SEQS = 8
SEQ = 512
QT = SEQ // P
TOK_TILES = SEQS * QT
HEADS = 16
HD = 8
GROUPS = 4
TILE = 512
TILES = 23
CHOICES = 2 * TOK_TILES
EPS_LN = 1e-5
EPS_EXPERT = 1e-12


def build(nc, x, w_qkv, b_qkv, w_proj, b_proj, router_w, w1, v1, w2, ffn_bias,
          Wq, Wk, Wv, Wc, Ltri, Wr, br, Wi, bi, Wg, bg, Wo, bo, gamma, beta, out):
    D = x.shape[2]
    F0 = w1.shape[2]
    F1 = Wi.shape[2]
    SCALE = float(HD) ** -0.5
    CH = [[(0, 128), (128, 128), (256, F0 - 256)], [(c * 128, 128) for c in range(F1 // 128)]]
    DX = D + 1
    slots_x = [nc.dram_tensor(f"slots_x{L}", [TILES * TILE, DX], F32, kind="Internal").ap() for L in range(2)]
    TOKENS, TOKEN_ROW = SEQS * SEQ, TILES * TILE
    token_y = nc.dram_tensor("token_y", [TOKEN_ROW + 2 * TOKENS, D], F32, kind="Internal").ap()
    q_halves = nc.dram_tensor("q_halves", [SEQS, HEADS, 32, SEQ], F32, kind="Internal").ap()
    k_halves = nc.dram_tensor("k_halves", [SEQS, HEADS, 32, SEQ], F32, kind="Internal").ap()

    ctx = ExitStack()
    with ctx:
        def sb(name, shape, dt=F32):
            return ctx.enter_context(nc.sbuf_tensor(name, shape, dt))

        def sem(name):
            return ctx.enter_context(nc.semaphore(name))

        ps = ctx.enter_context(nc.psum_tensor("ps", [P, 8, 512], F32))

        with nc.sbuf_tensor("Km01", [P, 2, 4, SEQ], F32R) as Km01:
            pass
        xres = sb("xres", [P, TOK_TILES, D])
        xn = sb("xn", [P, TOK_TILES, DX])
        attn = sb("attn", [P, TOK_TILES, D])
        xT_hi = sb("xT_hi", [P, SEQS, SEQ], F32R)
        xT_lo = sb("xT_lo", [P, SEQS, SEQ], F32R)

        ident = sb("ident", [P, P])
        before = sb("before", [P, P], BF16)
        ones_b = sb("ones_b", [P, 1], BF16)
        before64 = sb("before64", [CHOICES, CHOICES])
        ones64 = sb("ones64", [CHOICES, P])
        causal = sb("causal", [P, P])
        tri = sb("tri", [P, P], F32R)
        cotri = sb("cotri", [P, P], F32R)
        key8 = sb("key8", [P, EXPERTS])
        thr = sb("thr", [P, EXPERTS])
        before8 = sb("before8", [P, EXPERTS, EXPERTS])
        tile_no = sb("tile_no", [1, TILES])
        half = sb("half", [P, TOK_TILES])
        one_row = sb("one_row", [1, P])
        cols = sb("cols", [P, 3])
        kmask = sb("kmask", [P, 4])
        bproj_bc = sb("bproj_bc", [P, D])
        fbias_bc = sb("fbias_bc", [P, D])
        br_bc = sb("br_bc", [P, EXPERTS])
        bqkv_row = sb("bqkv_row", [1, 3 * D])

        wqkv = sb("wqkv", [P, 3 * D])
        wq_hi = sb("wq_hi", [P, 3, D], F32R)
        wq_lo = sb("wq_lo", [P, 3, D], F32R)
        wproj = sb("wproj", [P, D])
        wrout = sb("wrout", [P, 2, EXPERTS])
        wr = sb("wr", [P, 2, 2, EXPERTS], F32R)
        w4 = sb("w4", [P, 4, D])
        w4T = sb("w4T", [P, 4, D])
        w3_hi = sb("w3_hi", [P, 3, D], F32R)
        w3_lo = sb("w3_lo", [P, 3, D], F32R)
        ltri = sb("ltri", [P, HD])
        ldiag = sb("ldiag", [P, HEADS, HD])
        ldiagT = sb("ldiagT", [P, P])
        bdiag = sb("bdiag", [P, P])
        wcomb = sb("wcomb", [P, D])
        ebias_rows = sb("ebias_rows", [2 * 4 * EXPERTS, P])
        ebias = sb("ebias", [P, EXPERTS, 8])

        stats = sb("stats", [P, TOK_TILES, 6])
        mv = sb("mv", [P, TOK_TILES, 2])
        veps = sb("veps", [P, TOK_TILES])
        rstd = sb("rstd", [P, TOK_TILES])
        logits = sb("logits", [P, TOK_TILES, EXPERTS])
        elog = sb("elog", [P, TOK_TILES, EXPERTS])
        esum = sb("esum", [P, TOK_TILES])
        top = sb("top", [P, TOK_TILES, 2])
        pick = sb("pick", [P, TOK_TILES, EXPERTS])
        kmax = sb("kmax", [P, TOK_TILES])
        lmax = sb("lmax", [P, TOK_TILES])
        hot = sb("hot", [P, TOK_TILES, 2, EXPERTS])
        hot_b = sb("hot_b", [P, TOK_TILES, 2, EXPERTS], BF16)
        wsel = sb("wsel", [P, TOK_TILES, 2])
        tot = sb("tot", [CHOICES, EXPERTS])
        carry = sb("carry", [CHOICES, CHOICES, EXPERTS])
        cmp8 = sb("cmp8", [P, EXPERTS, EXPERTS])
        ntile = sb("ntile", [P, EXPERTS])
        first = sb("first", [P, EXPERTS])
        off = sb("off", [P, EXPERTS])
        posw = sb("posw", [P, CHOICES, EXPERTS])
        posf = sb("posf", [P, CHOICES])
        pos = sb("pos", [P, CHOICES], U32)
        ecmp = sb("ecmp", [1, TILES, EXPERTS - 1])
        eidf = sb("eidf", [1, TILES])
        eid = sb("eid", [1, TILES], I32)

        rden = sb("rden", [P, QT, 4])
        nmax = sb("nmax", [P, 2, 16])
        m_hi = sb("m_hi", [16, 2, P], F32R)
        m_lo = sb("m_lo", [16, 2, P], F32R)
        ids = sb("ids", [P, TILES, 4], U32)
        ids_now = sb("ids_now", [P, 2, 4], U32)
        ebcol = sb("ebcol", [P, 2, 8])
        estats = sb("estats", [P, 4, 6])
        eagg = sb("eagg", [P, 5, 4])
        emean = sb("emean", [P, 4])
        everstd = sb("everstd", [P, 2, 4])

        def stage():
            space = ExitStack()
            count = [0]

            def take(*shape, dt=F32):
                count[0] += 1
                return space.enter_context(nc.sbuf_tensor(f"stage{len(stages)}_{count[0]}", [P, *shape], dt)
                                           )[tuple([slice(None)] * (1 + len(shape)))]
            stages.append(space)
            return take, lambda *shape: take(*shape, dt=F32R)

        stages = []
        take, take_r = stage()
        NZ = TILES * TILE // P
        zeros = take(NZ, DX)
        stages[-1].close()
        take, take_r = stage()
        Km23 = take_r(2, 4, SEQ)
        Km = [Km01[:, 0, :, :], Km01[:, 1, :, :], Km23[:, 0, :, :], Km23[:, 1, :, :]]
        probs = take(2, 4, SEQ)
        vaug = take(QT, HEADS, 32)
        vT = take(SEQ)
        o_sb = take(SEQ)
        onorm = take(QT, D)
        onT = take(SEQ)
        Qs = take_r(GROUPS, SEQ)
        Hi = take_r(2, SEQ)
        Lo = take_r(2, SEQ)
        stages[-1].close()
        take, take_r = stage()
        stages[-1].close()
        take, take_r = stage()
        xs = take_r(4, 2, P)
        qkv = take(4, 3, D)
        kv = take(2, HEADS, HD, HD)
        kv_hi = take_r(4, HEADS * HD * HD)
        kv_lo = take_r(4, HEADS * HD * HD)
        qkv_sum = take(HEADS, HD, HD)
        y1 = take(2, D)
        y1T = take(2, P)
        stages[-1].close()
        take, take_r = stage()
        wu_hi = take_r(2, 2 * F1)
        wu_lo = take_r(2, 2 * F1)
        gT_hi = take_r(2, TILE)
        gT_lo = take_r(2, TILE)
        wraw = take(2, 2 * F1)
        wdn = take(2, 4, D)
        xg = take(2, 4, DX)
        xb = take(2, 4, D)
        gact = take(2, TILE)
        gsig = take(2, TILE)
        hT = take(2, TILE)
        ysb = take(2, 4, D)
        vecs = take(2, 3, D)
        stages[-1].close()
        take, take_r = stage()
        yg = take(4, 2, QT, D)
        zg = take(2, QT, D)
        sg = take(2, QT, D)
        stages[-1].close()

        ld_x = [sem(f"ld_x{n}") for n in range(2)]
        ld_x_again = sem("ld_x_again")
        ld_a = sem("ld_a")
        ld_b = sem("ld_b")
        zero_set = sem("zero_set")
        slots_zero = sem("slots_zero")
        pool_mem = sem("pool_mem")
        pool_con = sem("pool_con")
        dve_chain = sem("dve_chain")
        pe_setup = sem("pe_setup")
        setup_ev = sem("setup_ev")
        setup_done = sem("setup_done")
        two = lambda name: [sem(f"{name}{L}") for L in range(2)]
        veps_set, rstd_set, xn_set = two("veps_set"), two("rstd_set"), two("xn_set")
        tp_done, xhi_set, xlo_set = two("tp_done"), two("xhi_set"), two("xlo_set")
        logit_mm, z_set, e_set = two("logit_mm"), two("z_set"), two("e_set")
        hot_set, tot_mm, carry_set = two("hot_set"), two("tot_mm"), two("carry_set")
        pos_mm, pos_set, scattered = two("pos_mm"), two("pos_set"), two("scattered")
        row_set, ids_set, ids_now_set = sem("row_set"), two("ids_set"), two("ids_now_set")
        up_in = [[sem(f"up_in{L}{r}") for r in range(2)] for L in range(2)]
        xg_in = [[sem(f"xg_in{L}{r}") for r in range(2)] for L in range(2)]
        dn_in = [[sem(f"dn_in{L}{r}") for r in range(2)] for L in range(2)]
        vec_in = [sem(f"vec_in{r}") for r in range(2)]
        w_hi_set, w_lo_set = two("w_hi_set"), two("w_lo_set")
        gT_mm, ghi_set, glo_set = two("gT_mm"), two("ghi_set"), two("glo_set")
        gate_mm, up_mm, act_set = two("gate_mm"), two("up_mm"), two("act_set")
        h_set, down_mm, y_read = two("h_set"), two("down_mm"), two("y_read")
        xb_set, y_set = sem("xb_set"), two("y_set")
        est_chain, evar_set, erstd_set, xhat_set = (
            sem("est_chain"), sem("evar_set"), sem("erstd_set"), sem("xhat_set"))
        rows_go = sem("rows_go")
        y_stored = [[sem(f"y_stored{L}{r}") for r in range(2)] for L in range(2)]
        gelu_set = sem("gelu_set")
        gathered = [sem(f"gathered{n}") for n in range(4)]
        z_ready, silu_set, x_set = two("z_ready"), two("silu_set"), two("x_set")
        z_first, gated_set = two("z_first"), sem("gated_set")
        stored = sem("stored")
        proj_mm, hi_set, lo_set, halves_out = (
            sem("proj_mm"), sem("hi_set"), sem("lo_set"), sem("halves_out"))
        group_in = [sem(f"group_in{r}") for r in range(2)]
        s_mm, max_set, nmT_mm, mhi_set, mlo_set, m_in = (
            sem("s_mm"), sem("max_set"), sem("nmT_mm"), sem("mhi_set"), sem("mlo_set"), sem("m_in"))
        km_set = sem("km_set")
        st_mm, exp_set, pv_mm, o_read, oT_mm, onorm_set = (
            sem("st_mm"), sem("exp_set"), sem("pv_mm"), sem("o_read"), sem("oT_mm"), sem("onorm_set"))
        rden_set = sem("rden_set")
        vT_mm, vT_set, vtp_mm, vaug_set = sem("vT_mm"), sem("vT_set"), sem("vtp_mm"), sem("vaug_set")
        vaug_const = sem("vaug_const")
        onT_mm, onT_set, out_mm, attn_set = sem("onT_mm"), sem("onT_set"), sem("out_mm"), sem("attn_set")
        xs_in = [sem(f"xs_in{n}") for n in range(4)]
        kv_eighth_set = sem("kv_eighth_set")
        qkv_mm, qkv_set, kv_set, kv_hi_set, kv_lo_set = (
            sem("qkv_mm"), sem("qkv_set"), sem("kv_set"), sem("kv_hi_set"), sem("kv_lo_set"))
        sum_mm, weigh_set, y1_set, y1T_mm, y1T_set, out1_mm, attn1_set = (
            sem("sum_mm"), sem("weigh_set"), sem("y1_set"), sem("y1T_mm"), sem("y1T_set"),
            sem("out1_mm"), sem("attn1_set"))

        def spread(ap, axis, shape):
            return ap.unsqueeze(axis).to_broadcast(shape)

        def seq_of(tile, b):
            return tile[:, b, :] if isinstance(b, int) else tile[:, bass.ds(b, 1), :].rearrange("p a n -> p (a n)")

        def rows_of(tile, b):
            return tile[:, b * QT:(b + 1) * QT, :] if isinstance(b, int) else tile[:, bass.ds(b * QT, QT), :]

        def split3(pe, out_ap, w_hi_ap, w_lo_ap, x_hi_ap, x_lo_ap, start=True, stop=True):
            pe.matmul(out_ap, w_hi_ap, x_hi_ap, start=start, stop=False)
            pe.matmul(out_ap, w_hi_ap, x_lo_ap, start=False, stop=False)
            return pe.matmul(out_ap, w_lo_ap, x_hi_ap, start=False, stop=stop)

        def steps(eng, step):
            class Now:
                def __init__(self, u):
                    self.main, self.tail = 0 <= u < 32, 1 <= u <= 32
                    self.max, self.load, self.low = 0 <= u + 2 < 32, 0 <= u + 3 < 32, 0 <= u + 1 < 32
                    self.next = u % GROUPS == 2 and -2 <= u < 24
                    self.halves = u % GROUPS == 3 and -1 <= u < 25
                    self.first = u < 1
            for u in range(-3, 1):
                step(u, u % GROUPS, u // GROUPS, Now(u))
            with eng.Fori(0, SEQS - 2) as b:
                for s in range(1, 5):
                    step(b * 4 + s, s % GROUPS, b + s // GROUPS, Now(s + 4))
            for u in range(25, 33):
                step(u, u % GROUPS, u // GROUPS, Now(u))

        def chunk_steps(eng, step):
            for m in range(-4, 2):
                step(m, m, 0, lambda n, m=m: 0 <= m + n < TOK_TILES)
            with eng.Fori(0, TOK_TILES // 8 - 1) as k:
                for s in range(2, 10):
                    step(k * 8 + s, s, k, lambda n: True)
            for m in range(26, TOK_TILES + 2):
                step(m, m, 0, lambda n, m=m: 0 <= m + n < TOK_TILES)

        def outer_product(eng, s):
            four = [P, HEADS, HD, HD]
            by_head = qkv[:, s % 4, :, :].rearrange("p n (h r) -> p n h r", r=HD)
            return eng.tensor_tensor(kv[:, s % 2, :, :, :], spread(by_head[:, 1, :, :], 2, four),
                                     spread(by_head[:, 2, :, :], 3, four), ALU.mult)

        def chunk_of(s, k):
            return k * 2 + (s // 8 * 2 + s % 2), s % 8 // 2

        def bank_of(i):
            return 1 if i == 15 else i % 3

        def read_before(i):
            return {0: -3, 1: 0, 2: -1, 15: 14}.get(i, i - 2)

        N_A, N_B = 8, 7
        NDN = [2, 2]
        block = ctx.enter_context(nc.Block())

        @block.sync
        def _(sp):
            for n in range(2):
                sp.dma_start(xres[:, 16 * n:16 * n + 16, :],
                             x[4 * n:4 * n + 4, :, :].rearrange("s (t p) d -> p (s t) d", p=P)).then_inc(ld_x[n], 16)
            sp.dma_start(wqkv[:, :], w_qkv).then_inc(ld_a, 16)
            sp.dma_start(bqkv_row[:, :], b_qkv.rearrange("(a n) -> a n", a=1)).then_inc(ld_a, 16)
            sp.dma_start(wproj[:, :], w_proj).then_inc(ld_a, 16)
            sp.dma_start(wrout[:, 0, :], router_w).then_inc(ld_a, 16)
            sp.dma_start(wrout[:, 1, :], Wr).then_inc(ld_a, 16)
            sp.dma_start(bproj_bc[:, :], b_proj.partition_broadcast(P)).then_inc(ld_a, 16)
            sp.dma_start(fbias_bc[:, :], ffn_bias.partition_broadcast(P)).then_inc(ld_a, 16)
            sp.dma_start(br_bc[:, :], br.partition_broadcast(P)).then_inc(ld_a, 16)
            for n, w in enumerate((Wq, Wk, Wv, Wc)):
                sp.dma_start(w4[:, n, :], w).then_inc(ld_b, 16)
            sp.dma_start(ltri[:, :], Ltri.rearrange("h e f -> (h e) f")).then_inc(ld_b, 16)
            nb = 4 * EXPERTS
            sp.dma_start(ebias_rows[0:nb, :], bi.rearrange("e (c p) -> (e c) p", p=P)).then_inc(ld_b, 16)
            sp.dma_start(ebias_rows[nb:2 * nb, :], bg.rearrange("e (c p) -> (e c) p", p=P)).then_inc(ld_b, 16)
            sp.wait_ge(zero_set, 4)
            sp.dma_start(slots_x[0].rearrange("(p a) d -> p a d", p=P), zeros).then_inc(slots_zero, 16)

            sp.dma_start(q_halves[:, :, 24:32, :].rearrange("b h r (m c) -> (b h) (r m) c", c=P),
                         zeros[:, 0:32, 0:P]).then_inc(slots_zero, 16)

            def max_rows(u, r, g):
                sp.wait_ge(mhi_set, u + 1)
                sp.wait_ge(mlo_set, u + 1)
                for row, src in ((24, m_hi), (25, m_lo)):
                    dst = Qs[row:P:32, g, :].bitcast(F32)
                    sp.dma_start(dst, src[:, r, :].bitcast(F32)).then_inc(m_in, 16)

            def store_halves(b):
                for o, dst in enumerate((k_halves, q_halves)):
                    sp.wait_ge(lo_set, b * 2 + (o + 1))
                    for n, half_rows in enumerate(((Hi, Lo, Hi), (Hi, Hi, Lo))[o]):
                        rows = (dst[b, :, 8 * n:8 * n + 8, :] if isinstance(b, int) else
                                dst[bass.ds(b, 1), :, 8 * n:8 * n + 8, :].rearrange("a h r n -> (a h) r n"))
                        sp.dma_start(rows, half_rows[:, 1 - o, :].bitcast(F32)).then_inc(halves_out, 16)

            def load_group(u, g, bw):
                if not (isinstance(u, int) and u < 1):
                    sp.wait_ge(st_mm, u * 16)
                sp.wait_ge(halves_out, bw * 96 + 96)
                g3 = (g + 3) % GROUPS

                def rows_of_heads(src, h0, h1, n):
                    rows = src[bw, h0:h1, 0:n, :] if isinstance(bw, int) else \
                        src[bass.ds(bw, 1), h0:h1, 0:n, :].rearrange("a h r n -> (a h) r n")
                    return rows.rearrange("h r n -> (h r) n")
                for j in range(4):
                    sp.dma_start(Km[g3][32 * j:32 * j + 24, j, :].bitcast(F32),
                                 rows_of_heads(k_halves, 4 * g3 + j, 4 * g3 + j + 1, 24)).then_inc(group_in[g3 % 2], 16)
                sp.dma_start(Qs[:, g3, :].bitcast(F32),
                             rows_of_heads(q_halves, 4 * g3, 4 * g3 + 4, 32)).then_inc(group_in[g3 % 2], 16)

            def attend(u, g, b, now):
                if now.halves:
                    store_halves(b + 2)
                if now.low:
                    max_rows(u + 1, (g + 1) % 2, (g + 1) % GROUPS)
                if now.load:
                    load_group(u, g, b if g == 0 else b + 1)
                if isinstance(u, int) and u < 1:
                    part = TILES * TILE // 8
                    for n in (2 * u + 6, 2 * u + 7):
                        rows = slice(n * part, (n + 1) * part)
                        sp.dma_start(slots_x[1][rows, :], slots_x[0][rows, :]).then_inc(slots_zero, 16)

            store_halves(0)
            sp.wait_ge(slots_zero, 32)
            sp.wait_ge(km_set, GROUPS)
            steps(sp, attend)

            def expert_loads(L):
                nch = len(CH[L])
                F = (F0, F1)[L]
                gate, up, down = ((w1, v1, w2), (Wi, Wg, Wo))[L]

                def expert_of(i):
                    return sp.value_load(eid[0:1, bass.ds(i, 1)], min_val=0, max_val=EXPERTS - 1)

                def load_up(i, r, e=None):
                    e = expert_of(i) if e is None else e
                    for n, w in enumerate((gate, up)):
                        sp.dma_start(wraw[:, r, n * F:(n + 1) * F],
                                     w[bass.ds(e, 1), :, :].rearrange("a p n -> (a p) n")).then_inc(up_in[L][r], 16)

                def load_x(i, r):
                    sp.dma_start(xg[:, r, :, :].rearrange("p k d -> p (k d)"),
                                 slots_x[L][bass.ds(i * TILE, TILE), :].rearrange("(p k) d -> p (k d)", p=P)
                                 ).then_inc(xg_in[L][r], 16)

                def load_down(i, r, e=None):
                    e = expert_of(i) if e is None else e
                    wd = down[bass.ds(e, 1), :, :].rearrange("a f n -> (a f) n")
                    if L == 0:
                        sp.dma_start(wdn[:, r, 0:2, :],
                                     wd[0:2 * P, :].rearrange("(c p) n -> p c n", p=P)).then_inc(dn_in[L][r], 16)
                        sp.dma_start(wdn[0:F - 2 * P, r, 2, :], wd[2 * P:F, :]).then_inc(dn_in[L][r], 16)
                    else:
                        sp.dma_start(wdn[:, r, :, :],
                                     wd.rearrange("(c p) n -> p c n", p=P)).then_inc(dn_in[L][r], 16)
                        sp.dma_start(ebcol[:, r, :],
                                     ebias[:, bass.ds(e, 1), :].rearrange("p a n -> p (a n)")).then_inc(dn_in[L][r], 16)

                def load_vecs(i, r, e=None):
                    e = expert_of(i) if e is None else e
                    for n, w in enumerate((bo, gamma, beta)):
                        sp.dma_start(vecs[:, r, n, :],
                                     w[bass.ds(e, 1), :].to_broadcast([P, D])).then_inc(vec_in[r], 16)

                sp.wait_ge(pos_set[L], 2)
                sp.wait_ge(scattered[L], 16 * CHOICES)
                sp.wait_ge((attn_set, attn1_set)[L], (SEQS + 1, TOK_TILES)[L])
                for i in range(2):
                    load_up(i, i)
                    load_x(i, i)
                    load_down(i, i)
                    if L == 1:
                        load_vecs(i, i)
                sp.wait_ge(w_lo_set[L], 1)
                load_up(2, 0)
                if L == 0:
                    sp.dma_start(xres[:, :, :], x.rearrange("s (t p) d -> p (s t) d", p=P)).then_inc(ld_x_again, 16)

                def refill(i, r, down=True, up=True):
                    e1 = expert_of(i + 1) if down else None
                    e3 = expert_of(i + 3) if up else None
                    if down:
                        sp.wait_ge(down_mm[L], i * nch)
                        load_down(i + 1, 1 - r, e1)
                    if up:
                        sp.wait_ge(w_lo_set[L], i + 2)
                        load_up(i + 3, 1 - r, e3)
                    sp.wait_ge(gT_mm[L], i + 1)
                    sp.wait_ge(ids_set[L], i + 1)
                    if L == 1:
                        sp.wait_ge(xb_set, i + 1)
                    load_x(i + 2, r)
                    if L == 1 and down:
                        sp.wait_ge(y_set[1], i)
                        load_vecs(i + 1, 1 - r, e1)

                refill(0, 0, down=False)
                refill(1, 1)
                with sp.Fori(1, TILES // 2 - 1) as k:
                    refill(k * 2, 0)
                    refill(k * 2 + 1, 1)
                refill(TILES - 3, 0, up=False)
                sp.wait_ge(down_mm[L], (TILES - 2) * nch)
                load_down(TILES - 1, 0)
                if L == 1:
                    sp.wait_ge(y_set[1], TILES - 2)
                    load_vecs(TILES - 1, 0)

            def load_outputs(L):
                for r in range(2):
                    sp.wait_ge(y_stored[L][r], 64 * ((TILES + 1 - r) // 2))
                for b in range(SEQS):
                    if b >= 4:
                        sp.wait_ge(z_ready[L], b - 3)
                    for n in range(2):
                        at = TOKEN_ROW + n * TOKENS + b * SEQ
                        sp.dma_start(yg[:, b % 4, n, :, :],
                                     token_y[at:at + SEQ, :].rearrange("(t p) d -> p t d", p=P)
                                     ).then_inc(gathered[b % 4], 16)

            def store_out(b):
                sp.wait_ge(x_set[1], b + 1)
                sp.dma_start(out[b, :, :].rearrange("(t p) d -> p t d", p=P),
                             xres[:, QT * b:QT * (b + 1), :]).then_inc(stored, 16)

            expert_loads(0)
            load_outputs(0)

            def load_chunk(m, s, k, now):
                if now(4):
                    if now(0):
                        sp.wait_ge(qkv_mm, m + 1)
                    b, c = chunk_of(s + 4, k)
                    for n, src in enumerate((xT_hi, xT_lo)):
                        sp.dma_start(xs[:, s % 4, n, :].bitcast(F32),
                                     seq_of(src, b)[:, c * P:(c + 1) * P].bitcast(F32)).then_inc(xs_in[s % 4], 16)

            sp.wait_ge(pos_set[1], 2)
            sp.wait_ge(xlo_set[1], SEQS)
            chunk_steps(sp, load_chunk)
            expert_loads(1)
            load_outputs(1)
            for b in range(SEQS):
                store_out(b)
            sp.wait_ge(stored, 16 * SEQS)

        @block.gpsimd
        def _(pool):
            def fill(ap, value):
                pool.memset(ap, value).then_inc(pool_mem, 1)

            fill(ident[:, :], 0.0)
            fill(before[:, :], 1.0)
            fill(ones_b[:, :], 1.0)
            fill(before64[:, :], 1.0)
            fill(ones64[:, :], 1.0)
            fill(causal[:, :], 1.0)
            fill(before8[:, :, :], 1.0)
            fill(half[:, :], -0.5)
            fill(one_row[:, :], 1.0)
            fill(kmask[:, :], 1.0)
            pool.wait_ge(pool_mem, 10)

            def keep(ap, pattern, base, mult, op=ALU.is_ge, fill_with=0.0):
                pool.affine_select(out=ap, in_=ap, compare_op=op, fill=fill_with, base=base,
                                   pattern=pattern, channel_multiplier=mult).then_inc(pool_con, 1)

            keep(ident[:, :], [[-1, P]], 0, 1, ALU.not_equal, 1.0)
            keep(before[:, :], [[1, P]], -1, -1)
            keep(before64[:, :], [[1, CHOICES]], -1, -1)
            keep(causal[:, :], [[1, P]], 0, -1)
            keep(before8[:, :, :], [[1, EXPERTS], [-1, EXPERTS]], -1, 0)
            pool.iota(key8[:, :], [[-1, EXPERTS]], base=EXPERTS, channel_multiplier=0,
                      allow_small_or_imprecise_dtypes=True).then_inc(pool_con, 1)
            pool.iota(thr[:, :], [[TILE, EXPERTS]], base=0, channel_multiplier=0,
                      allow_small_or_imprecise_dtypes=True).then_inc(pool_con, 1)
            pool.iota(tile_no[:, :], [[1, TILES]], base=0, channel_multiplier=0,
                      allow_small_or_imprecise_dtypes=True).then_inc(pool_con, 1)
            keep(kmask[:, :], [[-32, 4]], -24, 1)
            for n in (32, 64):
                pool.memset(zeros[:, n:min(n + 32, NZ), :], 0.0).then_inc(zero_set, 1)
            pool.wait_ge(zero_set, 3)
            pool.iota(zeros[:, :, D:DX], [[1, NZ], [0, 1]], base=0, channel_multiplier=NZ,
                      allow_small_or_imprecise_dtypes=True).then_inc(zero_set, 1)

            def diagonal_weights():
                pool.wait_ge(ld_b, 16 * N_B)
                pool.tensor_copy(ldiag[:, :, :], spread(ltri[:, :], 1, [P, HEADS, HD])).then_inc(pool_con, 1)
                pool.wait_ge(pool_con, 10)
                keep(kmask[:, :], [[32, 4]], 25, -1)
                keep(ldiag[:, :, :], [[-HD, HEADS], [-1, HD]], 0, 1)
                pool.wait_ge(pool_con, 12)
                keep(ldiag[:, :, :], [[HD, HEADS], [0, HD]], HD - 1, -1)

            def outer(m):
                if m % 8 == 7:
                    return
                pool.wait_ge(qkv_set, m + 1)
                if m >= 2:
                    pool.wait_ge(kv_lo_set, m - 1)
                outer_product(pool, m).then_inc(kv_set, 1)

            def token_root(L, b):
                t = slice(b * QT, (b + 1) * QT)
                pool.wait_ge(veps_set[L], b + 1)
                pool.tensor_tensor(rstd[:, t], veps[:, t], half[:, t], ALU.pow).then_inc(rstd_set[L], 1)

            def gated(L, b):
                r = b % 2
                pool.wait_ge(silu_set[L], b + 1)
                pool.tensor_tensor(sg[:, r, :, :], sg[:, r, :, :], rows_of(attn, b), ALU.mult).then_inc(gated_set, 1)

            def add(b):
                r = b % 2
                if b == 0:
                    pool.wait_ge(ld_x_again, 16)
                gated(0, b)
                pool.wait_ge(gated_set, b + 1)
                pool.tensor_tensor(rows_of(xres, b), rows_of(xres, b), sg[:, r, :, :], ALU.add).then_inc(x_set[0], 1)

            def norm_and_scatter(L):
                if L == 0:
                    pool.wait_ge(slots_zero, 32)
                    pool.wait_ge(pos_set[0], 2)
                    pool.memset(vaug, 0.0).then_inc(vaug_const, 1)
                    pool.wait_ge(vaug_const, 1)
                    pool.memset(vaug[:, :, :, HD:HD + 1], 1.0).then_inc(vaug_const, 1)
                    pool.wait_ge(slots_zero, 32 + 8 * 16)
                else:
                    for m in (0, 1):
                        outer(m)
                for n in range(2):
                    if n == 1:
                        pool.wait_ge(scattered[L], 16 * TOK_TILES)
                    pool.wait_ge(xn_set[L], SEQS)
                    pool.iota(xn[:, :, D:DX], [[P, TOK_TILES], [0, 1]], base=TOKEN_ROW + n * TOKENS, channel_multiplier=1,
                              allow_small_or_imprecise_dtypes=True).then_inc(row_set, 1)
                    pool.wait_ge(row_set, 2 * L + n + 1)
                    pool.wait_ge(pos_set[L], 1)
                    for t in range(TOK_TILES):
                        c = 2 * t + n
                        m = (n * TOK_TILES + t) // 2 + 2
                        if L == 1 and t % 2 == 0 and m < TOK_TILES:
                            outer(m)
                        pool.indirect_dma_start(
                            out=slots_x[L], out_offset=bass.IndirectOffsetOnAxis(ap=pos[:, c:c + 1], axis=0),
                            in_=xn[:, t, :], in_offset=None).then_inc(scattered[L], 16)

            def experts(L):
                NW = 2 * (F0, F1)[L]
                nch = len(CH[L])

                def low_weights(i, r):
                    pool.wait_ge(w_hi_set[L], i + 1)
                    pool.tensor_tensor(wu_lo[:, r, 0:NW], wraw[:, r, 0:NW],
                                       wu_hi[:, r, 0:NW].bitcast(F32), ALU.subtract).then_inc(w_lo_set[L], 1)

                def add_bias(i, r, k):
                    pool.wait_ge(vec_in[r], (k + 1) * 48)
                    pool.wait_ge(xg_in[L][r], (k + 1) * 16)
                    if not (isinstance(i, int) and i < 2):
                        pool.wait_ge(y_read[L], i - 1)
                    pool.tensor_tensor(xb[:, r, :, :], xg[:, r, :, 0:D],
                                       spread(vecs[:, r, 0, :], 1, [P, 4, D]), ALU.add).then_inc(xb_set, 1)

                def root(i, r):
                    pool.wait_ge(evar_set, i + 1)
                    pool.tensor_tensor(everstd[:, r, :], everstd[:, r, :], half[:, 0:4], ALU.pow
                                       ).then_inc(erstd_set, 1)

                def rows_of_tile(i, r):
                    pool.wait_ge(ids_set[L], i + 1)
                    if not (isinstance(i, int) and i < 2):
                        pool.wait_ge(y_stored[L][r], (i - r) * 32)
                    pool.tensor_copy(ids_now[:, r, :], ids[:, i, :] if isinstance(i, int) else
                                     ids[:, bass.ds(i, 1), :].rearrange("p a q -> p (a q)")).then_inc(ids_now_set[L], 1)

                def scatter(i, r, part=range(4)):
                    if 0 in part:
                        pool.wait_ge(ids_now_set[L], i + 1)
                        pool.wait_ge((y_read[0], y_set[1])[L], i + 1)
                        pool.sem_inc(rows_go, 1)
                    for q in part:
                        pool.indirect_dma_start(
                            out=token_y, out_offset=bass.IndirectOffsetOnAxis(ap=ids_now[:, r, q:q + 1], axis=0),
                            in_=ysb[:, r, q, :], in_offset=None).then_inc(y_stored[L][r], 16)

                low_weights(0, 0)
                low_weights(1, 1)
                if L == 0:
                    def rows(i, r):
                        rows_of_tile(i, r)
                        scatter(i, r)

                    low_weights(2, 0)
                    rows(0, 0)
                    for i in (2, 3):
                        low_weights(i + 1, 1 - i % 2)
                        rows(i - 1, 1 - i % 2)
                    with pool.Fori(2, TILES // 2) as k:
                        for r in range(2):
                            low_weights(k * 2 + r + 1, 1 - r)
                            rows(k * 2 + r - 1, 1 - r)
                    for i in range(TILES - 2, TILES):
                        rows(i, i % 2)
                    return

                def tile(i, r, k, more=True):
                    if more:
                        low_weights(i + 1, 1 - r)
                    rows_of_tile(i - 1, 1 - r)
                    add_bias(i, r, k)
                    rows = not (isinstance(i, int) and i < 2)
                    if rows:
                        scatter(i - 2, r, range(2))
                    root(i - 1, 1 - r)
                    if rows:
                        scatter(i - 2, r, range(2, 4))

                add_bias(0, 0, 0)
                for i in range(1, 4):
                    tile(i, i % 2, i // 2)
                with pool.Fori(2, TILES // 2) as k:
                    for r in range(2):
                        tile(k * 2 + r, r, k)
                tile(TILES - 1, 0, TILES // 2, more=False)
                rows_of_tile(TILES - 1, 0)
                scatter(TILES - 2, 1)
                root(TILES - 1, 0)
                scatter(TILES - 1, 0)

            for b in range(SEQS):
                token_root(0, b)
            diagonal_weights()
            norm_and_scatter(0)
            experts(0)
            for b in range(SEQS + 2):
                if b < SEQS:
                    add(b)
                if b >= 2:
                    token_root(1, b - 2)
            norm_and_scatter(1)
            experts(1)
            for b in range(SEQS):
                gated(1, b)

        @block.tensor
        def _(pe):
            def columns():
                pe.wait_ge(ld_a, 16 * N_A)
                for n in range(3):
                    mm = pe.matmul(ps[:, 7, n:n + 1], bqkv_row[0:1, n * D:(n + 1) * D], one_row[0:1, 0:1],
                                   start=True, stop=True)
                mm.then_inc(pe_setup, 1)

            def block1_weights():
                pe.wait_ge(pool_con, 13)
                pe.wait_ge(ld_b, 16 * N_B)
                for n in range(4):
                    pe.transpose(ps[:, 5, n * P:(n + 1) * P], w4[:, n, :], ident[:, :])
                nb = 8 * EXPERTS
                pe.transpose(ps[:, 3, 0:nb], ebias_rows[:, :], ident[0:nb, 0:nb])
                pe.transpose(ps[:, 4, 0:P], ldiag[:, :, :].rearrange("p h d -> p (h d)"), ident[:, :]
                             ).then_inc(pe_setup, 1)

                pe.wait_ge(setup_ev, 1)
                pe.matmul(ps[:, 4, P:2 * P], ldiagT[:, :], ldiagT[:, :], start=True, stop=True).then_inc(pe_setup, 1)
                pe.wait_ge(setup_ev, 2)
                pe.matmul(ps[:, 4, 2 * P:3 * P], bdiag[:, :], w4T[:, 3, :], start=True, stop=True
                          ).then_inc(pe_setup, 1)

            def norm(L):
                def router(b):
                    pe.wait_ge(xhi_set[L], b + 1)
                    pe.wait_ge(xlo_set[L], b + 1)
                    for t in range(QT):
                        at = (b * QT + t) * 2 * EXPERTS
                        tok = slice(t * P, (t + 1) * P)
                        pe.matmul(ps[:, 2, at:at + 2 * EXPERTS], xT_hi[:, b, tok],
                                  wr[:, L, :, :].rearrange("p n e -> p (n e)"), start=True, stop=False,
                                  skip_group_check=True)
                        mm = pe.matmul(ps[:, 2, at:at + EXPERTS], xT_lo[:, b, tok], wr[:, L, 0, :],
                                       start=False, stop=True, skip_group_check=True)
                    mm.then_inc(logit_mm[L], 1)

                for b in range(SEQS):
                    if L == 0 and b == 4:
                        columns()
                    pe.wait_ge(xn_set[L], b + 1)
                    if b >= 2:
                        pe.wait_ge(xhi_set[L], b - 1)
                        pe.wait_ge(xlo_set[L], b - 1)
                    for t in range(QT):
                        mm = pe.transpose(ps[:, b % 2, t * P:(t + 1) * P], xn[:, b * QT + t, 0:D], ident[:, :])
                    mm.then_inc(tp_done[L], 1)
                    if b >= 1:
                        router(b - 1)
                router(SEQS - 1)

            def routing(L):
                pe.wait_ge(hot_set[L], 1)
                for e in range(EXPERTS):
                    mm = pe.matmul(ps[0:CHOICES, 3, e:e + 1],
                                   hot_b[:, :, :, e].rearrange("p t k -> p (t k)"), ones_b[:, :],
                                   start=True, stop=True)
                mm.then_inc(tot_mm[L], 1)
                pe.wait_ge(carry_set[L], 1)
                pe.matmul(ps[:, 4, 0:EXPERTS], ones64[:, :], tot[:, :], start=True, stop=True)
                pe.matmul(ps[:, 5, :], before[:, :], hot_b[:, :, :, :].rearrange("p t k e -> p (t k e)"),
                          start=True, stop=False)
                pe.matmul(ps[:, 5, :], ones64[:, :], carry[:, :, :].rearrange("p c e -> p (c e)"),
                          start=False, stop=True).then_inc(pos_mm[L], 1)

            def attend(u, g, b, now):
                v = u + 2
                for t in range(4):
                    if t == 0 and now.main:
                        pe.wait_ge(m_in, (u + 1) * 32)
                    if t == 0 and now.max:
                        pe.wait_ge(group_in[g % 2], (v - g % 2 + 2) * 40)
                    for j in range(4):
                        i = t * 4 + j
                        if now.main:
                            if not (now.first and i < 3):
                                pe.wait_ge(exp_set, u * 16 + read_before(i))
                            pe.matmul(ps[:, 2 + bank_of(i), :], Km[g][:, j, t * P:(t + 1) * P], Qs[:, g, :],
                                      start=True, stop=True).then_inc(st_mm, 1)
                        if now.max:
                            if not (isinstance(v, int) and v * 16 + i < 3):
                                pe.wait_ge(max_set, v * 16 + read_before(i))
                            g2 = (g + 2) % GROUPS
                            pe.matmul(ps[:, (0, 1, 7)[bank_of(i)], :], Qs[:, g2, t * P:(t + 1) * P], Km[g2][:, j, :],
                                      start=True, stop=True).then_inc(s_mm, 1)
                        if j == 1 and t == 0 and now.tail:
                            output(u - 1, (g + 3) % GROUPS, 3)
                        if j == 1 and t == 0 and now.low:
                            pe.wait_ge(max_set, (u + 2) * 16)
                            if now.halves:
                                pe.wait_ge(lo_set, b * 2 + 6)
                            if g == 1:
                                pe.wait_ge(attn_set, b + 1)
                            if isinstance(u, int) and u == 0:
                                pe.wait_ge(vT_set, 1)
                            if isinstance(u, int) and u >= 2:
                                pe.wait_ge(onorm_set, u - 1)
                            pe.transpose(ps[0:16, 6, 0:P], nmax[:, (g + 1) % 2, :], ident[:, :]).then_inc(nmT_mm, 1)
                        if j == 1 and t >= 1 and now.main:
                            if t == 1:
                                if not now.first:
                                    pe.wait_ge(o_read, u)
                                pe.wait_ge(vaug_set, b + 1)
                            output(u, g, t - 1)
                    if t == 0:
                        if g == 0 and now.main:
                            pe.wait_ge(mhi_set, u + 2)
                            pe.wait_ge(mlo_set, u + 2)
                            pe.wait_ge(vT_set, b + 1)
                            for q in range(QT):
                                mm = pe.transpose(ps[:, 6, q * P:(q + 1) * P], vT[:, q * P:(q + 1) * P], ident[:, :])
                            mm.then_inc(vtp_mm, 1)
                    if t == 1 and now.tail:
                        if g == 0 and now.main:
                            pe.wait_ge(vaug_set, b + 1)
                        elif now.low:
                            pe.wait_ge(mhi_set, u + 2)
                            pe.wait_ge(mlo_set, u + 2)
                        else:
                            pe.wait_ge(onorm_set, u - 1)
                        pe.wait_ge(o_read, u)
                        for q in range(QT):
                            mm = pe.transpose(ps[:, 6, q * P:(q + 1) * P], o_sb[:, q * P:(q + 1) * P], ident[:, :])
                        mm.then_inc(oT_mm, 1)
                    if t == 2:
                        if now.next:
                            if now.tail:
                                pe.wait_ge(onorm_set, u)
                            project(1, b + 2, 6)
                        if g == 0 and now.tail:
                            pe.wait_ge(onorm_set, u)
                            for q in range(QT):
                                mm = pe.transpose(ps[:, 6, q * P:(q + 1) * P], onorm[:, q, :], ident[:, :])
                            mm.then_inc(onT_mm, 1)
                        if g == 3 and now.load:
                            if now.tail:
                                pe.wait_ge(onorm_set, u)
                            elif now.low:
                                pe.wait_ge(mhi_set, u + 2)
                                pe.wait_ge(mlo_set, u + 2)
                            split3(pe, ps[:, 6, :], wq_hi[:, 2, :], wq_lo[:, 2, :], seq_of(xT_hi, b + 1),
                                   seq_of(xT_lo, b + 1)).then_inc(vT_mm, 1)
                    if t == 3:
                        if now.next:
                            pe.wait_ge(lo_set, b * 2 + 5)
                            project(0, b + 2, 6)
                        if g == 0 and now.tail:
                            pe.wait_ge(onT_set, b)
                            for q in range(QT):
                                mm = pe.matmul(ps[:, 6, q * P:(q + 1) * P], onT[:, q * P:(q + 1) * P], wproj[:, :],
                                               start=True, stop=True)
                            mm.then_inc(out_mm, 1)

            def project(which, b, bank):
                split3(pe, ps[:, bank, :], wq_hi[:, which, :], wq_lo[:, which, :],
                       seq_of(xT_hi, b), seq_of(xT_lo, b)).then_inc(proj_mm, 1)

            def output(u, g, t):
                pe.wait_ge(exp_set, u * 16 + (4 * t + 4))
                for j in range(4):
                    mm = pe.matmul(ps[32 * j:32 * j + 32, 5, :], vaug[:, t, 4 * g + j, :],
                                   probs[:, t % 2, j, :], start=(t == 0), stop=(t == 3))
                mm.then_inc(pv_mm, 1)

            def experts(L):
                F = (F0, F1)[L]
                nch = len(CH[L])
                last = nch - 1

                def turn(i, r, k):
                    pe.wait_ge(xg_in[L][r], (k + 1) * 16)
                    if not (isinstance(i, int) and i == 0):
                        pe.wait_ge(ghi_set[L], i)
                        pe.wait_ge(glo_set[L], i)
                    for q in range(4):
                        mm = pe.transpose(ps[:, 0, q * P:(q + 1) * P], xg[:, r, q, 0:D], ident[:, :])
                    mm.then_inc(gT_mm[L], 1)

                def up(i, r, f, fresh=False):
                    n, par = i * nch + f, (r * nch + f) % 2
                    at, M = CH[L][f]
                    if f == 0:
                        pe.wait_ge(ghi_set[L], i + 1)
                        pe.wait_ge(glo_set[L], i + 1)
                        pe.wait_ge(w_lo_set[L], i + 1)
                    for bank, col, done, free in ((1, 0, gate_mm, act_set), (2, F, up_mm, (h_set, act_set)[L])):
                        if not fresh:
                            pe.wait_ge(free[L], n - 1)
                        c = slice(col + at, col + at + M)
                        split3(pe, ps[0:M, bank + 2 * par, :], wu_hi[:, r, c], wu_lo[:, r, c],
                               gT_hi[:, r, :], gT_lo[:, r, :]).then_inc(done[L], 1)

                def down(i, r, f, k, fresh=False):
                    n, par = i * nch + f, (r * nch + f) % 2
                    M = CH[L][f][1]
                    pe.wait_ge(h_set[L], n + 1)
                    if f == 0:
                        pe.wait_ge(dn_in[L][r], (k + 1) * 16 * NDN[L])
                        if not fresh:
                            pe.wait_ge(y_read[L], i - 1)
                    for q in range(4):
                        mm = pe.matmul(ps[:, 5 + r, q * P:(q + 1) * P], hT[0:M, par, q * P:(q + 1) * P],
                                       wdn[0:M, r, f, :], start=(f == 0 and q == 0), stop=(f == last and q == 3),
                                       skip_group_check=True)
                    mm.then_inc(down_mm[L], 1)

                def tile(i, r, k, fresh=False, more=True):
                    for f in range(nch):
                        if f < last:
                            up(i, r, f + 1, fresh=fresh and r == 0 and f + 1 < 2)
                        elif more:
                            up(i + 1, 1 - r, 0)
                        if f == 0 and more:
                            turn(i + 1, 1 - r, k + r)
                        down(i, r, f, k, fresh=fresh)

                turn(0, 0, 0)
                up(0, 0, 0, fresh=True)
                tile(0, 0, 0, fresh=True)
                tile(1, 1, 0, fresh=True)
                with pe.Fori(1, TILES // 2) as k:
                    for r in range(2):
                        tile(k * 2 + r, r, k)
                tile(TILES - 1, 0, TILES // 2, more=False)

            def chunk(m, s, k, now):
                if now(-2):
                    pe.wait_ge(y1T_set, m - 1)
                    pe.matmul(ps[:, 7, 0:P], y1T[:, s % 2, :], wcomb[:, :], start=True, stop=True
                              ).then_inc(out1_mm, 1)
                if now(3):
                    r = (s + 3) % 4
                    pe.wait_ge(xs_in[r], (k * 2 + ((s + 3) // 4 + 1)) * 32)
                    if now(1):
                        pe.wait_ge(qkv_set, m + 2)
                    w = [v[:, :, :].rearrange("p n d -> p (n d)") for v in (w3_hi, w3_lo)]
                    bank = ps[:, 4 + (s + 3) % 2, 0:3 * D]
                    pe.matmul(bank, xs[:, r, 0, :], w[0], start=True, stop=False)
                    pe.matmul(bank, xs[:, r, 0, :], w[1], start=False, stop=False)
                    pe.matmul(bank, xs[:, r, 1, :], w[0], start=False, stop=True).then_inc(qkv_mm, 1)

                def sums(at, mask, start, stop):
                    for n in range(2):
                        for half_kv in (kv_hi, kv_lo):
                            mm = pe.matmul(ps[:, 2 * (at % 2) + n, :], mask[:, :],
                                           half_kv[:, at % 4, n * 512:(n + 1) * 512],
                                           start=start and half_kv is kv_hi, stop=stop and half_kv is kv_lo,
                                           skip_group_check=True)
                    return mm

                if now(0):
                    pe.wait_ge(kv_lo_set, m + 1)
                    if now(-2):
                        pe.wait_ge(weigh_set, m - 1)
                    sums(s, tri, s % 8 < 2, s % 8 >= 6).then_inc(sum_mm, 1)
                if now(-1):
                    pe.wait_ge(weigh_set, m)
                    if (s - 1) % 8 < 6:
                        sums(s - 1, cotri, False, False)
                    pe.wait_ge(y1_set, m)
                    if now(-2):
                        pe.wait_ge(y1T_set, m - 1)
                    pe.transpose(ps[:, 6, 0:P], y1[:, (s - 1) % 2, :], ident[:, :]).then_inc(y1T_mm, 1)

            pe.wait_ge(pool_mem, 10)
            pe.wait_ge(pool_con, 9)
            norm(0)
            pe.wait_ge(setup_done, 1)
            project(1, 0, 7)
            project(0, 0, 6)
            routing(0)
            pe.wait_ge(pos_set[0], 2)
            pe.wait_ge(pos_set[0], 2)
            steps(pe, attend)
            pe.wait_ge(attn_set, SEQS + 1)
            block1_weights()
            experts(0)
            pe.wait_ge(y_read[0], TILES)
            norm(1)
            routing(1)
            pe.wait_ge(pos_set[1], 2)
            chunk_steps(pe, chunk)
            pe.wait_ge(attn1_set, TOK_TILES)
            experts(1)

        @block.scalar
        def _(act):
            ident_f, copy_f = ACT.Identity, ACT.Copy

            def high_tokens(L, b):
                act.wait_ge(tp_done[L], b + 1)
                act.activation(xT_hi[:, b, :], ps[:, b % 2, :], copy_f).then_inc(xhi_set[L], 1)

            def exponentials(L):
                act.wait_ge(z_set[L], 1)
                act.activation(elog[:, :, :], logits[:, :, :], ACT.Exp).then_inc(e_set[L], 1)

            def high_half(b, o, bank):
                act.wait_ge(proj_mm, b * 2 + (o + 1))
                if not (isinstance(b, int) and b < 1):
                    act.wait_ge(halves_out, b * 96)
                act.activation(Hi[:, 1 - o, :], ps[:, bank, :], ident_f, bias=cols[:, 1 - o:2 - o]).then_inc(hi_set, 1)

            def attend(u, g, b, now):
                for t in range(4):
                    for j in range(4):
                        i = t * 4 + j
                        if now.main:
                            if j == 0 and not (now.first and t < 2):
                                act.wait_ge(pv_mm, u * 4 + (t - 1))
                            act.wait_ge(st_mm, u * 16 + (i + 1))
                            act.activation(probs[:, t % 2, j, :], ps[:, 2 + bank_of(i), :], ACT.Exp,
                                           scale=SCALE).then_inc(exp_set, 1)
                        if (t, j) == (0, 3) and now.tail:
                            act.wait_ge(pv_mm, u * 4)
                            act.activation(o_sb, ps[:, 5, :], copy_f).then_inc(o_read, 1)
                        if (t, j) == (0, 2) and now.low:
                            act.wait_ge(nmT_mm, u + 2)
                            if not (isinstance(u, int) and u + 1 < 2):
                                act.wait_ge(m_in, u * 32)
                            act.activation(m_hi[:, (g + 1) % 2, :], ps[0:16, 6, 0:P], copy_f).then_inc(mhi_set, 1)
                        if (t, j) == (3, 0) and now.next:
                            high_half(b + 2, 0, 6)
                        if (t, j) == (0, 0) and now.halves:
                            high_half(b + 2, 1, 6)
                        if (t, j) == (3, 0) and g == 3 and now.load:
                            act.wait_ge(vT_mm, b + 2)
                            act.activation(vT, ps[:, 6, :], ident_f, bias=cols[:, 2:3]).then_inc(vT_set, 1)
                        if (t, j) == (3, 0) and g == 0 and now.tail:
                            act.wait_ge(onT_mm, b)
                            act.activation(onT, ps[:, 6, :], copy_f).then_inc(onT_set, 1)

            def experts(L):
                nch = len(CH[L])

                def high_rows(i, r):
                    act.wait_ge(gT_mm[L], i + 1)
                    act.activation(gT_hi[:, r, :], ps[:, 0, :], copy_f).then_inc(ghi_set[L], 1)

                def write_y(i, r, k):
                    act.wait_ge(down_mm[L], (i + 1) * nch)
                    act.wait_ge(ids_now_set[L], i + 1)
                    act.activation(ysb[:, r, :, :].rearrange("p q d -> p (q d)"), ps[:, 5 + r, :], copy_f
                                   ).then_inc(y_read[L], 1)

                def tile(i, r, k, first=False, last=False):
                    for f in range(nch):
                        n, par, M = i * nch + f, (r * nch + f) % 2, CH[L][f][1]
                        if L == 1 and f == 0:
                            act.wait_ge(dn_in[L][r], (k + 1) * 16 * NDN[L])
                        if not (first and r == 0 and f < 2):
                            act.wait_ge(h_set[L], n - 1)
                        act.wait_ge(gate_mm[L], n + 1)
                        if L == 0:
                            act.activation(gact[0:M, par, :], ps[0:M, 1 + 2 * par, :], ACT.Gelu).then_inc(act_set[L], 1)
                        else:
                            act.activation(gact[:, par, :], ps[:, 1 + 2 * par, :], ACT.Gelu,
                                           bias=ebcol[:, r, f:f + 1]).then_inc(gelu_set, 1)
                            act.wait_ge(up_mm[L], n + 1)
                            act.activation(gsig[:, par, :], ps[:, 2 + 2 * par, :], ACT.Tanh, scale=0.5,
                                           bias=ebcol[:, r, 4 + f:5 + f]).then_inc(act_set[L], 1)
                        if L == 0 and f == nch - 1 and not (first and r == 0):
                            write_y(i - 1, 1 - r, k - 1 + r)
                        if f == 1 and not last:
                            high_rows(i + 1, 1 - r)

                high_rows(0, 0)
                tile(0, 0, 0, first=True)
                tile(1, 1, 0, first=True)
                with act.Fori(1, TILES // 2) as k:
                    tile(k * 2, 0, k)
                    tile(k * 2 + 1, 1, k)
                tile(TILES - 1, 0, TILES // 2, last=True)
                if L == 0:
                    write_y(TILES - 1, 0, TILES // 2)

            def chunk(m, s, k, now):
                if now(1):
                    if (s + 1) % 8 == 7:
                        act.wait_ge(kv_eighth_set, k + (s + 1) // 8 + 1)
                    else:
                        act.wait_ge(kv_set, k * 7 + (s + 2 - (s + 1) // 8))
                    act.activation(kv_hi[:, (s + 1) % 4, :], kv[:, (s + 1) % 2, :, :, :].rearrange("p h e d -> p (h e d)"),
                                   copy_f).then_inc(kv_hi_set, 1)
                if now(3):
                    act.wait_ge(qkv_mm, m + 4)
                    if now(-1):
                        act.wait_ge(weigh_set, m)
                    act.activation(qkv[:, (s + 3) % 4, :, :].rearrange("p n d -> p (n d)"),
                                   ps[:, 4 + (s + 3) % 2, 0:3 * D], copy_f).then_inc(qkv_set, 1)
                if now(-2):
                    b, c = chunk_of(s - 2, k)
                    t = b * QT + c
                    act.wait_ge(out1_mm, m - 1)
                    act.activation(attn[:, t, :] if isinstance(t, int) else
                                   attn[:, bass.ds(t, 1), :].rearrange("p a d -> p (a d)"),
                                   ps[:, 7, 0:P], copy_f).then_inc(attn1_set, 1)
                if now(-1):
                    act.wait_ge(y1T_mm, m)
                    act.activation(y1T[:, (s - 1) % 2, :], ps[:, 6, 0:P], copy_f).then_inc(y1T_set, 1)

            def first_rows(L, b):
                r = b % 2
                act.wait_ge(gathered[b % 4], 64 * L + 32 * (b // 4 + 1))
                if b >= 2:
                    act.wait_ge(silu_set[L], b - 1)
                for q in range(QT):
                    ins = act.activation(zg[:, r, q, :], yg[:, b % 4, 0, q, :], copy_f,
                                         scale=wsel[:, b * QT + q, 0:1])
                ins.then_inc(z_first[L], 1)

            def gate(L, b):
                r = b % 2
                act.wait_ge(z_ready[L], b + 1)
                if b >= 2:
                    act.wait_ge(x_set[L], b - 1)
                act.activation(sg[:, r, :, :], zg[:, r, :, :], ACT.Silu).then_inc(silu_set[L], 1)

            for b in range(SEQS):
                high_tokens(0, b)
            act.wait_ge(setup_done, 1)
            high_half(0, 0, 7)
            high_half(0, 1, 6)
            exponentials(0)
            act.wait_ge(pool_con, 13)
            act.wait_ge(slots_zero, 32)
            act.wait_ge(xn_set[0], SEQS)
            for g in range(GROUPS):
                act.activation(Km[g], spread(kmask[:, :], 2, [P, 4, SEQ]), copy_f).then_inc(km_set, 1)
            act.wait_ge(pos_set[0], 2)
            steps(act, attend)
            experts(0)
            first_rows(0, 0)
            for b in range(SEQS + 3):
                if b + 1 < SEQS:
                    first_rows(0, b + 1)
                if b < SEQS:
                    gate(0, b)
                if b >= 3:
                    high_tokens(1, b - 3)
            exponentials(1)
            chunk_steps(act, chunk)
            experts(1)
            first_rows(1, 0)
            for b in range(SEQS):
                if b + 1 < SEQS:
                    first_rows(1, b + 1)
                gate(1, b)

        @block.vector
        def _(dve):
            links = [0]

            def link(ins):
                ins.then_inc(dve_chain, 1)
                links[0] += 1
                dve.wait_ge(dve_chain, links[0])

            def split(hi, lo, src):
                link(dve.tensor_copy(hi, src))
                link(dve.tensor_tensor(lo, src, hi.bitcast(F32), ALU.subtract))

            def setup():
                dve.wait_ge(ld_a, 16 * N_A)
                split(wr[:, :, 0, :], wr[:, :, 1, :], wrout[:, :, :])
                split(wq_hi[:, :, :].rearrange("p n d -> p (n d)"), wq_lo[:, :, :].rearrange("p n d -> p (n d)"),
                      wqkv[:, :])

            def setup_end():
                dve.wait_ge(pe_setup, 1)
                dve.tensor_copy(cols[:, :], ps[:, 7, 0:3]).then_inc(setup_done, 1)
                dve.wait_ge(setup_done, 1)

            def block1_weights():
                dve.wait_ge(pe_setup, 2)
                link(dve.tensor_copy(w4T[:, :, :].rearrange("p n m -> p (n m)"), ps[:, 5, :]))
                dve.tensor_copy(ldiagT[:, :], ps[:, 4, 0:P]).then_inc(setup_ev, 1)
                dve.wait_ge(pool_con, 13)
                link(dve.tensor_copy(tri[:, :], causal[:, :]))
                link(dve.tensor_scalar(cotri[:, :], causal[:, :], -1.0, 1.0, ALU.mult, ALU.add))
                split(w3_hi[:, :, :], w3_lo[:, :, :], w4T[:, 0:3, :])
                nb = 4 * EXPERTS
                link(dve.tensor_copy(ebias[:, :, 0:4], ps[:, 3, 0:nb].rearrange("p (e c) -> p e c", e=EXPERTS)))
                link(dve.tensor_scalar(ebias[:, :, 4:8], ps[:, 3, nb:2 * nb].rearrange("p (e c) -> p e c", e=EXPERTS),
                                       0.5, None, ALU.mult))
                dve.wait_ge(pe_setup, 3)
                dve.tensor_copy(bdiag[:, :], ps[:, 4, P:2 * P]).then_inc(setup_ev, 1)
                dve.wait_ge(pe_setup, 4)
                dve.tensor_copy(wcomb[:, :], ps[:, 4, 2 * P:3 * P]).then_inc(setup_ev, 1)

            def statistics(L, b):
                tiles = range(b * QT, (b + 1) * QT)
                for t in tiles:
                    ins = dve.bn_stats(stats[:, t, :], xres[:, t, :])
                link(ins)
                for t in tiles:
                    ins = dve.bn_aggr(mv[:, t, :], stats[:, t, :])
                link(ins)
                t = slice(b * QT, (b + 1) * QT)
                dve.tensor_scalar(veps[:, t], mv[:, t, 1], EPS_LN, None, ALU.add).then_inc(veps_set[L], 1)

            def normed(L, b):
                dve.wait_ge(rstd_set[L], b + 1)
                if L == 1:
                    dve.wait_ge(scattered[0], 16 * CHOICES)
                for t in range(b * QT, (b + 1) * QT):
                    ins = dve.tensor_scalar(xn[:, t, 0:D], xres[:, t, :], mv[:, t, 0:1], rstd[:, t:t + 1],
                                            ALU.subtract, ALU.mult)
                ins.then_inc(xn_set[L], 1)

            def low_tokens(L, b):
                dve.wait_ge(xhi_set[L], b + 1)
                dve.wait_ge(tp_done[L], b + 1)
                dve.tensor_tensor(xT_lo[:, b, :], ps[:, b % 2, :], xT_hi[:, b, :].bitcast(F32),
                                  ALU.subtract).then_inc(xlo_set[L], 1)

            def routing(L):
                S3 = [P, TOK_TILES, EXPERTS]
                dve.wait_ge(logit_mm[L], SEQS)
                dve.wait_ge(pool_con, 13)
                link(dve.tensor_reduce(logits[:, :, :], ps[:, 2, :].rearrange("p (t n e) -> p t e n", n=2, e=EXPERTS),
                                       AX, ALU.add))
                if L == 1:
                    link(dve.tensor_tensor(logits[:, :, :], logits[:, :, :], spread(br_bc[:, :], 1, S3), ALU.add))
                link(dve.tensor_reduce(lmax[:, :], logits[:, :, :], AX, ALU.max))
                dve.tensor_tensor(logits[:, :, :], logits[:, :, :], spread(lmax[:, :], 2, S3),
                                  ALU.subtract).then_inc(z_set[L], 1)
                dve.wait_ge(e_set[L], 1)
                link(dve.tensor_reduce(esum[:, :], elog[:, :, :], AX, ALU.add))
                for k in range(2):
                    link(dve.tensor_reduce(top[:, :, k], elog[:, :, :], AX, ALU.max))
                    link(dve.tensor_tensor(pick[:, :, :], elog[:, :, :], spread(top[:, :, k], 2, S3), ALU.is_ge))
                    link(dve.tensor_tensor(pick[:, :, :], pick[:, :, :], spread(key8[:, :], 1, S3), ALU.mult))
                    link(dve.tensor_reduce(kmax[:, :], pick[:, :, :], AX, ALU.max))
                    link(dve.tensor_tensor(hot[:, :, k, :], pick[:, :, :], spread(kmax[:, :], 2, S3), ALU.is_equal))
                    if k == 0:
                        link(dve.scalar_tensor_tensor(elog[:, :, :], hot[:, :, 0, :], -2.0, elog[:, :, :],
                                                      ALU.mult, ALU.add))
                dve.tensor_copy(hot_b[:, :, :, :], hot[:, :, :, :]).then_inc(hot_set[L], 1)
                if L == 1:
                    link(dve.tensor_tensor(esum[:, :], top[:, :, 0], top[:, :, 1], ALU.add))
                link(dve.reciprocal(esum[:, :], esum[:, :]))
                link(dve.tensor_tensor(wsel[:, :, :], top[:, :, :], spread(esum[:, :], 2, [P, TOK_TILES, 2]), ALU.mult))
                dve.wait_ge(tot_mm[L], 1)
                link(dve.tensor_copy(tot[:, :], ps[0:CHOICES, 3, 0:EXPERTS]))
                C3 = [CHOICES, CHOICES, EXPERTS]
                dve.tensor_tensor(carry[:, :, :], spread(before64[:, :], 2, C3), spread(tot[:, :], 1, C3),
                                  ALU.mult).then_inc(carry_set[L], 1)
                dve.wait_ge(pos_mm[L], 1)
                E3 = [P, EXPERTS, EXPERTS]
                link(dve.tensor_copy(off[:, :], ps[:, 4, 0:EXPERTS]))
                link(dve.tensor_tensor(cmp8[:, :, :], spread(off[:, :], 2, E3), spread(thr[:, :], 1, E3), ALU.is_gt))
                link(dve.tensor_reduce(ntile[:, :], cmp8[:, :, :], AX, ALU.add))
                link(dve.tensor_tensor(cmp8[:, :, :], before8[:, :, :], spread(ntile[:, :], 1, E3), ALU.mult))
                link(dve.tensor_reduce(first[:, :], cmp8[:, :, :], AX, ALU.add))
                link(dve.tensor_scalar(off[:, :], first[:, :], float(TILE), None, ALU.mult))
                W3 = [P, CHOICES, EXPERTS]
                link(dve.tensor_tensor(posw[:, :, :], ps[:, 5, :].rearrange("p (c e) -> p c e", e=EXPERTS),
                                       spread(off[:, :], 1, W3), ALU.add))
                link(dve.tensor_tensor(posw[:, :, :], posw[:, :, :],
                                       hot[:, :, :, :].rearrange("p t k e -> p (t k) e"), ALU.mult))
                link(dve.tensor_reduce(posf[:, :], posw[:, :, :], AX, ALU.add))
                if L == 1:
                    dve.wait_ge(z_ready[0], SEQS)
                dve.tensor_copy(pos[:, :], posf[:, :]).then_inc(pos_set[L], 1)
                N3 = [1, TILES, EXPERTS - 1]
                link(dve.tensor_tensor(ecmp[:, :, :], spread(first[0:1, 1:EXPERTS], 1, N3),
                                       spread(tile_no[:, :], 2, N3), ALU.is_le))
                link(dve.tensor_reduce(eidf[:, :], ecmp[:, :, :], AX, ALU.add))
                dve.tensor_copy(eid[:, :], eidf[:, :]).then_inc(pos_set[L], 1)

            def low_half(b, o, bank):
                dve.wait_ge(hi_set, b * 2 + (o + 1))
                dve.scalar_tensor_tensor(Lo[:, 1 - o, :], ps[:, bank, :], cols[:, 1 - o:2 - o],
                                         Hi[:, 1 - o, :].bitcast(F32), ALU.add, ALU.subtract).then_inc(lo_set, 1)

            def attend(u, g, b, now):
                gt, v = (g + 3) % GROUPS, u + 2
                for t in range(4):
                    for j in range(4):
                        i = t * 4 + j
                        if now.max:
                            dve.wait_ge(s_mm, v * 16 + (i + 1))
                            at = j * 4 + t
                            dve.tensor_reduce(nmax[:, g % 2, at:at + 1], ps[:, (0, 1, 7)[bank_of(i)], :], AX, ALU.max,
                                              negate=True).then_inc(max_set, 1)
                        if (t, j) == (0, 3) and now.low:
                            dve.wait_ge(mhi_set, u + 2)
                            dve.wait_ge(nmT_mm, u + 2)
                            if not (isinstance(u, int) and u + 1 < 2):
                                dve.wait_ge(m_in, u * 32)
                            r = (g + 1) % 2
                            dve.tensor_tensor(m_lo[:, r, :], ps[0:16, 6, 0:P], m_hi[:, r, :].bitcast(F32),
                                              ALU.subtract).then_inc(mlo_set, 1)
                        if (t, j) == (1, 0) and g == 0 and now.main:
                            dve.wait_ge(vtp_mm, b + 1)
                            dve.tensor_copy(vaug[:, :, :, 0:HD],
                                            ps[:, 6, :].rearrange("p (t h r) -> p t h r", t=QT, r=HD)).then_inc(vaug_set, 1)
                        if (t, j) == (3, 2) and now.next:
                            low_half(b + 2, 0, 6)
                        if (t, j) == (0, 1) and now.halves:
                            low_half(b + 2, 1, 6)
                        if (t, j) == (2, 1) and now.tail:
                            dve.wait_ge(oT_mm, u)
                            turned = ps[:, 6, :].rearrange("p (q j r) -> p q j r", q=QT, j=4)
                            dve.reciprocal(rden[:, :, :], turned[:, :, :, HD]).then_inc(rden_set, 1)
                            dve.wait_ge(rden_set, u)
                            dve.tensor_tensor(onorm[:, :, 32 * gt:32 * gt + 32].rearrange("p q (j r) -> p q j r", j=4),
                                              turned[:, :, :, 0:HD], spread(rden[:, :, :], 3, [P, QT, 4, HD]),
                                              ALU.mult).then_inc(onorm_set, 1)
                        if (t, j) == (3, 3) and g == 0 and now.tail:
                            dve.wait_ge(out_mm, b)
                            dve.tensor_tensor(rows_of(attn, b - 1), ps[:, 6, :].rearrange("p (q d) -> p q d", q=QT),
                                              spread(bproj_bc[:, :], 1, [P, QT, D]), ALU.add).then_inc(attn_set, 1)

            def experts(L):
                NW = 2 * (F0, F1)[L]
                nch = len(CH[L])

                def high_weights(i, r, k):
                    dve.wait_ge(up_in[L][r], (k + 1) * 32)
                    dve.tensor_copy(wu_hi[:, r, 0:NW], wraw[:, r, 0:NW]).then_inc(w_hi_set[L], 1)

                def low_rows(i, r):
                    dve.wait_ge(gT_mm[L], i + 1)
                    dve.wait_ge(ghi_set[L], i + 1)
                    dve.tensor_copy(ids[:, i, :] if isinstance(i, int) else
                                    ids[:, bass.ds(i, 1), :].rearrange("p a q -> p (a q)"),
                                    xg[:, r, :, D]).then_inc(ids_set[L], 1)
                    dve.tensor_tensor(gT_lo[:, r, :], ps[:, 0, :], gT_hi[:, r, :].bitcast(F32),
                                      ALU.subtract).then_inc(glo_set[L], 1)

                def residual(i, r):
                    dve.wait_ge(down_mm[L], (i + 1) * nch)
                    dve.wait_ge(xb_set, i + 1)
                    dve.wait_ge(ids_now_set[L], i + 1)
                    dve.scalar_tensor_tensor(ysb[:, r, :, :].rearrange("p q d -> p (q d)"), ps[:, 5 + r, :], 0.5,
                                             xb[:, r, :, :].rearrange("p q d -> p (q d)"), ALU.mult, ALU.add
                                             ).then_inc(y_read[L], 1)
                    dve.wait_ge(y_read[L], i + 1)
                    for q in range(4):
                        dve.bn_stats(estats[:, q, :], ysb[:, r, q, :]).then_inc(est_chain, 1)

                def variance(i, r):
                    even, odd = estats[:, :, 0:3], estats[:, :, 3:6]
                    dve.wait_ge(est_chain, i * 10 + 4)
                    dve.tensor_tensor(eagg[:, 0, :], even[:, :, 1], odd[:, :, 1], ALU.add).then_inc(est_chain, 1)
                    dve.tensor_tensor(eagg[:, 1, :], even[:, :, 1], odd[:, :, 1], ALU.subtract).then_inc(est_chain, 1)
                    dve.tensor_tensor(eagg[:, 2, :], even[:, :, 2], odd[:, :, 2], ALU.add).then_inc(est_chain, 1)
                    dve.wait_ge(est_chain, i * 10 + 7)
                    dve.tensor_scalar(emean[:, :], eagg[:, 0, :], 0.5, None, ALU.mult).then_inc(est_chain, 1)
                    dve.tensor_tensor(eagg[:, 3, :], eagg[:, 1, :], eagg[:, 1, :], ALU.mult).then_inc(est_chain, 1)
                    dve.tensor_scalar(eagg[:, 4, :], eagg[:, 2, :], 1.0 / D, EPS_EXPERT, ALU.mult, ALU.add
                                      ).then_inc(est_chain, 1)
                    dve.wait_ge(est_chain, i * 10 + 10)
                    dve.scalar_tensor_tensor(everstd[:, r, :], eagg[:, 3, :], 0.25, eagg[:, 4, :],
                                             ALU.mult, ALU.add).then_inc(evar_set, 1)

                def center(i, r):
                    y = ysb[:, r, :, :]
                    dve.wait_ge(est_chain, i * 10 + 10)
                    for q in range(4):
                        ins = dve.scalar_tensor_tensor(y[:, q, :], y[:, q, :], emean[:, q:q + 1], vecs[:, r, 1, :],
                                                       ALU.subtract, ALU.mult)
                    ins.then_inc(xhat_set, 1)

                def normalize(i, r):
                    y = ysb[:, r, :, :]
                    dve.wait_ge(erstd_set, i + 1)
                    dve.wait_ge(xhat_set, i + 1)
                    for q in range(4):
                        ins = dve.scalar_tensor_tensor(y[:, q, :], y[:, q, :], everstd[:, r, q:q + 1], vecs[:, r, 2, :],
                                                       ALU.mult, ALU.add)
                    ins.then_inc(y_set[L], 1)

                def tile(i, r, k, first=False, last=False):
                    for f in range(nch):
                        n, par, M = i * nch + f, (r * nch + f) % 2, CH[L][f][1]
                        dve.wait_ge(act_set[L], n + 1)
                        if not (first and r == 0 and f < 2):
                            dve.wait_ge(down_mm[L], n - 1)
                        if L == 0:
                            dve.wait_ge(up_mm[L], n + 1)
                            dve.tensor_tensor(hT[0:M, par, :], ps[0:M, 2 + 2 * par, :], gact[0:M, par, :],
                                              ALU.mult).then_inc(h_set[L], 1)
                        else:
                            dve.scalar_tensor_tensor(hT[:, par, :], gsig[:, par, :], 1.0, gact[:, par, :],
                                                     ALU.add, ALU.mult).then_inc(h_set[L], 1)
                        if f == 0 and not last:
                            high_weights(i + 1, 1 - r, k + r)
                        if f == 1 and not last:
                            low_rows(i + 1, 1 - r)
                        if L == 1 and not (first and r == 0):
                            for ending in ((), (residual,), (variance, center), (normalize,))[f]:
                                ending(i - 1, 1 - r)

                high_weights(0, 0, 0)
                low_rows(0, 0)
                tile(0, 0, 0, first=True)
                tile(1, 1, 0, first=True)
                with dve.Fori(1, TILES // 2) as k:
                    tile(k * 2, 0, k)
                    tile(k * 2 + 1, 1, k)
                tile(TILES - 1, 0, TILES // 2, last=True)
                if L == 1:
                    for ending in (residual, variance, center, normalize):
                        ending(TILES - 1, 0)

            def chunk(m, s, k, now):
                if now(1):
                    r = (s + 1) % 4
                    dve.wait_ge(kv_hi_set, m + 2)
                    dve.tensor_tensor(kv_lo[:, r, :], kv[:, r % 2, :, :, :].rearrange("p h e d -> p (h e d)"),
                                      kv_hi[:, r, :].bitcast(F32), ALU.subtract).then_inc(kv_lo_set, 1)
                if (s + 2) % 8 == 7 and now(2):
                    dve.wait_ge(qkv_set, m + 3)
                    if now(0):
                        dve.wait_ge(kv_lo_set, m + 1)
                    outer_product(dve, s + 2).then_inc(kv_eighth_set, 1)
                if now(0):
                    dve.wait_ge(sum_mm, m + 1)
                    if now(-1):
                        dve.wait_ge(y1_set, m)
                    bank = 2 * (s % 2)
                    sums = ps[:, bank:bank + 2, :].rearrange("p n (h e d) -> p (n h) e d", e=HD, d=HD)
                    q = qkv[:, s % 4, 0, :].rearrange("p (h d) -> p h d", d=HD)
                    dve.tensor_tensor(qkv_sum, sums, spread(q, 2, [P, HEADS, HD, HD]), ALU.mult
                                      ).then_inc(weigh_set, 1)
                    dve.wait_ge(weigh_set, m + 1)
                    if now(-2):
                        dve.wait_ge(y1T_mm, m - 1)
                    dve.tensor_reduce(y1[:, s % 2, :].rearrange("p (h e) -> p h e", e=HD), qkv_sum, AX, ALU.add
                                      ).then_inc(y1_set, 1)

            def combine(L):
                def weigh(b):
                    r = b % 2
                    dve.wait_ge(gathered[b % 4], 64 * L + 32 * (b // 4 + 1))
                    dve.wait_ge(z_first[L], b + 1)
                    for q in range(QT):
                        ins = dve.scalar_tensor_tensor(zg[:, r, q, :], yg[:, b % 4, 1, q, :],
                                                       wsel[:, b * QT + q, 1:2], zg[:, r, q, :], ALU.mult, ALU.add)
                    if L == 0:
                        link(ins)
                        ins = dve.tensor_tensor(zg[:, r, :, :], zg[:, r, :, :],
                                                spread(fbias_bc[:, :], 1, [P, QT, D]), ALU.add)
                    ins.then_inc(z_ready[L], 1)

                def add(b):
                    r = b % 2
                    dve.wait_ge(gated_set, SEQS + b + 1)
                    ins = dve.tensor_tensor(rows_of(xres, b), rows_of(xres, b), sg[:, r, :, :], ALU.add)
                    ins.then_inc(x_set[L], 1)

                if L == 1:
                    for b in range(SEQS + 2):
                        if b < SEQS:
                            weigh(b)
                        if b >= 2:
                            add(b - 2)
                    return
                for b in range(SEQS + 4):
                    if b < SEQS:
                        weigh(b)
                    if 2 <= b < SEQS + 2:
                        dve.wait_ge(x_set[0], b - 1)
                        statistics(1, b - 2)
                    if 3 <= b < SEQS + 3:
                        normed(1, b - 3)
                    if b >= 4:
                        low_tokens(1, b - 4)

            dve.memset(zeros[:, 0:32, :], 0.0).then_inc(zero_set, 1)
            for b in range(SEQS + 3):
                if b < SEQS:
                    if b % 4 == 0:
                        dve.wait_ge(ld_x[b // 4], 16)
                    statistics(0, b)
                if 2 <= b < SEQS + 2:
                    normed(0, b - 2)
                if b == 3:
                    setup()
                if b >= 3:
                    low_tokens(0, b - 3)
            setup_end()
            low_half(0, 0, 7)
            low_half(0, 1, 6)
            routing(0)
            dve.sem_inc(attn_set, 1)
            dve.wait_ge(vaug_const, 2)
            steps(dve, attend)
            block1_weights()
            experts(0)
            combine(0)
            routing(1)
            chunk_steps(dve, chunk)
            experts(1)
            combine(1)


_INS = ['L0_attn_x', 'L0_attn_w_qkv', 'L0_attn_b_qkv', 'L0_attn_w_proj', 'L0_attn_b_proj', 'L0_ffn_router_w',
        'L0_ffn_w1', 'L0_ffn_v1', 'L0_ffn_w2', 'L0_ffn_bias', 'L1_attn_Wq', 'L1_attn_Wk', 'L1_attn_Wv',
        'L1_attn_Wc', 'L1_attn_Ltri', 'L1_ffn_Wr', 'L1_ffn_br', 'L1_ffn_Wi', 'L1_ffn_bi', 'L1_ffn_Wg',
        'L1_ffn_bg', 'L1_ffn_Wo', 'L1_ffn_bo', 'L1_ffn_gamma', 'L1_ffn_beta']


def kernel(**inputs):
    import numpy as np
    import concourse.bacc as bacc
    from concourse.bass_utils import run_bass_kernel_spmd

    nc = bacc.Bacc("TRN2", target_bir_lowering=False, num_devices=1)
    arrays, args = {}, []
    for name in _INS:
        a = np.ascontiguousarray(inputs[name])
        arrays[f"in_{name}"] = a
        args.append(nc.dram_tensor(f"in_{name}", a.shape, mybir.dt.from_np(a.dtype), kind="ExternalInput").ap())
    shape = inputs['L0_attn_x'].shape
    args.append(nc.dram_tensor("out_x", shape, F32, kind="ExternalOutput").ap())
    build(nc, *args)
    r = run_bass_kernel_spmd(nc, [arrays], core_ids=[0])
    return r.results[0]["out_x"]
```
